# Optimizing a Trainium2 kernel written in Bass

```python
import numpy as np
import jax
import jax.numpy as jnp

def _softmax(x, axis=-1):
    return jax.nn.softmax(x, axis=axis)

def _gelu(x):
    return jax.nn.gelu(x, approximate=True)

def _silu(x):
    return jax.nn.silu(x)

def _sigmoid(x):
    return jax.nn.sigmoid(x)

def _layernorm(x, axis=-1, eps=1e-05):
    m = jnp.mean(x, axis=axis, keepdims=True)
    v = jnp.var(x, axis=axis, keepdims=True)
    return (x - m) / jnp.sqrt(v + eps)

def _scatter_add(tgt, idx, src, axis=0):
    return tgt.at[idx].add(src)

def _segment_sum(src, seg, n):
    return jax.ops.segment_sum(src, seg, n)
kernel_name = 'mk_early_fusion_d1_tok_img768_r4_d3c0bb'

def setup_inputs(seed: int=0):
    np.random.seed(seed)
    _w = jnp.asarray

    def _rec_inputs():
        import jax
        import jax.numpy as jnp
        _rk = jax.random.key(seed)
        x = -0.000147625 + 0.999875 * jax.random.normal(jax.random.fold_in(_rk, 1), (16, 3, 224, 224), jnp.float32)
        txt = 0.00880239 + 1.14618 * jax.random.normal(jax.random.fold_in(_rk, 2), (16, 128, 192), jnp.float32)
        return (x, txt)
    x, txt = _rec_inputs()

    def _L0_tok_setup():
        import jax, jax.numpy as jnp
        import numpy as np
        P = 16

        def _patchify(x):
            B, C, H, W = x.shape
            gh, gw = (H // P, W // P)
            x = x.reshape(B, C, gh, P, gw, P)
            x = x.transpose(0, 2, 4, 1, 3, 5)
            return x.reshape(B, gh * gw, C * P * P)
        key = jax.random.key(seed)
        k1, k2, k3, k4, k5 = jax.random.split(key, 5)
        B, C, H, W_ = (64, 3, 224, 224)
        D = 192
        Din = P * P * C
        seq = H // P * (W_ // P) + 1
        return {'x': jax.random.normal(k1, (B, C, H, W_), dtype=jnp.float32), 'W': jax.random.normal(k2, (D, Din), dtype=jnp.float32) * 0.02, 'b': jax.random.normal(k3, (D,), dtype=jnp.float32) * 0.02, 'class_token': jax.random.normal(k4, (D,), dtype=jnp.float32), 'pos_emb': jax.random.normal(k5, (seq, D), dtype=jnp.float32)}
    _L0_tok_all = _L0_tok_setup()
    _L0_tok_in = {k: v for k, v in _L0_tok_all.items() if k in ('W', 'b', 'class_token', 'pos_emb')}
    del _L0_tok_all

    def _L0_attn_setup():
        import jax, jax.numpy as jnp
        import numpy as np
        key = jax.random.key(seed)
        k1, k2, k3, k4, k5 = jax.random.split(key, 5)
        B, N, C = (16, 256, 192)
        x = jax.random.normal(k1, (B, N, C), dtype=jnp.float32)
        sc_token = jax.random.normal(k2, (1, 196, C), dtype=jnp.float32) * 0.02
        W_qkv = jax.random.normal(k3, (C, 3 * C), dtype=jnp.float32) * 0.02
        W_proj = jax.random.normal(k4, (C, C), dtype=jnp.float32) * 0.02
        b_proj = jax.random.normal(k5, (C,), dtype=jnp.float32) * 0.02
        return {'x': x, 'sc_token': sc_token, 'W_qkv': W_qkv, 'W_proj': W_proj, 'b_proj': b_proj}
    _L0_attn_all = _L0_attn_setup()
    _L0_attn_in = {k: v for k, v in _L0_attn_all.items() if k in ('sc_token', 'W_qkv', 'W_proj', 'b_proj')}
    del _L0_attn_all

    def _L0_ffn_setup():
        import jax, jax.numpy as jnp
        import numpy as np
        TOP_K = 2
        key = jax.random.key(seed)
        ks = jax.random.split(key, 5)
        B, S, D, H, E = (1, 512, 192, 768, 8)
        x = jax.random.normal(ks[0], (B, S, D), dtype=jnp.float32)
        gate_w = jax.random.normal(ks[1], (E, D), dtype=jnp.float32) * 0.02
        w1 = jax.random.normal(ks[2], (E, D, H), dtype=jnp.float32) * 0.02
        b1 = jnp.zeros((E, H), dtype=jnp.float32)
        w2 = jax.random.normal(ks[3], (E, H, D), dtype=jnp.float32) * 0.02
        b2 = jnp.zeros((E, D), dtype=jnp.float32)
        return {'x': x, 'gate_w': gate_w, 'w1': w1, 'b1': b1, 'w2': w2, 'b2': b2}
    _L0_ffn_all = _L0_ffn_setup()
    _L0_ffn_in = {k: v for k, v in _L0_ffn_all.items() if k in ('gate_w', 'w1', 'b1', 'w2', 'b2')}
    del _L0_ffn_all
    return {'x': x, 'txt': txt, 'L0_tok_W': _L0_tok_in['W'], 'L0_tok_b': _L0_tok_in['b'], 'L0_tok_class_token': _L0_tok_in['class_token'], 'L0_tok_pos_emb': _L0_tok_in['pos_emb'], 'L0_attn_sc_token': _L0_attn_in['sc_token'], 'L0_attn_W_qkv': _L0_attn_in['W_qkv'], 'L0_attn_W_proj': _L0_attn_in['W_proj'], 'L0_attn_b_proj': _L0_attn_in['b_proj'], 'L0_ffn_gate_w': _L0_ffn_in['gate_w'], 'L0_ffn_w1': _L0_ffn_in['w1'], 'L0_ffn_b1': _L0_ffn_in['b1'], 'L0_ffn_w2': _L0_ffn_in['w2'], 'L0_ffn_b2': _L0_ffn_in['b2']}

def reference(x, txt, L0_tok_W, L0_tok_b, L0_tok_class_token, L0_tok_pos_emb, L0_attn_sc_token, L0_attn_W_qkv, L0_attn_W_proj, L0_attn_b_proj, L0_ffn_gate_w, L0_ffn_w1, L0_ffn_b1, L0_ffn_w2, L0_ffn_b2):
    import jax
    import jax.numpy as jnp

    def _L0_tok_ref(x, W, b, class_token, pos_emb):
        import jax, jax.numpy as jnp
        import numpy as np
        P = 16

        def _patchify(x):
            B, C, H, W = x.shape
            gh, gw = (H // P, W // P)
            x = x.reshape(B, C, gh, P, gw, P)
            x = x.transpose(0, 2, 4, 1, 3, 5)
            return x.reshape(B, gh * gw, C * P * P)
        B = x.shape[0]
        patches = _patchify(x)
        tok = jnp.einsum('bnd,ed->bne', patches, W) + b
        cls = jnp.broadcast_to(class_token, (B, 1, class_token.shape[0]))
        emb = jnp.concatenate([cls, tok], axis=1)
        return emb + pos_emb[None, :, :]

    def _L0_attn_ref(x, sc_token, W_qkv, W_proj, b_proj):
        import jax, jax.numpy as jnp
        import numpy as np
        B, N, C = x.shape
        H = 12
        Dh = C // H
        scale = Dh ** (-0.5)
        xt = jnp.concatenate([x, jnp.broadcast_to(sc_token, (B,) + sc_token.shape[1:])], axis=1)
        N1 = xt.shape[1]
        qkv = (xt @ W_qkv).reshape(B, N1, 3, H, Dh)
        q = qkv[:, :, 0].transpose(0, 2, 1, 3)
        k = qkv[:, :, 1].transpose(0, 2, 1, 3)
        v = qkv[:, :, 2].transpose(0, 2, 1, 3)
        attn = jax.nn.softmax(jnp.einsum('bhqd,bhkd->bhqk', q, k) * scale, axis=-1)
        out = jnp.einsum('bhqk,bhkd->bhqd', attn, v)
        out = out.transpose(0, 2, 1, 3).reshape(B, N1, C)
        out = out[:, :N, :]
        return out @ W_proj + b_proj

    def _L0_ffn_ref(x, gate_w, w1, b1, w2, b2):
        import jax, jax.numpy as jnp
        import numpy as np
        TOP_K = 2
        B, S, D = x.shape
        E, _, H = w1.shape
        T = B * S
        K = TOP_K
        xf = x.reshape(T, D)
        logits = xf @ gate_w.T
        probs = jax.nn.softmax(logits, axis=-1)
        top_w, top_i = jax.lax.top_k(probs, K)
        top_w = top_w / (jnp.sum(top_w, axis=-1, keepdims=True) + 1e-09)
        flat_e = top_i.reshape(-1)
        flat_w = top_w.reshape(-1)
        tok_idx = jnp.repeat(jnp.arange(T), K)
        order = jnp.argsort(flat_e)
        se = flat_e[order]
        pt = tok_idx[order]
        pw = flat_w[order]
        counts = jax.ops.segment_sum(jnp.ones(T * K, jnp.int32), se, num_segments=E)
        starts = jnp.concatenate([jnp.zeros((1,), jnp.int32), jnp.cumsum(counts)[:-1]])
        pos = jnp.arange(T * K) - starts[se]
        cap = T * K
        padded = jnp.zeros((E, cap, D), x.dtype).at[se, pos].set(xf[pt])
        hidden = jax.nn.gelu(jnp.einsum('ecd,edh->ech', padded, w1) + b1[:, None, :], approximate=False)
        out = jnp.einsum('ech,ehd->ecd', hidden, w2) + b2[:, None, :]
        expert_out = out[se, pos] * pw[:, None]
        final = jnp.zeros((T, D), x.dtype).at[pt].add(expert_out)
        return final.reshape(B, S, D)
    h = _L0_tok_ref(x, L0_tok_W, L0_tok_b, L0_tok_class_token, L0_tok_pos_emb)
    h = jnp.concatenate([h, txt], axis=1)
    h = h + _L0_attn_ref(_layernorm(h, axis=-1), L0_attn_sc_token, L0_attn_W_qkv, L0_attn_W_proj, L0_attn_b_proj)
    h = h + _L0_ffn_ref(_layernorm(h, axis=-1), L0_ffn_gate_w, L0_ffn_w1, L0_ffn_b1, L0_ffn_w2, L0_ffn_b2)
    return h

_drawn_inputs = setup_inputs


def setup_inputs(seed=0):
    import zlib

    import numpy as np

    out = dict(_drawn_inputs(seed))
    spreads = {'L0_ffn_b1': (0.0, 1.174), 'L0_ffn_b2': (0.0, 0.38)}
    factors = {'L0_tok_b': 3.659,
     'L0_attn_sc_token': 64.0,
     'L0_attn_W_qkv': 8.0,
     'L0_attn_W_proj': 8.0,
     'L0_attn_b_proj': 9.663,
     'L0_ffn_w1': 2.998}
    for name, (base, spread) in spreads.items():
        noise = np.random.default_rng([zlib.crc32(name.encode()), seed]).standard_normal(out[name].shape)
        drawn = base * np.exp(spread * noise) if base else spread * noise
        out[name] = jnp.asarray(drawn.astype(out[name].dtype))
    for name, factor in factors.items():
        out[name] = (out[name] * factor).astype(out[name].dtype)
    return out
```

```python
import concourse.bass as bass
from concourse import mybir
from contextlib import ExitStack
import numpy as np

F32 = mybir.dt.float32
F32R = mybir.dt.float32r
I32 = mybir.dt.int32
U32 = mybir.dt.uint32
ALU = mybir.AluOpType
ACT = mybir.ActivationFunctionType
AX = mybir.AxisListType

B, CH, IMG, P = 16, 3, 224, 16
G = IMG // P
D, H, DH = 192, 12, 16
TXT = 128
SC = 196
NPATCH = G * G
N = NPATCH + 1 + TXT
NP = N + 1
ROWS = [NPATCH // 2, NPATCH // 2 + 1, TXT]
FIRST = [0, ROWS[0], ROWS[0] + ROWS[1]]
NT = 3
SCR = SC // 2
KD = D // 2
HG = 4
NG = H // HG
KC5 = NT + 2
PX = 8
E, HID, TOPK = 8, 768, 2
T = B * N
BLK = 256
NBLK = (T * TOPK + E * (BLK - 1)) // BLK
REG = T + BLK
XROWS = E * REG + BLK
ROW = D + 1
SCALE = float(DH) ** -0.5
LN_EPS = 1e-5
SKIP = 1 << 20
KMAX, KEXP = 126, 128
UNITS = [s for s in range(30) if s % 5 != 4][:18]


def has(b):
    return not isinstance(b, int) or 0 <= b < B


def wait(eng, sem, value):
    if isinstance(value, int) and value <= 0:
        return
    eng.wait_ge(sem, value)


def hold(eng):
    eng.nop(nofuse=True)


def wait_nearest(eng, candidates):
    for b, sem, value in candidates:
        if has(b):
            wait(eng, sem, value)
            return


def run_steps(eng, step):
    for i in (-2, -1, 0):
        step(i, i % 2)
    with eng.Fori(1, B - 4, 2) as i:
        step(i, 1)
        step(i + 1, 0)
    for i in range(B - 3, B + 1):
        step(i, i % 2)


def build(nc, x, txt, tok_w, tok_b, cls, pos, sc_tok, w_qkv, w_proj, b_proj, gate_w, w1, b1, w2, b2, out):
    eq_d = nc.dram_tensor("eq_d", [2, 2, 2, H, DH, NP], F32, kind="Internal").ap()
    em_d = nc.dram_tensor("em_d", [2, 2, H, NP], F32, kind="Internal").ap()
    ec_d = nc.dram_tensor("ec_d", [2, H, DH, SC], F32, kind="Internal").ap()
    xs_d = nc.dram_tensor("xs_d", [XROWS, ROW], F32, kind="Internal").ap()
    ys_d = nc.dram_tensor("ys_d", [TOPK * T, D], F32, kind="Internal").ap()

    keep = ExitStack()
    sb = lambda st, name, shape, dt=F32: st.enter_context(nc.sbuf_tensor(name, shape, dt))
    pb = lambda st, name, shape: st.enter_context(nc.psum_tensor(name, shape, F32))
    sem = lambda st, name: st.enter_context(nc.semaphore(name))

    with keep:
        hs = sb(keep, "hs", [128, B, NT, D])
        gw = sb(keep, "gw", [128, B, NT, TOPK])
        ident = sb(keep, "ident", [128, 128])
        base = sb(keep, "base", [128, NT + 1, E])

        attend = ExitStack()
        with attend:
            wp = sb(attend, "wp", [KD, PX, D])
            posb = sb(attend, "posb", [ROWS[1], 2, D])
            wqkv = sb(attend, "wqkv", [KD, 2, 3 * D])
            wpj = sb(attend, "wpj", [KD + 1, 2, D])
            gt = sb(attend, "gt", [KD, 2, E])
            ut = sb(attend, "ut", [128, 128])
            ones = sb(attend, "ones", [128, 128])
            iota8 = sb(attend, "iota8", [128, E])
            halfneg = sb(attend, "halfneg", [128, NT])
            ids = sb(attend, "ids", [128, NT, TOPK])
            qs = [sb(attend, f"qs{p}", [KEXP, H, NP], F32R) for p in range(2)]
            ko = [sb(attend, f"ko{p}", [KEXP, H, NP], F32R) for p in range(2)]
            kc = sb(attend, "kc", [KEXP, H, SC], F32R)
            va = [sb(attend, f"va{p}", [128, NT, H, 32]) for p in range(2)]
            vc = sb(attend, "vc", [SCR, 2, H, 32])
            xt = [sb(attend, f"xt{p}", [KD, 2, NP]) for p in range(2)]
            img = sb(attend, "img", [KD, G, IMG])

            setup(nc, sb, pb, sem, locals())
            attention(nc, sb, pb, sem, locals())
        routed = ExitStack()
        with routed:
            table = sb(routed, "table", [1, 2, NBLK], I32)
            routing(nc, sb, pb, sem, locals())
            experts(nc, sb, pb, sem, locals())
            combine(nc, sb, pb, sem, locals())


def store_rows(sp, out, hs, done):
    for b in range(B):
        sp.dma_start(out[b, 1:1 + ROWS[0], :], hs[0:ROWS[0], b, 0, :]).then_inc(done, 16)
        sp.dma_start(out[b, 1 + ROWS[0]:1 + NPATCH, :], hs[0:ROWS[0], b, 1, :]).then_inc(done, 16)
        sp.dma_start(out[b, 0:1, :], hs[ROWS[0]:ROWS[1], b, 1, :]).then_inc(done, 16)
        sp.dma_start(out[b, NPATCH + 1:N, :], hs[0:TXT, b, 2, :]).then_inc(done, 16)


def setup(nc, sb, pb, sem, t):
    hs, ident, base = t["hs"], t["ident"], t["base"]
    wp, posb, wqkv, wpj, gt, ut, ones = (t[k] for k in "wp posb wqkv wpj gt ut ones".split())
    iota8, halfneg, ids, qs, ko, kc, va, vc, xt = (t[k] for k in "iota8 halfneg ids qs ko kc va vc xt".split())
    x, ec_d = t["x"], t["ec_d"]
    with ExitStack() as st:
        wraw = sb(st, "wraw", [KD, 2, CH * P * P])
        wperm = sb(st, "wperm", [KD, 2, PX, 2, KD // 2])
        graw = sb(st, "graw", [E, D])
        sraw = sb(st, "sraw", [SCR, 2, D])
        bias = sb(st, "bias", [ROWS[1], 2, D])
        sct = sb(st, "sct", [KD, 2, SC])
        kcs = sb(st, "kcs", [KD, 2, 2, SC], F32R)
        ps = [pb(st, f"su{i}", [128, 512]) for i in range(4)]
        w_in, s_in, q_in, c_in, p_in, b_in, h_in = (sem(st, f"su_{n}") for n in
                                                    ("w_in", "s_in", "q_in", "c_in", "p_in", "b_in", "h_in"))
        zeroed, made, turned, copied = (sem(st, f"su_{n}") for n in ("zeroed", "made", "turned", "copied"))
        summed, hi_done, ec_out, kc_in, cls_in, w_perm = (sem(st, f"su_{n}") for n in
                                                          ("summed", "hi_done", "ec_out", "kc_in", "cls_in", "w_perm"))
        block = st.enter_context(nc.Block())
        JOBS = PX + 1 + 2 + 2 + 2

        @block.sync
        def _(sp):
            sp.dma_start(wraw[:, :, :], t["tok_w"].rearrange("(h e) d -> e h d", h=2)).then_inc(w_in, 16)
            sp.dma_start(graw[:, :], t["gate_w"]).then_inc(s_in, 16)
            sp.dma_start(sraw[:, :, :], t["sc_tok"][0].rearrange("(a p) d -> p a d", a=2)).then_inc(s_in, 16)
            sp.dma_start(wqkv[:, :, :], t["w_qkv"].rearrange("(c p) n -> p c n", c=2)).then_inc(q_in, 16)
            pos = t["pos"]
            sp.dma_start(posb[0:ROWS[0], :, :],
                         pos[1:1 + NPATCH, :].rearrange("(a p) d -> p a d", a=2)).then_inc(p_in, 16)
            sp.dma_start(posb[ROWS[0]:ROWS[1], 1:2, :], pos[0:1, :].unsqueeze(1)).then_inc(p_in, 16)
            tb = t["tok_b"].unsqueeze(0)
            sp.dma_start(bias[0:ROWS[0], 0, :], tb.broadcast_to([ROWS[0], D])).then_inc(p_in, 16)
            sp.dma_start(bias[0:ROWS[0], 1, :], tb.broadcast_to([ROWS[0], D])).then_inc(p_in, 16)
            sp.dma_start(bias[ROWS[0]:ROWS[1], 1, :], t["cls"].unsqueeze(0)).then_inc(p_in, 16)
            sp.dma_start(hs[:, :, 2, :], t["txt"].rearrange("b t d -> t b d")).then_inc(h_in, 16)
            sp.dma_start(wpj[0:KD, :, :], t["w_proj"].rearrange("(c p) n -> p c n", c=2)).then_inc(b_in, 16)
            sp.dma_start(wpj[KD:KD + 1, 1, :], t["b_proj"].unsqueeze(0)).then_inc(b_in, 16)
            sp.wait_ge(summed, 2)
            sp.dma_start(hs[ROWS[0]:ROWS[1], :, 1, :],
                         posb[ROWS[0]:ROWS[1], 1:2, :].broadcast_to([1, B, D])).then_inc(cls_in, 16)
            sp.wait_ge(summed, 4)
            for hl in range(2):
                sp.dma_start(ec_d[hl].rearrange("(c h) d n -> (h d) c n", c=2),
                             kcs[:, hl, :, :].bitcast(F32)).then_inc(ec_out, 16)
            sp.wait_ge(ec_out, 32)
            sp.wait_ge(zeroed, 10)
            for s, hl in enumerate((0, 1, 0)):
                sp.dma_start(kc[DH * s:DH * s + DH, :, :].bitcast(F32),
                             ec_d[hl].rearrange("h d n -> d h n")).then_inc(kc_in, 16)
            sp.wait_ge(kc_in, 48)
            sp.wait_ge(cls_in, 16)
            sp.wait_ge(b_in, 32)
            sp.wait_ge(h_in, 16)

        @block.gpsimd
        def _(pool):
            pool.memset(ident[:, :], 0.0).then_inc(zeroed, 1)
            pool.memset(ut[:, :], 0.0).then_inc(zeroed, 1)
            pool.wait_ge(zeroed, 2)
            pool.affine_select(out=ident[:, :], in_=ident[:, :], compare_op=ALU.not_equal, fill=1.0, base=0,
                               pattern=[[-1, 128]], channel_multiplier=1).then_inc(made, 1)
            pool.affine_select(out=ut[:, :], in_=ut[:, :], compare_op=ALU.is_ge, fill=1.0, base=0,
                               pattern=[[-1, 128]], channel_multiplier=1).then_inc(made, 1)
            pool.iota(iota8[:, :], pattern=[[1, E]], base=0, channel_multiplier=0,
                      allow_small_or_imprecise_dtypes=True).then_inc(made, 1)
            pool.iota(base[:, 0, :], pattern=[[REG, E]], base=0, channel_multiplier=0,
                      allow_small_or_imprecise_dtypes=True).then_inc(made, 1)
            for tile in range(NT):
                pool.iota(ids[:, tile, :], pattern=[[T, TOPK]], base=FIRST[tile], channel_multiplier=1,
                          allow_small_or_imprecise_dtypes=True).then_inc(made, 1)
            pool.memset(halfneg[:, :], -0.5).then_inc(made, 1)
            for p in range(2):
                pool.memset(qs[p][:, :, :].bitcast(F32), 0.0).then_inc(zeroed, 1)
                pool.memset(ko[p][:, :, :].bitcast(F32), 0.0).then_inc(zeroed, 1)
                pool.memset(va[p][:, :, :, :], 0.0).then_inc(zeroed, 1)
            pool.memset(kc[:, :, :].bitcast(F32), 0.0).then_inc(zeroed, 1)
            pool.memset(vc[:, :, :, :], 0.0).then_inc(zeroed, 1)
            pool.wait_ge(zeroed, 10)
            for n, one in enumerate((ko[0][64:KEXP, :, :].bitcast(F32), ko[1][64:KEXP, :, :].bitcast(F32),
                                     kc[64:KEXP, :, :].bitcast(F32), va[0][:, :, :, DH:DH + 1],
                                     va[1][:, :, :, DH:DH + 1], vc[:, :, :, DH:DH + 1])):
                pool.wait_ge(made, 8 + n)
                pool.memset(one, 1.0).then_inc(made, 1)
            pool.wait_ge(made, 14)

        @block.tensor
        def _(pe):
            pe.wait_ge(made, 1)
            pe.wait_ge(w_perm, 2)
            job = 0
            for i in range(PX):
                if job >= 4:
                    pe.wait_ge(copied, job - 3)
                for eh in range(2):
                    last = pe.transpose(ps[job % 4][0:KD, eh * KD:(eh + 1) * KD],
                                        wperm[:, eh, i, :, :].rearrange("e j c -> e (j c)"), ident[0:KD, 0:KD])
                last.then_inc(turned, 1)
                job += 1
            pe.wait_ge(s_in, 32)
            pe.wait_ge(copied, job - 3)
            for c in range(2):
                last = pe.transpose(ps[job % 4][0:KD, c * E:(c + 1) * E], graw[:, c * KD:(c + 1) * KD], ident[0:E, 0:E])
            last.then_inc(turned, 1)
            job += 1
            for c in range(2):
                pe.wait_ge(copied, job - 3)
                for a in range(2):
                    last = pe.transpose(ps[job % 4][0:KD, a * SCR:(a + 1) * SCR], sraw[:, a, c * KD:(c + 1) * KD],
                                        ident[0:SCR, 0:SCR])
                last.then_inc(turned, 1)
                job += 1
            pe.wait_ge(q_in, 16)
            pe.wait_ge(copied, job)
            for c in range(2):
                for kd in range(2):
                    last = pe.matmul(ps[job % 4][0:KD, 0:SC], wqkv[:, kd, D + c * KD:D + (c + 1) * KD], sct[:, kd, :],
                                     start=kd == 0, stop=kd == 1)
                last.then_inc(turned, 1)
                job += 1
            for a in range(2):
                for kd in range(2):
                    last = pe.matmul(ps[job % 4][0:SCR, 0:D], sct[:, kd, a * SCR:(a + 1) * SCR], wqkv[:, kd, 2 * D:3 * D],
                                     start=kd == 0, stop=kd == 1)
                last.then_inc(turned, 1)
                job += 1
            assert job == JOBS

        @block.scalar
        def _(act):
            job = 0
            for i in range(PX):
                act.wait_ge(turned, job + 1)
                act.activation(wp[:, i, :], ps[job % 4][0:KD, 0:D], ACT.Copy).then_inc(copied, 1)
                job += 1
            act.wait_ge(turned, job + 1)
            act.activation(gt[:, :, :], ps[job % 4][0:KD, 0:2 * E].rearrange("p (c e) -> p c e", c=2),
                           ACT.Copy).then_inc(copied, 1)
            job += 1
            for c in range(2):
                act.wait_ge(turned, job + 1)
                act.activation(sct[:, c, :], ps[job % 4][0:KD, 0:SC], ACT.Copy).then_inc(copied, 1)
                job += 1
            for c in range(2):
                act.wait_ge(turned, job + 1)
                act.activation(kcs[:, 0, c, :], ps[job % 4][0:KD, 0:SC], ACT.Copy).then_inc(hi_done, 1)
                job += 1
            act.wait_ge(zeroed, 10)
            act.wait_ge(made, 14)
            for a in range(2):
                act.wait_ge(turned, job + 1)
                act.activation(vc[:, a, :, 0:DH], ps[job % 4][0:SCR, 0:D].rearrange("p (h d) -> p h d", h=H),
                               ACT.Copy).then_inc(copied, 1)
                job += 1
            act.wait_ge(copied, JOBS - 2)

        @block.vector
        def _(dve):
            for p in range(2):
                dve.memset(xt[p][:, :, N:NP], 0.0)
            dve.wait_ge(w_in, 16)
            for eh in range(2):
                dve.tensor_copy(wperm[:, eh, :, :, :],
                                wraw[:, eh, :].rearrange("e (c j i) -> e i j c", j=2, i=PX)).then_inc(w_perm, 1)
            dve.wait_ge(p_in, 16 * 5)
            dve.tensor_tensor(posb[0:ROWS[0], 0, :], posb[0:ROWS[0], 0, :], bias[0:ROWS[0], 0, :],
                              ALU.add).then_inc(summed, 1)
            dve.tensor_tensor(posb[:, 1, :], posb[:, 1, :], bias[:, 1, :], ALU.add).then_inc(summed, 1)
            for c in range(2):
                dve.wait_ge(hi_done, c + 1)
                dve.tensor_tensor(kcs[:, 1, c, :], ps[(PX + 3 + c) % 4][0:KD, 0:SC], kcs[:, 0, c, :].bitcast(F32),
                                  ALU.subtract).then_inc(summed, 1)
            dve.wait_ge(summed, 4)


def attention(nc, sb, pb, sem, t):
    hs, gw, ident, base = t["hs"], t["gw"], t["ident"], t["base"]
    wp, posb, wqkv, wpj, gt, ut, ones = (t[k] for k in "wp posb wqkv wpj gt ut ones".split())
    iota8, halfneg, ids, qs, ko, kc, va, vc, xt, img = (t[k] for k in "iota8 halfneg ids qs ko kc va vc xt img".split())
    x, eq_d, em_d, xs_d = t["x"], t["eq_d"], t["em_d"], t["xs_d"]
    with ExitStack() as st:
        xh = sb(st, "xh", [128, NT, D])
        qp = sb(st, "qp", [KD, 2, 2, 2, NP], F32R)
        pt = sb(st, "pt", [128, 3, HG, N])
        ots = sb(st, "ots", [128, N])
        rec = sb(st, "rec", [128, NT, HG])
        on = sb(st, "on", [128, NT, D])
        o2t = sb(st, "o2t", [KD + 1, 2, N])
        mxp = sb(st, "mxp", [128, NT * H, 2])
        negm = sb(st, "negm", [128, NT, H])
        negm2 = sb(st, "negm2", [128, NT, 2, H])
        mr = sb(st, "mr", [2 * H, NP], F32R)
        xa = sb(st, "xa", [128, NT, TOPK, ROW])
        x2t = sb(st, "x2t", [KD, 2, N])
        st1 = sb(st, "st1", [128, NT, 6])
        mv1 = sb(st, "mv1", [128, NT, 2])
        rs1 = sb(st, "rs1", [128, NT])
        st2 = sb(st, "st2", [128, NT, 6])
        mv2 = sb(st, "mv2", [128, NT, 2])
        rs2 = sb(st, "rs2", [128, NT])
        top = sb(st, "top", [128, NT, E])
        topi = sb(st, "topi", [128, NT, E], U32)
        topf = sb(st, "topf", [128, NT, TOPK])
        msk = sb(st, "msk", [128, NT, TOPK, E])
        both = sb(st, "both", [128, NT, E])
        ex = sb(st, "ex", [128, NT, E])
        zsum = sb(st, "zsum", [128, NT])
        den = sb(st, "den", [128, NT])
        place = sb(st, "place", [128, NT, E])
        pick = sb(st, "pick", [128, NT, TOPK, E])
        slotf = sb(st, "slotf", [128, NT, TOPK])
        slot = sb(st, "slot", [128, NT, TOPK], I32)

        ps_s = [pb(st, f"ps_s{i}", [128, 2, 512]) for i in range(2)]
        ps_m = [pb(st, f"ps_m{i}", [128, 512]) for i in range(2)]
        ps_o = pb(st, "ps_o", [128, 512])
        ps_j = pb(st, "ps_j", [128, 512])

        S = {}
        for n in """img_in patch_done patch_used ln1_stat ln1_mv ln1_eps ln1_rstd xh_done xt_done xt_copied
                    qk_done qk_hi qk_split eq_out q_in k_in v_done v_copied
                    mx_filled mx_read mx_comb m_split mt_done mt_copied em_out m_in
                    st_filled exp_done pv_done ot_copied ot_turned rec_done on_done on_turned o2_copied
                    proj_done h2_done ln2_stat ln2_mv ln2_eps ln2_rstd xa_done xa_copied ids_next x2t_done x2t_copied
                    logit_done top_done topi_done topf_done msk_done both_done prefix_done base_step place_done
                    pick_done slotf_done slot_done ex_sub ex_done z_done den_a den_done rden_done gw_done
                    sent cleared""".split():
            S[n] = sem(st, n)
        g_in = [[sem(st, f"{n}_in{g}") for g in range(NG)] for n in "qk"]
        block = st.enter_context(nc.Block())


        @block.sync
        def _(sp):
            def load_image(b):
                for h in range(2):
                    for c in range(CH):
                        src = x[b, c].rearrange("(g y) w -> y g w", y=P)
                        r = h * CH * P + c * P
                        sp.dma_start(img[r:r + P, :, 0:IMG - PX * h], src[:, :, PX * h:IMG]).then_inc(S["img_in"], 16)

            def expand(b, par, g):
                hh = slice(HG * g, HG * g + HG)
                for qk, dst, order in ((0, qs[par], (0, 0, 1)), (1, ko[par], (0, 1, 0))):
                    for s, hl in enumerate(order):
                        sp.dma_start(dst[DH * s:DH * s + DH, hh, :].bitcast(F32),
                                     eq_d[par, qk, hl, hh].rearrange("h d n -> d h n")).then_inc(g_in[qk][g], 16)

            def step(i, par):
                if isinstance(i, int) and i == -2:
                    load_image(0)
                if has(i + 3):
                    wait(sp, S["patch_done"], i + 3)
                    hold(sp)
                    load_image(i + 3)
                if has(i + 2):
                    wait(sp, S["qk_split"], 4 * (i + 2) + 4)
                    hold(sp)
                    for g in range(NG):
                        for qk in range(2):
                            wait(sp, g_in[qk][g], 48 * (i + 1) if not isinstance(i, int) or i >= 0 else 0)
                            hold(sp)
                    for qk in range(2):
                        for hl in range(2):
                            sp.dma_start(eq_d[par, qk, hl].rearrange("(c h) d n -> (h d) c n", c=2),
                                         qp[:, qk, hl, :, :].bitcast(F32)).then_inc(S["eq_out"], 16)
                if has(i + 1):
                    wait(sp, S["mt_copied"], i + 2)
                    hold(sp)
                    sp.dma_start(em_d[1 - par].rearrange("l h n -> (l h) n"), mr[:, :].bitcast(F32)).then_inc(S["em_out"], 16)
                if has(i + 2):
                    wait(sp, S["eq_out"], 64 * (i + 3))
                    hold(sp)
                    wait(sp, S["st_filled"], 30 * i + 10)
                    hold(sp)
                    expand(i + 2, par, 0)
                if has(i + 1):
                    wait(sp, S["em_out"], 16 * (i + 2))
                    hold(sp)
                    sp.dma_start(qs[1 - par][KMAX:KEXP, :, :].bitcast(F32), em_d[1 - par]).then_inc(S["m_in"], 16)
                if has(i + 2):
                    for g in (1, 2):
                        wait(sp, S["st_filled"], 30 * i + 10 * g + 10)
                        hold(sp)
                        expand(i + 2, par, g)

            run_steps(sp, step)

        @block.gpsimd
        def _(pool):
            def rstd(b, mv, rs, mv_done, eps_done, rstd_done):
                wait(pool, mv_done, 3 * b + 3)
                hold(pool)
                pool.tensor_scalar(rs[:, :], mv[:, :, 1], LN_EPS, None, ALU.add).then_inc(eps_done, 1)
                wait(pool, eps_done, b + 1)
                hold(pool)
                pool.tensor_tensor(rs[:, :], rs[:, :], halfneg[:, :], ALU.pow).then_inc(rstd_done, 1)

            def step(i, par):
                if has(i + 2):
                    rstd(i + 2, mv1, rs1, S["ln1_mv"], S["ln1_eps"], S["ln1_rstd"])
                if has(i - 1):
                    rstd(i - 1, mv2, rs2, S["ln2_mv"], S["ln2_eps"], S["ln2_rstd"])
                    for tile in range(NT):
                        wait(pool, S["xa_done"], 3 * (i - 1) + tile + 1)
                        hold(pool)
                        r = ROWS[tile]
                        pool.tensor_copy(xa[0:r, tile, 1, 0:D], xa[0:r, tile, 0, 0:D]).then_inc(S["xa_copied"], 1)
                    pool.tensor_copy(xa[:, :, :, D:ROW].bitcast(I32), ids[:, :, :].unsqueeze(3)).then_inc(S["xa_copied"], 1)
                    pool.tensor_scalar(ids[:, :, :], ids[:, :, :], float(N), None, ALU.add).then_inc(S["ids_next"], 1)
                    wait(pool, S["slot_done"], i)
                    wait(pool, S["xa_copied"], 4 * i)
                    hold(pool)
                    for tile in range(NT):
                        for k in range(TOPK):
                            r = ROWS[tile]
                            pool.indirect_dma_start(
                                xs_d, bass.IndirectOffsetOnAxis(ap=slot[0:r, tile, k:k + 1], axis=0),
                                xa[0:r, tile, k, :], None).then_inc(S["sent"], 16)

            run_steps(pool, step)
            pool.wait_ge(S["sent"], 16 * 6 * B)

        @block.scalar
        def _(act):
            def step(i, par):
                for s in range(30):
                    if has(i):
                        u, pr = s // 2, s % 2
                        kcn = u % KC5
                        r = ROWS[kcn] if kcn < NT else SCR
                        wait(act, S["st_filled"], 30 * i + s + 1)
                        if pr == 0:
                            wait(act, S["pv_done"], 15 * i + u - 2)
                        act.activation(pt[0:r, u % 3, 2 * pr:2 * pr + 2, :], ps_s[s % 2][0:r, :, 0:N], ACT.Exp,
                                       scale=SCALE).then_inc(S["exp_done"], 1)
                    if s in (3, 13, 23):
                        b, g = (i - 1, 2) if s == 3 else (i, s // 10 - 1)
                        if has(b):
                            wait(act, S["pv_done"], 15 * b + 5 * g + 5)
                            wait(act, S["ot_turned"], 3 * b + g)
                            act.activation(ots[:, :], ps_o[:, 0:N], ACT.Copy).then_inc(S["ot_copied"], 1)
                    if s in (10, 11) and has(i + 2):
                        c = s - 10
                        wait(act, S["xt_done"], 2 * (i + 2) + c + 1)
                        act.activation(xt[par][:, c, 0:N], ps_j[0:KD, 0:N], ACT.Copy).then_inc(S["xt_copied"], 1)
                    if s in (6, 7) and has(i - 1):
                        c = s - 6
                        wait(act, S["on_turned"], 2 * (i - 1) + c + 1)
                        wait(act, S["proj_done"], 2 * (i - 1))
                        act.activation(o2t[0:KD, c, :], ps_j[0:KD, 0:N], ACT.Copy).then_inc(S["o2_copied"], 1)
                    if s in (13, 14) and has(i - 1):
                        c = s - 13
                        wait(act, S["x2t_done"], 2 * (i - 1) + c + 1)
                        wait(act, S["logit_done"], i - 1)
                        act.activation(x2t[:, c, :], ps_j[0:KD, 0:N], ACT.Copy).then_inc(S["x2t_copied"], 1)
                    if s in (17, 18, 19, 21) and has(i + 2):
                        j = (17, 18, 19, 21).index(s)
                        wait(act, S["qk_done"], 4 * (i + 2) + j + 1)
                        wait(act, S["eq_out"], 64 * (i + 2))
                        act.activation(qp[:, j // 2, 0, j % 2, :], ps_j[0:KD, 0:NP], ACT.Copy).then_inc(S["qk_hi"], 1)
                    if s == 22 and has(i - 1):
                        wait(act, S["ex_sub"], i)
                        act.activation(ex[:, :, :], ex[:, :, :], ACT.Exp).then_inc(S["ex_done"], 1)
                    if s in (26, 27) and has(i + 1):
                        vp = va[1 - par]
                        wait(act, S["v_done"], 2 * (i + 1) + s - 25)
                        for tile in (0, 1) if s == 26 else (2,):
                            r = ROWS[tile]
                            a = tile % 2
                            act.activation(vp[0:r, tile, :, 0:DH],
                                           ps_j[0:r, a * D:(a + 1) * D].rearrange("p (h d) -> p h d", h=H),
                                           ACT.Copy).then_inc(S["v_copied"], 1)

            run_steps(act, step)

        @block.tensor
        def _(pe):
            def patches(i, tile, lo, hi_):
                for p in range(lo, hi_):
                    last = pe.matmul(ps_j[0:ROWS[0], tile * D:(tile + 1) * D],
                                     img[:, 7 * tile:7 * tile + 7, :].rearrange("k g (w q) -> k q (g w)", q=P)[:, p],
                                     wp[:, p, :], start=p == 0, stop=p == PX - 1)
                return last

            def turn(i, src, c, done):
                for tile in range(NT):
                    r = ROWS[tile]
                    last = pe.transpose(ps_j[0:KD, FIRST[tile]:FIRST[tile] + r], src(tile, r, c), ident[0:r, 0:r])
                last.then_inc(done, 1)

            def turn_outputs(b, g):
                pe.wait_ge(S["ot_copied"], 3 * b + g + 1)
                for tile in range(NT):
                    last = pe.transpose(ps_j[:, 128 * tile:128 * tile + 128], ots[:, FIRST[tile]:FIRST[tile] + 128],
                                        ident[:, :])
                last.then_inc(S["ot_turned"], 1)

            def values(i, tiles, par):
                for tile in tiles:
                    r = ROWS[tile]
                    for kd in range(2):
                        last = pe.matmul(ps_j[0:r, (tile % 2) * D:(tile % 2 + 1) * D],
                                         xt[1 - par][:, kd, FIRST[tile]:FIRST[tile] + r], wqkv[:, kd, 2 * D:3 * D],
                                         start=kd == 0, stop=kd == 1)
                last.then_inc(S["v_done"], 1)

            def with_values(b, par, u):
                g, kcn = u // KC5, u % KC5
                wait(pe, S["exp_done"], 30 * b + 2 * u + 2)
                if kcn == 0:
                    wait(pe, S["ot_copied"], 3 * b + g)
                    if g == 0:
                        wait(pe, S["v_copied"], 3 * b + 3)
                for j in range(HG):
                    h = HG * g + j
                    r = ROWS[kcn] if kcn < NT else SCR
                    v = va[par][0:r, kcn, h, :] if kcn < NT else vc[:, kcn - NT, h, :]
                    last = pe.matmul(ps_o[32 * j:32 * j + 32, 0:N], v, pt[0:r, u % 3, j, :],
                                     start=kcn == 0, stop=kcn == KC5 - 1)
                last.then_inc(S["pv_done"], 1)

            def maxima(i, par, unit, fills):
                b = i + 1
                g, tile, pr = unit // 6, unit % 6 // 2, unit % 2
                r = ROWS[tile]
                if unit % 6 == 0 and 0 in fills:
                    pe.wait_ge(g_in[0][g], 48 * (b + 1))
                    pe.wait_ge(g_in[1][g], 48 * (b + 1))
                for f in fills:
                    n = 3 * unit + f
                    bank = ps_m[n % 2]
                    wait(pe, S["mx_read"], 54 * b + n - 1)
                    for e in ((f,) if f < 2 else (0, 1)):
                        h = HG * g + 2 * pr + e
                        q = qs[1 - par][0:KMAX, h, FIRST[tile]:FIRST[tile] + r]
                        if f < 2:
                            last = pe.matmul(bank[0:r, 0:NP], q, ko[1 - par][0:KMAX, h, :], start=True, stop=True)
                        else:
                            last = pe.matmul(bank[0:r, e * SC:(e + 1) * SC], q, kc[0:KMAX, h, :], start=True, stop=True)
                    last.then_inc(S["mx_filled"], 1)

            def step(i, par):
                for s in range(30):
                    u, pr = s // 2, s % 2
                    if has(i):
                        g, kcn = u // KC5, u % KC5
                        r = ROWS[kcn] if kcn < NT else SCR
                        if s == 0:
                            pe.wait_ge(S["m_in"], 16 * (i + 1))
                        wait(pe, S["exp_done"], 30 * i + s - 1)
                        for e in range(2):
                            h = HG * g + 2 * pr + e
                            k = ko[par][:, h, FIRST[kcn]:FIRST[kcn] + r] if kcn < NT else \
                                kc[:, h, (kcn - NT) * SCR:(kcn - NT + 1) * SCR]
                            last = pe.matmul(ps_s[s % 2][0:r, e, 0:NP], k, qs[par][:, h, :], start=True, stop=True)
                        last.then_inc(S["st_filled"], 1)
                    if s in UNITS and has(i + 1):
                        maxima(i, par, UNITS.index(s), (0, 1))
                    if s < 4 and has(i + 2):
                        if s == 0:
                            wait_nearest(pe, [(i, S["v_copied"], 3 * i + 3),
                                              (i + 1, S["qk_split"], 4 * (i + 2))])
                            pe.wait_ge(S["img_in"], 96 * (i + 3))
                        last = patches(i, s // 2, 4 * (s % 2), 4 * (s % 2) + 4)
                        if s == 3:
                            last.then_inc(S["patch_done"], 1)
                    if s == 5 and has(i - 1):
                        wait_nearest(pe, [(i + 2, S["patch_used"], i + 3), (i, S["v_copied"], 3 * i + 3),
                                          (i - 1, S["on_done"], 3 * i - 1)])
                        turn_outputs(i - 1, 2)
                    if s in (6, 7) and has(i - 1):
                        c = s - 6
                        if c == 0:
                            pe.wait_ge(S["on_done"], 3 * i)
                        else:
                            pe.wait_ge(S["o2_copied"], 2 * (i - 1) + 1)
                        turn(i, lambda tile, r, c: on[0:r, tile, c * KD:(c + 1) * KD], c, S["on_turned"])
                    if s in (8, 9) and has(i - 1):
                        if s == 8:
                            pe.wait_ge(S["o2_copied"], 2 * i)
                        else:
                            pe.wait_ge(S["h2_done"], 3 * i - 1)
                        for tile in (0, 1) if s == 8 else (2,):
                            rr = ROWS[tile]
                            for kd in range(2):
                                last = pe.matmul(ps_j[0:rr, (tile % 2) * D:(tile % 2 + 1) * D],
                                                 o2t[0:KD + kd, kd, FIRST[tile]:FIRST[tile] + rr],
                                                 wpj[0:KD + kd, kd, :], start=kd == 0, stop=kd == 1)
                        last.then_inc(S["proj_done"], 1)
                    if s in (10, 11) and has(i + 2):
                        c = s - 10
                        if c == 0:
                            pe.wait_ge(S["xh_done"], 3 * (i + 2) + 3)
                            wait_nearest(pe, [(i - 1, S["h2_done"], 3 * i), (i + 2, S["patch_used"], i + 3)])
                        else:
                            pe.wait_ge(S["xt_copied"], 2 * (i + 2) + 1)
                        turn(i, lambda tile, r, c: xh[0:r, tile, c * KD:(c + 1) * KD], c, S["xt_done"])
                    if s in (13, 14) and has(i - 1):
                        c = s - 13
                        if c == 0:
                            pe.wait_ge(S["xa_done"], 3 * i)
                            wait_nearest(pe, [(i + 2, S["xt_copied"], 2 * (i + 2) + 2), (i - 1, S["h2_done"], 3 * i)])
                        else:
                            pe.wait_ge(S["x2t_copied"], 2 * (i - 1) + 1)
                        turn(i, lambda tile, r, c: xa[0:r, tile, 0, c * KD:(c + 1) * KD], c, S["x2t_done"])
                    if s == 15 and has(i):
                        wait_nearest(pe, [(i - 1, S["x2t_copied"], 2 * i), (i + 2, S["xt_copied"], 2 * (i + 2) + 2)])
                        turn_outputs(i, 0)
                    if s == 16 and has(i - 1):
                        pe.wait_ge(S["x2t_copied"], 2 * (i - 1) + 2)
                        wait_nearest(pe, [(i, S["on_done"], 3 * i + 1)])
                        for tile in range(NT):
                            rr = ROWS[tile]
                            for kd in range(2):
                                last = pe.matmul(ps_j[0:rr, tile * E:(tile + 1) * E],
                                                 x2t[:, kd, FIRST[tile]:FIRST[tile] + rr], gt[:, kd, :],
                                                 start=kd == 0, stop=kd == 1)
                        last.then_inc(S["logit_done"], 1)
                    if s in (17, 18, 19, 21) and has(i + 2):
                        j = (17, 18, 19, 21).index(s)
                        if j == 0:
                            pe.wait_ge(S["xt_copied"], 2 * (i + 2) + 2)
                            wait_nearest(pe, [(i - 1, S["topi_done"], 3 * i), (i, S["on_done"], 3 * i + 1)])
                        elif j == 3:
                            wait_nearest(pe, [(i - 1, S["place_done"], i), (i + 2, S["qk_split"], 4 * (i + 2) + 3)])
                        else:
                            pe.wait_ge(S["qk_split"], 4 * (i + 2) + j)
                        for kd in range(2):
                            last = pe.matmul(ps_j[0:KD, 0:NP],
                                             wqkv[:, kd, (j // 2) * D + (j % 2) * KD:(j // 2) * D + (j % 2 + 1) * KD],
                                             xt[par][:, kd, :], start=kd == 0, stop=kd == 1)
                        last.then_inc(S["qk_done"], 1)
                    if s == 20 and has(i - 1):
                        wait_nearest(pe, [(i + 2, S["qk_split"], 4 * (i + 2) + 3), (i - 1, S["topi_done"], 3 * i)])
                        pe.wait_ge(S["both_done"], i)
                        m = both[:, :, :].rearrange("p t e -> p (t e)")
                        pe.matmul(ps_j[:, 0:NT * E], ut[:, :], m, start=True, stop=True)
                        pe.matmul(ps_j[:, NT * E:2 * NT * E], ones[:, :], m, start=True, stop=True)\
                            .then_inc(S["prefix_done"], 1)
                    if s == 23 and has(i + 1):
                        pe.wait_ge(S["m_split"], 2 * (i + 2))
                        wait_nearest(pe, [(i + 2, S["qk_split"], 4 * (i + 3)), (i - 1, S["place_done"], i),
                                          (i, S["on_done"], 3 * i + 1)])
                        for tile in range(NT):
                            rr = ROWS[tile]
                            last = pe.transpose(ps_j[0:2 * H, FIRST[tile]:FIRST[tile] + rr],
                                                negm2[0:rr, tile, :, :].rearrange("p l h -> p (l h)"), ident[0:rr, 0:rr])
                        last.then_inc(S["mt_done"], 1)
                    if s == 25 and has(i):
                        wait_nearest(pe, [(i + 1, S["mt_copied"], i + 2), (i - 1, S["place_done"], i),
                                          (i, S["on_done"], 3 * i + 1)])
                        turn_outputs(i, 1)
                    if s in (26, 27) and has(i + 1):
                        if s == 26:
                            wait_nearest(pe, [(i, S["on_done"], 3 * i + 2), (i + 1, S["mt_copied"], i + 2)])
                        else:
                            pe.wait_ge(S["v_copied"], 3 * (i + 1) + 2)
                        values(i, (0, 1) if s == 26 else (2,), par)
                    if pr == 1:
                        if u < 2:
                            if has(i - 1):
                                with_values(i - 1, 1 - par, 13 + u)
                        elif has(i):
                            with_values(i, par, u - 2)
                    if s in UNITS and has(i + 1):
                        maxima(i, par, UNITS.index(s), (2,))

            run_steps(pe, step)

        @block.vector
        def _(dve):
            def stats(b, src, stt, mv, s_stat, s_mv):
                hold(dve)
                for tile in range(NT):
                    r = ROWS[tile]
                    dve.bn_stats(stt[0:r, tile, :], src[0:r, b, tile, :]).then_inc(s_stat, 1)
                for tile in range(NT):
                    r = ROWS[tile]
                    wait(dve, s_stat, 3 * b + tile + 1)
                    hold(dve)
                    dve.bn_aggr(mv[0:r, tile, :], stt[0:r, tile, :]).then_inc(s_mv, 1)

            def maxima(b, unit, fills):
                g, tile, pr = unit // 6, unit % 6 // 2, unit % 2
                r = ROWS[tile]
                if unit == 0 and 0 in fills:
                    wait(dve, S["mx_comb"], b)
                for f in fills:
                    n = 3 * unit + f
                    c = tile * H + HG * g + 2 * pr
                    wait(dve, S["mx_filled"], 54 * b + n + 1)
                    if f < 2:
                        dve.tensor_reduce(mxp[0:r, c + f:c + f + 1, 0], ps_m[n % 2][0:r, 0:N], AX.X, ALU.max)\
                            .then_inc(S["mx_read"], 1)
                    else:
                        dve.tensor_reduce(mxp[0:r, c:c + 2, 1],
                                          ps_m[n % 2][0:r, 0:2 * SC].rearrange("p (e n) -> p e n", e=2),
                                          AX.X, ALU.max).then_inc(S["mx_read"], 1)

            def norm_outputs(b, g):
                o = ps_j[:, 0:NT * 128].rearrange("p (t h c) -> p t h c", t=NT, h=HG)
                wait(dve, S["ot_turned"], 3 * b + g + 1)
                dve.reciprocal(rec[:, :, :], o[:, :, :, DH]).then_inc(S["rec_done"], 1)
                wait(dve, S["rec_done"], 3 * b + g + 1)
                if g == 0:
                    wait(dve, S["on_turned"], 2 * b)
                w = HG * DH
                dve.tensor_tensor(on[:, :, g * w:(g + 1) * w].rearrange("p t (h c) -> p t h c", h=HG), o[:, :, :, 0:DH],
                                  rec[:, :, :].unsqueeze(3).broadcast_to([128, NT, HG, DH]), ALU.mult)\
                    .then_inc(S["on_done"], 1)

            def step(i, par):
                for s in range(30):
                    if s in UNITS and has(i + 1):
                        maxima(i + 1, UNITS.index(s), (0, 1))
                    if s == 4 and has(i + 2):
                        b = i + 2
                        wait(dve, S["patch_done"], b + 1)
                        dve.tensor_tensor(hs[0:ROWS[0], b, 0:2, :],
                                          ps_j[0:ROWS[0], 0:2 * D].rearrange("p (a d) -> p a d", a=2),
                                          posb[0:ROWS[0], :, :], ALU.add).then_inc(S["patch_used"], 1)
                        wait(dve, S["patch_used"], b + 1)
                        wait(dve, S["ln1_rstd"], b)
                        stats(b, hs, st1, mv1, S["ln1_stat"], S["ln1_mv"])
                    if s == 5 and has(i - 1):
                        norm_outputs(i - 1, 2)
                    if s in (8, 9) and has(i - 1):
                        b = i - 1
                        wait(dve, S["proj_done"], 2 * b + s - 7)
                        for tile in (0, 1) if s == 8 else (2,):
                            r = ROWS[tile]
                            dve.tensor_tensor(hs[0:r, b, tile, :], ps_j[0:r, (tile % 2) * D:(tile % 2 + 1) * D],
                                              hs[0:r, b, tile, :], ALU.add).then_inc(S["h2_done"], 1)
                        if s == 9:
                            wait(dve, S["h2_done"], 3 * b + 3)
                            wait(dve, S["ln2_rstd"], b)
                            stats(b, hs, st2, mv2, S["ln2_stat"], S["ln2_mv"])
                    if s == 8 and has(i + 2):
                        b = i + 2
                        wait(dve, S["ln1_rstd"], b + 1)
                        wait(dve, S["xt_done"], 2 * b)
                        for tile in range(NT):
                            r = ROWS[tile]
                            dve.tensor_scalar(xh[0:r, tile, :], hs[0:r, b, tile, :], mv1[0:r, tile, 0:1],
                                              rs1[0:r, tile:tile + 1], ALU.subtract, ALU.mult).then_inc(S["xh_done"], 1)
                    if s == 11 and has(i - 1):
                        b = i - 1
                        wait(dve, S["ln2_rstd"], b + 1)
                        wait(dve, S["sent"], 96 * b)
                        wait(dve, S["x2t_done"], 2 * b)
                        for tile in range(NT):
                            r = ROWS[tile]
                            dve.tensor_scalar(xa[0:r, tile, 0, 0:D], hs[0:r, b, tile, :], mv2[0:r, tile, 0:1],
                                              rs2[0:r, tile:tile + 1], ALU.subtract, ALU.mult).then_inc(S["xa_done"], 1)
                    if s == 15 and has(i):
                        norm_outputs(i, 0)
                    if s == 16 and has(i - 1):
                        b = i - 1
                        wait(dve, S["logit_done"], b + 1)
                        hold(dve)
                        for tile in range(NT):
                            r = ROWS[tile]
                            dve.max(top[0:r, tile, :], ps_j[0:r, tile * E:(tile + 1) * E]).then_inc(S["top_done"], 1)
                        for tile in range(NT):
                            r = ROWS[tile]
                            wait(dve, S["top_done"], 3 * b + tile + 1)
                            hold(dve)
                            dve.max_index(topi[0:r, tile, :], top[0:r, tile, :], ps_j[0:r, tile * E:(tile + 1) * E])\
                                .then_inc(S["topi_done"], 1)
                        wait(dve, S["topi_done"], 3 * b + 3)
                        dve.tensor_copy(topf[:, :, :], topi[:, :, 0:TOPK]).then_inc(S["topf_done"], 1)
                        wait(dve, S["topf_done"], b + 1)
                        full = [128, NT, TOPK, E]
                        dve.tensor_tensor(msk[:, :, :, :], iota8[:, :].unsqueeze(1).unsqueeze(1).broadcast_to(full),
                                          topf[:, :, :].unsqueeze(3).broadcast_to(full), ALU.is_equal)\
                            .then_inc(S["msk_done"], 1)
                        wait(dve, S["msk_done"], b + 1)
                        dve.tensor_tensor(both[:, :, :], msk[:, :, 0, :], msk[:, :, 1, :], ALU.add)\
                            .then_inc(S["both_done"], 1)
                    if s in (17, 18, 19, 21) and has(i + 2):
                        j = (17, 18, 19, 21).index(s)
                        wait(dve, S["qk_hi"], 4 * (i + 2) + j + 1)
                        dve.tensor_tensor(qp[:, j // 2, 1, j % 2, :], ps_j[0:KD, 0:NP],
                                          qp[:, j // 2, 0, j % 2, :].bitcast(F32), ALU.subtract)\
                            .then_inc(S["qk_split"], 1)
                    if s == 20 and has(i - 1):
                        b = i - 1
                        wait(dve, S["prefix_done"], b + 1)
                        for tile in range(NT):
                            wait(dve, S["base_step"], 4 * b + tile)
                            dve.tensor_tensor(base[:, tile + 1, :], ps_j[:, (NT + tile) * E:(NT + tile + 1) * E],
                                              base[:, tile, :], ALU.add).then_inc(S["base_step"], 1)
                        wait(dve, S["base_step"], 4 * b + NT)
                        dve.tensor_tensor(place[:, :, :], ps_j[:, 0:NT * E].rearrange("p (t e) -> p t e", t=NT),
                                          base[:, 0:NT, :], ALU.add).then_inc(S["place_done"], 1)
                        wait(dve, S["place_done"], b + 1)
                        dve.tensor_copy(base[:, 0, :], base[:, NT, :]).then_inc(S["base_step"], 1)
                        dve.tensor_tensor(pick[:, :, :, :], msk[:, :, :, :],
                                          place[:, :, :].unsqueeze(2).broadcast_to([128, NT, TOPK, E]), ALU.mult)\
                            .then_inc(S["pick_done"], 1)
                        wait(dve, S["pick_done"], b + 1)
                        dve.tensor_reduce(slotf[:, :, :], pick[:, :, :, :], AX.X, ALU.add).then_inc(S["slotf_done"], 1)
                        wait(dve, S["slotf_done"], b + 1)
                        wait(dve, S["sent"], 96 * b)
                        dve.tensor_copy(slot[:, :, :], slotf[:, :, :]).then_inc(S["slot_done"], 1)
                        dve.tensor_tensor(ex[:, :, :], top[:, :, :], top[:, :, 0:1].broadcast_to([128, NT, E]),
                                          ALU.subtract).then_inc(S["ex_sub"], 1)
                    if s == 22 and has(i + 1):
                        b = i + 1
                        wait(dve, S["mx_read"], 54 * b + 54)
                        wait(dve, S["mt_done"], b)
                        dve.tensor_reduce(negm[:, :, :].rearrange("p t h -> p (t h)"), mxp[:, :, :], AX.X, ALU.max,
                                          negate=True).then_inc(S["mx_comb"], 1)
                        wait(dve, S["mx_comb"], b + 1)
                        dve.tensor_copy(negm2[:, :, 0, :].bitcast(F32R), negm[:, :, :]).then_inc(S["m_split"], 1)
                        wait(dve, S["m_split"], 2 * b + 1)
                        dve.tensor_tensor(negm2[:, :, 1, :].bitcast(F32R), negm[:, :, :], negm2[:, :, 0, :],
                                          ALU.subtract).then_inc(S["m_split"], 1)
                    if s == 23 and has(i + 1):
                        b = i + 1
                        wait(dve, S["mt_done"], b + 1)
                        wait(dve, S["em_out"], 16 * b)
                        dve.tensor_copy(mr[:, 0:N], ps_j[0:2 * H, 0:N]).then_inc(S["mt_copied"], 1)
                    if s == 23 and has(i - 1):
                        b = i - 1
                        wait(dve, S["ex_done"], b + 1)
                        dve.tensor_reduce(zsum[:, :], ex[:, :, :], AX.X, ALU.add).then_inc(S["z_done"], 1)
                        wait(dve, S["z_done"], b + 1)
                        dve.scalar_tensor_tensor(out=den[:, :], in0=zsum[:, :], scalar=1e-9, in1=ex[:, :, 1],
                                                 op0=ALU.mult, op1=ALU.add).then_inc(S["den_a"], 1)
                        wait(dve, S["den_a"], b + 1)
                        dve.tensor_tensor(den[:, :], den[:, :], ex[:, :, 0], ALU.add).then_inc(S["den_done"], 1)
                        wait(dve, S["den_done"], b + 1)
                        dve.reciprocal(den[:, :], den[:, :]).then_inc(S["rden_done"], 1)
                        wait(dve, S["rden_done"], b + 1)
                        dve.tensor_tensor(gw[:, b, :, :], ex[:, :, 0:TOPK],
                                          den[:, :].unsqueeze(2).broadcast_to([128, NT, TOPK]), ALU.mult)\
                            .then_inc(S["gw_done"], 1)
                    if s == 25 and has(i):
                        norm_outputs(i, 1)
                    if s in UNITS and has(i + 1):
                        maxima(i + 1, UNITS.index(s), (2,))

            dve.memset(mxp[:, :, :], 0.0).then_inc(S["cleared"], 1)
            dve.memset(topi[:, :, :], 99).then_inc(S["cleared"], 1)
            dve.memset(top[:, :, :], 0.0).then_inc(S["cleared"], 1)
            dve.memset(mv1[:, :, :], 1.0).then_inc(S["cleared"], 1)
            dve.memset(mv2[:, :, :], 1.0).then_inc(S["cleared"], 1)
            dve.memset(mr[:, N:NP].bitcast(F32), 0.0).then_inc(S["cleared"], 1)
            dve.memset(ones[:, :], 1.0).then_inc(S["cleared"], 1)
            dve.memset(o2t[KD:KD + 1, :, :], 1.0).then_inc(S["cleared"], 1)
            dve.wait_ge(S["cleared"], 8)
            run_steps(dve, step)
            dve.wait_ge(S["gw_done"], B)


def routing(nc, sb, pb, sem, t):
    base, xs_d, table = t["base"], t["xs_d"], t["table"]
    with ExitStack() as st:
        zrow = sb(st, "zrow", [128, 2, ROW])
        start = sb(st, "start", [1, E])
        count = sb(st, "count", [1, E])
        counti = sb(st, "counti", [1, E], I32)
        nblk = sb(st, "nblk", [1, E])
        upto = sb(st, "upto", [1, E])
        skip = sb(st, "skip", [1, E])
        iblk = sb(st, "iblk", [1, NBLK])
        past = sb(st, "past", [1, NBLK, E])
        part = sb(st, "part", [1, NBLK, E])
        tabf = sb(st, "tabf", [1, 2, NBLK])
        nexti = sb(st, "nexti", [1, E], I32)
        made, chain, ready, listed, filled = (sem(st, f"ro_{n}") for n in ("made", "chain", "ready", "listed", "filled"))
        block = st.enter_context(nc.Block())

        @block.gpsimd
        def _(pool):
            pool.memset(zrow[:, :, 0:D], 0.0).then_inc(made, 1)
            pool.iota(zrow[:, :, D:ROW].bitcast(I32), pattern=[[0, 2], [0, 1]], base=SKIP,
                      channel_multiplier=0).then_inc(made, 1)
            pool.iota(start[:, :], pattern=[[REG, E]], base=0, channel_multiplier=0,
                      allow_small_or_imprecise_dtypes=True).then_inc(made, 1)
            pool.iota(iblk[:, :], pattern=[[1, NBLK]], base=0, channel_multiplier=0,
                      allow_small_or_imprecise_dtypes=True).then_inc(made, 1)

        @block.vector
        def _(dve):
            dve.wait_ge(made, 4)
            dve.tensor_copy(nexti[:, :], base[0:1, 0, :]).then_inc(ready, 1)
            dve.tensor_tensor(count[:, :], base[0:1, 0, :], start[:, :], ALU.subtract).then_inc(chain, 1)
            dve.wait_ge(chain, 1)
            dve.tensor_scalar(counti[:, :], count[:, :], float(BLK - 1), None, ALU.add).then_inc(chain, 1)
            dve.wait_ge(chain, 2)
            dve.tensor_scalar(counti[:, :], counti[:, :], BLK.bit_length() - 1, None, ALU.arith_shift_right)\
                .then_inc(chain, 1)
            dve.wait_ge(chain, 3)
            dve.tensor_copy(nblk[:, :], counti[:, :]).then_inc(chain, 1)
            dve.wait_ge(chain, 4)
            dve.tensor_scalar(skip[:, :], nblk[:, :], -float(BLK), float(REG), ALU.mult, ALU.add).then_inc(chain, 1)
            dve.tensor_copy(upto[:, 0:1], nblk[:, 0:1]).then_inc(chain, 1)
            for e in range(1, E):
                dve.wait_ge(chain, 5 + e)
                dve.tensor_tensor(upto[:, e:e + 1], nblk[:, e:e + 1], upto[:, e - 1:e], ALU.add).then_inc(chain, 1)
            dve.wait_ge(chain, 5 + E)
            full = [1, NBLK, E]
            dve.tensor_tensor(past[:, :, :], iblk[:, :].unsqueeze(2).broadcast_to(full),
                              upto[:, :].unsqueeze(1).broadcast_to(full), ALU.is_ge).then_inc(chain, 1)
            dve.wait_ge(chain, 6 + E)
            dve.tensor_tensor(part[:, :, :], past[:, :, :], skip[:, :].unsqueeze(1).broadcast_to(full), ALU.mult)\
                .then_inc(chain, 1)
            dve.tensor_reduce(tabf[:, 0, :], past[:, :, :], AX.X, ALU.add).then_inc(chain, 1)
            dve.wait_ge(chain, 7 + E)
            dve.tensor_reduce(tabf[:, 1, :], part[:, :, :], AX.X, ALU.add).then_inc(chain, 1)
            dve.wait_ge(chain, 9 + E)
            dve.tensor_scalar(tabf[:, 0, :], tabf[:, 0, :], float(E - 1), None, ALU.min).then_inc(chain, 1)
            dve.scalar_tensor_tensor(out=tabf[:, 1, :], in0=iblk[:, :], scalar=float(BLK), in1=tabf[:, 1, :],
                                     op0=ALU.mult, op1=ALU.add).then_inc(chain, 1)
            dve.wait_ge(chain, 11 + E)
            dve.tensor_scalar(tabf[:, 1, :], tabf[:, 1, :], float(E * REG), None, ALU.min).then_inc(chain, 1)
            dve.wait_ge(chain, 12 + E)
            dve.tensor_copy(table[:, :, :], tabf[:, :, :]).then_inc(listed, 1)
            dve.wait_ge(listed, 1)

        @block.sync
        def _(sp):
            sp.wait_ge(made, 2)
            sp.dma_start(xs_d[E * REG:XROWS, :].rearrange("(a p) n -> p a n", p=128), zrow[:, :, :]).then_inc(filled, 16)
            sp.wait_ge(ready, 1)
            for e in range(E):
                row = sp.value_load(nexti[0:1, e:e + 1], min_val=e * REG, max_val=e * REG + T)
                sp.dma_start(xs_d[bass.ds(row, BLK), :].rearrange("(a p) n -> p a n", p=128), zrow[:, :, :])\
                    .then_inc(filled, 16)
            sp.wait_ge(filled, 16 * (E + 1))


def experts(nc, sb, pb, sem, t):
    ident, xs_d, ys_d, table = t["ident"], t["xs_d"], t["ys_d"], t["table"]
    HC = HID // 128
    RING = 4
    with ExitStack() as st:
        xb = [sb(st, f"xb{p}", [128, 2, ROW]) for p in range(RING)]
        w1b = [sb(st, f"w1b{p}", [KD + 1, 2, HID]) for p in range(RING)]
        w2b = [sb(st, f"w2b{p}", [128, HC, D]) for p in range(RING)]
        b2b = [sb(st, f"b2b{p}", [128, D]) for p in range(RING)]
        xbt = [sb(st, f"xbt{p}", [KD + 1, 2, BLK]) for p in range(RING)]
        ht = [sb(st, f"ht{p}", [128, HC, BLK]) for p in range(RING)]
        yb = [sb(st, f"yb{p}", [128, 2, D]) for p in range(RING)]
        ps_t = pb(st, "ps_t", [128, 512])
        ps_h = [[pb(st, f"ps_h{p}{m}", [128, 512]) for m in range(HC // 2)] for p in range(2)]
        ps_y = pb(st, "ps_y", [128, 512])
        x_in = [sem(st, f"x_in{p}") for p in range(RING)]
        w1_in = [sem(st, f"w1_in{p}") for p in range(RING)]
        w2_in = [sem(st, f"w2_in{p}") for p in range(RING)]
        y_sent = [sem(st, f"y_sent{p}") for p in range(RING)]
        xt_done, xt_copied, h_done, h_act, y_done, y_sum, set_up = (
            sem(st, f"ex_{n}") for n in ("xt_done", "xt_copied", "h_done", "h_act", "y_done", "y_sum", "set_up"))
        block = st.enter_context(nc.Block())

        def after(blk, d=1):
            i, p, uses = blk
            return i + d, (p + d) % RING, uses + (p + d) // RING

        def run_blocks(eng, one):
            for i in range(RING):
                one((i, i, 0))
            turns = NBLK // RING
            with eng.Fori(1, turns - 1) as n:
                for p in range(RING):
                    one((n * RING + p, p, n))
            for i in range(RING * (turns - 1), NBLK):
                one((i, i % RING, i // RING))

        @block.sync
        def _(sp):
            def load(blk):
                i, p, uses = blk
                for done, value in ((xt_done, i - RING + 1), (y_done, i - RING + 1), (y_sum, i - RING + 1),
                                    (y_sent[p], 32 * uses)):
                    wait(sp, done, value)
                    hold(sp)
                e = sp.value_load(table[0:1, 0, bass.ds(i, 1)], min_val=0, max_val=E - 1)
                row = sp.value_load(table[0:1, 1, bass.ds(i, 1)], min_val=0, max_val=E * REG)
                sp.dma_start(xb[p][:, :, :], xs_d[bass.ds(row, BLK), :].rearrange("(a p) n -> p a n", p=128))\
                    .then_inc(x_in[p], 16)
                sp.dma_start(w1b[p][0:KD, :, :], t["w1"][bass.ds(e, 1)].rearrange("a (c p) n -> p (a c) n", c=2))\
                    .then_inc(w1_in[p], 16)
                sp.dma_start(w1b[p][KD:KD + 1, 1, :], t["b1"][bass.ds(e, 1), :]).then_inc(w1_in[p], 16)
                sp.dma_start(w2b[p][:, :, :], t["w2"][bass.ds(e, 1)].rearrange("a (c p) n -> p (a c) n", c=HC))\
                    .then_inc(w2_in[p], 16)
                sp.dma_start(b2b[p][:, :], t["b2"][bass.ds(e, 1), :].broadcast_to([128, D])).then_inc(w2_in[p], 16)

            run_blocks(sp, load)

        @block.tensor
        def _(pe):
            def turn(blk):
                i, p, uses = blk
                wait(pe, x_in[p], 16 * (uses + 1))
                wait(pe, xt_copied, i)
                for c in range(2):
                    for a in range(2):
                        last = pe.transpose(ps_t[0:KD, c * BLK + a * 128:c * BLK + a * 128 + 128],
                                            xb[p][:, a, c * KD:(c + 1) * KD], ident[:, :])
                last.then_inc(xt_done, 1)

            def up(blk):
                i, p, uses = blk
                wait(pe, xt_copied, i + 1)
                wait(pe, w1_in[p], 32 * (uses + 1))
                for m in range(HC):
                    bank = ps_h[p % 2][m // 2]
                    if m % 2 == 0:
                        wait(pe, h_act, 3 * (i - 2) + m // 2 + 1)
                    for c in range(2):
                        last = pe.matmul(bank[:, (m % 2) * BLK:(m % 2 + 1) * BLK], w1b[p][0:KD + c, c, m * 128:(m + 1) * 128],
                                         xbt[p][0:KD + c, c, :], start=c == 0, stop=c == 1)
                    if m % 2:
                        last.then_inc(h_done, 1)

            def down(blk):
                i, p, uses = blk
                wait(pe, w2_in[p], 32 * (uses + 1))
                wait(pe, h_act, 3 * i + 3)
                wait(pe, y_sum, i)
                for a in range(2):
                    for m in range(HC):
                        last = pe.matmul(ps_y[:, a * D:(a + 1) * D], ht[p][:, m, a * 128:(a + 1) * 128],
                                         w2b[p][:, m, :], start=m == 0, stop=m == HC - 1)
                last.then_inc(y_done, 1)

            def one(blk):
                if isinstance(blk[0], int) and blk[0] == 0:
                    turn(blk)
                    up(blk)
                    turn(after(blk))
                    return
                up(blk)
                if not isinstance(blk[0], int) or blk[0] + 1 < NBLK:
                    turn(after(blk))
                down(after(blk, -1))

            run_blocks(pe, one)
            down((NBLK - 1, (NBLK - 1) % RING, (NBLK - 1) // RING))

        @block.scalar
        def _(act):
            def one(blk):
                i, p, uses = blk
                wait(act, y_done, i - RING + 1)
                for m in range(HC // 2):
                    wait(act, h_done, 3 * i + m + 1)
                    act.activation(ht[p][:, 2 * m:2 * m + 2, :], ps_h[p % 2][m][:, :].rearrange("p (m n) -> p m n", m=2),
                                   ACT.Gelu).then_inc(h_act, 1)

            run_blocks(act, one)

        @block.vector
        def _(dve):
            def copy(blk):
                i, p, uses = blk
                wait(dve, xt_done, i + 1)
                wait(dve, h_done, 3 * (i - RING + 1))
                dve.tensor_copy(xbt[p][0:KD, :, :], ps_t[0:KD, :].rearrange("p (c n) -> p c n", c=2)).then_inc(xt_copied, 1)

            def finish(blk):
                i, p, uses = blk
                wait(dve, y_done, i + 1)
                wait(dve, w2_in[p], 32 * (uses + 1))
                wait(dve, y_sent[p], 32 * uses)
                dve.tensor_tensor(yb[p][:, :, :], ps_y[:, 0:2 * D].rearrange("p (a d) -> p a d", a=2),
                                  b2b[p][:, :].unsqueeze(1).broadcast_to([128, 2, D]), ALU.add).then_inc(y_sum, 1)

            def one(blk):
                if isinstance(blk[0], int) and blk[0] == 0:
                    copy(blk)
                    copy(after(blk))
                    return
                if not isinstance(blk[0], int) or blk[0] + 1 < NBLK:
                    copy(after(blk))
                finish(after(blk, -1))

            for p in range(RING):
                dve.memset(xbt[p][KD:KD + 1, :, :], 1.0).then_inc(set_up, 1)
            run_blocks(dve, one)
            finish((NBLK - 1, (NBLK - 1) % RING, (NBLK - 1) // RING))

        @block.gpsimd
        def _(pool):
            def one(blk):
                i, p, uses = blk
                wait(pool, y_sum, i + 1)
                hold(pool)
                for a in range(2):
                    pool.indirect_dma_start(
                        ys_d, bass.IndirectOffsetOnAxis(ap=xb[p][:, a, D:ROW].bitcast(I32), axis=0), yb[p][:, a, :], None,
                        bounds_check=TOPK * T - 1, oob_is_err=False).then_inc(y_sent[p], 16)

            run_blocks(pool, one)
            for p in range(RING):
                pool.wait_ge(y_sent[p], 32 * NBLK // RING)


def combine(nc, sb, pb, sem, t):
    hs, gw, ys_d, out = t["hs"], t["gw"], t["ys_d"], t["out"]
    BUF = 4
    with ExitStack() as st:
        yl = [sb(st, f"yl{p}", [128, NT, TOPK, D]) for p in range(BUF)]
        y_in = [sem(st, f"yl_in{p}") for p in range(BUF)]
        half, summed, stored = (sem(st, f"co_{n}") for n in ("half", "summed", "stored"))
        block = st.enter_context(nc.Block())

        @block.sync
        def _(sp):
            def load(b, p):
                wait(sp, summed, NT * (b - BUF + 1))
                for tile in range(NT):
                    r = ROWS[tile]
                    rows = ys_d.rearrange("(k n) d -> n k d", k=TOPK)
                    at = b * N + FIRST[tile]
                    sp.dma_start(yl[p][0:r, tile, :, :], rows[bass.ds(at, r)] if not isinstance(b, int) else rows[at:at + r])\
                        .then_inc(y_in[p], 16)

            for b in range(B):
                load(b, b % BUF)

        @block.vector
        def _(dve):
            for b in range(B):
                p = b % BUF
                dve.wait_ge(y_in[p], 48 * (b // BUF + 1))
                for k in range(TOPK):
                    for tile in range(NT):
                        r = ROWS[tile]
                        if k:
                            dve.wait_ge(half, NT * b + tile + 1)
                        dve.scalar_tensor_tensor(out=hs[0:r, b, tile, :], in0=yl[p][0:r, tile, k, :],
                                                 scalar=gw[0:r, b, tile, k:k + 1], in1=hs[0:r, b, tile, :],
                                                 op0=ALU.mult, op1=ALU.add).then_inc(summed if k else half, 1)

        @block.scalar
        def _(act):
            for b in range(B):
                act.wait_ge(summed, NT * b + 2)
                act.dma_start(out[b, 1:1 + ROWS[0], :], hs[0:ROWS[0], b, 0, :]).then_inc(stored, 16)
                act.dma_start(out[b, 1 + ROWS[0]:1 + NPATCH, :], hs[0:ROWS[0], b, 1, :]).then_inc(stored, 16)
                act.dma_start(out[b, 0:1, :], hs[ROWS[0]:ROWS[1], b, 1, :]).then_inc(stored, 16)
                act.wait_ge(summed, NT * b + 3)
                act.dma_start(out[b, NPATCH + 1:N, :], hs[0:TXT, b, 2, :]).then_inc(stored, 16)
            act.wait_ge(stored, 16 * 4 * B)


_INS = ['x', 'txt', 'L0_tok_W', 'L0_tok_b', 'L0_tok_class_token', 'L0_tok_pos_emb', 'L0_attn_sc_token', 'L0_attn_W_qkv',
        'L0_attn_W_proj', 'L0_attn_b_proj', 'L0_ffn_gate_w', 'L0_ffn_w1', 'L0_ffn_b1', 'L0_ffn_w2', 'L0_ffn_b2']


def kernel(**inputs):
    import numpy as _np
    import concourse.bacc as _bacc
    from concourse import mybir as _mybir
    from concourse.bass_utils import run_bass_kernel_spmd as _run

    nc = _bacc.Bacc("TRN2", target_bir_lowering=False, num_devices=1)
    arrays, args = {}, []
    for name in _INS:
        a = _np.ascontiguousarray(inputs[name])
        arrays[f"in_{name}_dram"] = a
        args.append(nc.dram_tensor(f"in_{name}_dram", a.shape, _mybir.dt.from_np(a.dtype), kind="ExternalInput").ap())
    res = nc.dram_tensor("out_0_dram", (B, N, D), _mybir.dt.float32, kind="ExternalOutput").ap()
    build(nc, *args, res)
    r = _run(nc, [arrays], core_ids=[0])
    return r.results[0]["out_0_dram"]
```

```python
import concourse.bass as bass
from concourse import mybir
from contextlib import ExitStack
import numpy as np

F32 = mybir.dt.float32
F32R = mybir.dt.float32r
I32 = mybir.dt.int32
U32 = mybir.dt.uint32
ALU = mybir.AluOpType
ACT = mybir.ActivationFunctionType
AX = mybir.AxisListType

B, CH, IMG, P = 16, 3, 224, 16
G = IMG // P
D, H, DH = 192, 12, 16
TXT = 128
SC = 196
NPATCH = G * G
N = NPATCH + 1 + TXT
NP = N + 1
ROWS = [NPATCH // 2, NPATCH // 2 + 1, TXT]
FIRST = [0, ROWS[0], ROWS[0] + ROWS[1]]
NT = 3
SCR = SC // 2
KD = D // 2
HG = 4
NG = H // HG
KC5 = NT + 2
PX = 8
E, HID, TOPK = 8, 768, 2
T = B * N
BLK = 256
NBLK = (T * TOPK + E * (BLK - 1)) // BLK
REG = T + BLK
XROWS = E * REG + BLK
ROW = D + 1
SCALE = float(DH) ** -0.5
LN_EPS = 1e-5
SKIP = 1 << 20
KMAX, KEXP = 126, 128
QK_SLOTS = (10, 11, 12, 14)
UNITS = [23, 24, 26, 27, 28, 30, 31, 32, 33, 35, 38, 39, 40, 41, 43, 44, 45, 46]


def has(b):
    return not isinstance(b, int) or 0 <= b < B


def wait(eng, sem, value):
    if isinstance(value, int) and value <= 0:
        return
    eng.wait_ge(sem, value)


def hold(eng):
    eng.nop(nofuse=True)


def unit_at(i, s):
    for b, slot in ((i + 1, s + 30), (i + 2, s)):
        if slot in UNITS and has(b):
            return b, UNITS.index(slot)
    return None


def wait_nearest(eng, candidates):
    for b, sem, value in candidates:
        if has(b):
            wait(eng, sem, value)
            return


def run_steps(eng, step):
    for i in (-2, -1, 0):
        step(i, i % 2)
    with eng.Fori(1, B - 4, 2) as i:
        step(i, 1)
        step(i + 1, 0)
    for i in range(B - 3, B + 1):
        step(i, i % 2)


def build(nc, x, txt, tok_w, tok_b, cls, pos, sc_tok, w_qkv, w_proj, b_proj, gate_w, w1, b1, w2, b2, out):
    eq_d = nc.dram_tensor("eq_d", [2, 2, 2, H, DH, NP], F32, kind="Internal").ap()
    em_d = nc.dram_tensor("em_d", [2, 2, H, NP], F32, kind="Internal").ap()
    ec_d = nc.dram_tensor("ec_d", [2, H, DH, SC], F32, kind="Internal").ap()
    xs_d = nc.dram_tensor("xs_d", [XROWS, ROW], F32, kind="Internal").ap()
    ys_d = nc.dram_tensor("ys_d", [TOPK * T, D], F32, kind="Internal").ap()

    keep = ExitStack()
    sb = lambda st, name, shape, dt=F32: st.enter_context(nc.sbuf_tensor(name, shape, dt))
    pb = lambda st, name, shape: st.enter_context(nc.psum_tensor(name, shape, F32))
    sem = lambda st, name: st.enter_context(nc.semaphore(name))

    with keep:
        hs = sb(keep, "hs", [128, B, NT, D])
        gw = sb(keep, "gw", [128, B, NT, TOPK])
        ident = sb(keep, "ident", [128, 128])
        base = sb(keep, "base", [128, NT + 1, E])

        table = sb(keep, "table", [1, 2, NBLK], I32)

        attend = ExitStack()
        with attend:
            wp = sb(attend, "wp", [KD, PX, D])
            posb = sb(attend, "posb", [ROWS[1], 2, D])
            wqkv = sb(attend, "wqkv", [KD, 2, 3 * D])
            wpj = sb(attend, "wpj", [KD + 1, 2, D])
            gt = sb(attend, "gt", [KD, 2, E])
            ut = sb(attend, "ut", [128, 128])
            ones = sb(attend, "ones", [128, 128])
            iota8 = sb(attend, "iota8", [128, E])
            halfneg = sb(attend, "halfneg", [128, NT])
            ids = sb(attend, "ids", [128, NT, TOPK])
            qs = [sb(attend, f"qs{p}", [KEXP, H, NP], F32R) for p in range(2)]
            ko = [sb(attend, f"ko{p}", [KEXP, H, NP], F32R) for p in range(2)]
            kc = sb(attend, "kc", [KEXP, H, SC], F32R)
            va = [sb(attend, f"va{p}", [128, NT, H, 32]) for p in range(2)]
            vc = sb(attend, "vc", [SCR, 2, H, 32])
            xt = [sb(attend, f"xt{p}", [KD, 2, NP]) for p in range(2)]
            img = sb(attend, "img", [KD, G, IMG])

            kc_in = sem(attend, "kc_in")
            setup(nc, sb, pb, sem, locals())
            attention(nc, sb, pb, sem, locals())
        experts(nc, sb, pb, sem, locals())
        combine(nc, sb, pb, sem, locals())


def store_rows(sp, out, hs, done):
    for b in range(B):
        sp.dma_start(out[b, 1:1 + ROWS[0], :], hs[0:ROWS[0], b, 0, :]).then_inc(done, 16)
        sp.dma_start(out[b, 1 + ROWS[0]:1 + NPATCH, :], hs[0:ROWS[0], b, 1, :]).then_inc(done, 16)
        sp.dma_start(out[b, 0:1, :], hs[ROWS[0]:ROWS[1], b, 1, :]).then_inc(done, 16)
        sp.dma_start(out[b, NPATCH + 1:N, :], hs[0:TXT, b, 2, :]).then_inc(done, 16)


def load_image(sp, x, img, b, done):
    for h in range(2):
        for c in range(CH):
            src = x[b, c].rearrange("(g y) w -> y g w", y=P)
            r = h * CH * P + c * P
            sp.dma_start(img[r:r + P, :, 0:IMG - PX * h], src[:, :, PX * h:IMG]).then_inc(done, 16)


def setup(nc, sb, pb, sem, t):
    hs, ident, base = t["hs"], t["ident"], t["base"]
    wp, posb, wqkv, wpj, gt, ut, ones = (t[k] for k in "wp posb wqkv wpj gt ut ones".split())
    iota8, halfneg, ids, qs, ko, kc, va, vc, xt = (t[k] for k in "iota8 halfneg ids qs ko kc va vc xt".split())
    ec_d, kc_in = t["ec_d"], t["kc_in"]
    with ExitStack() as st:
        wraw = sb(st, "wraw", [KD, 2, CH * P * P])
        wperm = sb(st, "wperm", [KD, 2, PX, 2, KD // 2])
        graw = sb(st, "graw", [E, D])
        sraw = sb(st, "sraw", [SCR, 2, D])
        bias = sb(st, "bias", [ROWS[1], 2, D])
        sct = sb(st, "sct", [KD, 2, SC])
        kcs = sb(st, "kcs", [KD, 2, 2, SC], F32R)
        ps = [pb(st, f"su{i}", [128, 512]) for i in range(4)]
        w_in, s_in, q_in, img0_in, p_in, b_in, h_in = (sem(st, f"su_{n}") for n in
                                                    ("w_in", "s_in", "q_in", "img0_in", "p_in", "b_in", "h_in"))
        zeroed, made, turned, copied = (sem(st, f"su_{n}") for n in ("zeroed", "made", "turned", "copied"))
        summed, hi_done, ec_out, cls_in, w_perm, v_made, k_made, q_zeroed = (
            sem(st, f"su_{n}") for n in ("summed", "hi_done", "ec_out", "cls_in", "w_perm", "v_made", "k_made", "q_zeroed"))
        block = st.enter_context(nc.Block())
        JOBS = PX + 1 + 2 + 2 + 2

        @block.sync
        def _(sp):
            sp.dma_start(wraw[:, :, :], t["tok_w"].rearrange("(h e) d -> e h d", h=2)).then_inc(w_in, 16)
            sp.dma_start(graw[:, :], t["gate_w"]).then_inc(s_in, 16)
            sp.dma_start(sraw[:, :, :], t["sc_tok"][0].rearrange("(a p) d -> p a d", a=2)).then_inc(s_in, 16)
            sp.dma_start(wqkv[:, :, :], t["w_qkv"].rearrange("(c p) n -> p c n", c=2)).then_inc(q_in, 16)
            pos = t["pos"]
            sp.dma_start(posb[0:ROWS[0], :, :],
                         pos[1:1 + NPATCH, :].rearrange("(a p) d -> p a d", a=2)).then_inc(p_in, 16)
            sp.dma_start(posb[ROWS[0]:ROWS[1], 1:2, :], pos[0:1, :].unsqueeze(1)).then_inc(p_in, 16)
            tb = t["tok_b"].unsqueeze(0)
            sp.dma_start(bias[0:ROWS[0], 0, :], tb.broadcast_to([ROWS[0], D])).then_inc(p_in, 16)
            sp.dma_start(bias[0:ROWS[0], 1, :], tb.broadcast_to([ROWS[0], D])).then_inc(p_in, 16)
            sp.dma_start(bias[ROWS[0]:ROWS[1], 1, :], t["cls"].unsqueeze(0)).then_inc(p_in, 16)
            load_image(sp, t["x"], t["img"], 0, img0_in)
            sp.dma_start(hs[:, :, 2, :], t["txt"].rearrange("b t d -> t b d")).then_inc(h_in, 16)
            sp.dma_start(wpj[0:KD, :, :], t["w_proj"].rearrange("(c p) n -> p c n", c=2)).then_inc(b_in, 16)
            sp.dma_start(wpj[KD:KD + 1, 1, :], t["b_proj"].unsqueeze(0)).then_inc(b_in, 16)
            sp.wait_ge(summed, 2)
            sp.dma_start(hs[ROWS[0]:ROWS[1], :, 1, :],
                         posb[ROWS[0]:ROWS[1], 1:2, :].broadcast_to([1, B, D])).then_inc(cls_in, 16)
            sp.wait_ge(summed, 4)
            for hl in range(2):
                sp.dma_start(ec_d[hl].rearrange("(c h) d n -> (h d) c n", c=2),
                             kcs[:, hl, :, :].bitcast(F32)).then_inc(ec_out, 16)
            sp.wait_ge(ec_out, 32)
            sp.wait_ge(k_made, 1)
            for s, hl in enumerate((0, 1, 0)):
                sp.dma_start(kc[DH * s:DH * s + DH, :, :].bitcast(F32),
                             ec_d[hl].rearrange("h d n -> d h n")).then_inc(kc_in, 16)
            sp.wait_ge(img0_in, 96)
            sp.wait_ge(cls_in, 16)
            sp.wait_ge(b_in, 32)
            sp.wait_ge(h_in, 16)

        @block.gpsimd
        def _(pool):
            pool.memset(ident[:, :], 0.0).then_inc(zeroed, 1)
            pool.memset(ut[:, :], 0.0).then_inc(zeroed, 1)
            pool.wait_ge(zeroed, 2)
            pool.affine_select(out=ident[:, :], in_=ident[:, :], compare_op=ALU.not_equal, fill=1.0, base=0,
                               pattern=[[-1, 128]], channel_multiplier=1).then_inc(made, 1)
            pool.affine_select(out=ut[:, :], in_=ut[:, :], compare_op=ALU.is_ge, fill=1.0, base=0,
                               pattern=[[-1, 128]], channel_multiplier=1).then_inc(made, 1)
            pool.iota(iota8[:, :], pattern=[[1, E]], base=0, channel_multiplier=0,
                      allow_small_or_imprecise_dtypes=True).then_inc(made, 1)
            pool.iota(base[:, 0, :], pattern=[[REG, E]], base=0, channel_multiplier=0,
                      allow_small_or_imprecise_dtypes=True).then_inc(made, 1)
            for tile in range(NT):
                pool.iota(ids[:, tile, :], pattern=[[T, TOPK]], base=FIRST[tile], channel_multiplier=1,
                          allow_small_or_imprecise_dtypes=True).then_inc(made, 1)
            pool.memset(halfneg[:, :], -0.5).then_inc(made, 1)
            for n, v in enumerate((vc, va[0], va[1])):
                pool.memset(v[:, :, :, :], 0.0).then_inc(zeroed, 1)
                pool.wait_ge(zeroed, 3 + n)
                pool.memset(v[:, :, :, DH:DH + 1], 1.0).then_inc(v_made, 1)
            for k in (kc, ko[0], ko[1]):
                pool.memset(k[:, :, :].bitcast(F32), 1.0).then_inc(k_made, 1)
            pool.wait_ge(made, 8)
            pool.wait_ge(v_made, 3)
            pool.wait_ge(k_made, 3)

        @block.tensor
        def _(pe):
            pe.wait_ge(made, 1)
            pe.wait_ge(w_perm, 2)
            job = 0
            for i in range(PX):
                if job >= 4:
                    pe.wait_ge(copied, job - 3)
                for eh in range(2):
                    last = pe.transpose(ps[job % 4][0:KD, eh * KD:(eh + 1) * KD],
                                        wperm[:, eh, i, :, :].rearrange("e j c -> e (j c)"), ident[0:KD, 0:KD])
                last.then_inc(turned, 1)
                job += 1
            pe.wait_ge(s_in, 32)
            pe.wait_ge(copied, job - 3)
            for c in range(2):
                last = pe.transpose(ps[job % 4][0:KD, c * E:(c + 1) * E], graw[:, c * KD:(c + 1) * KD], ident[0:E, 0:E])
            last.then_inc(turned, 1)
            job += 1
            for c in range(2):
                pe.wait_ge(copied, job - 3)
                for a in range(2):
                    last = pe.transpose(ps[job % 4][0:KD, a * SCR:(a + 1) * SCR], sraw[:, a, c * KD:(c + 1) * KD],
                                        ident[0:SCR, 0:SCR])
                last.then_inc(turned, 1)
                job += 1
            pe.wait_ge(q_in, 16)
            pe.wait_ge(copied, job)
            for c in range(2):
                for kd in range(2):
                    last = pe.matmul(ps[job % 4][0:KD, 0:SC], wqkv[:, kd, D + c * KD:D + (c + 1) * KD], sct[:, kd, :],
                                     start=kd == 0, stop=kd == 1)
                last.then_inc(turned, 1)
                job += 1
            for a in range(2):
                for kd in range(2):
                    last = pe.matmul(ps[job % 4][0:SCR, 0:D], sct[:, kd, a * SCR:(a + 1) * SCR], wqkv[:, kd, 2 * D:3 * D],
                                     start=kd == 0, stop=kd == 1)
                last.then_inc(turned, 1)
                job += 1
            assert job == JOBS

        @block.scalar
        def _(act):
            job = 0
            for i in range(PX):
                act.wait_ge(turned, job + 1)
                act.activation(wp[:, i, :], ps[job % 4][0:KD, 0:D], ACT.Copy).then_inc(copied, 1)
                job += 1
            act.wait_ge(turned, job + 1)
            act.activation(gt[:, :, :], ps[job % 4][0:KD, 0:2 * E].rearrange("p (c e) -> p c e", c=2),
                           ACT.Copy).then_inc(copied, 1)
            job += 1
            for c in range(2):
                act.wait_ge(turned, job + 1)
                act.activation(sct[:, c, :], ps[job % 4][0:KD, 0:SC], ACT.Copy).then_inc(copied, 1)
                job += 1
            for c in range(2):
                act.wait_ge(turned, job + 1)
                act.activation(kcs[:, 0, c, :], ps[job % 4][0:KD, 0:SC], ACT.Copy).then_inc(hi_done, 1)
                job += 1
            act.wait_ge(v_made, 1)
            for a in range(2):
                act.wait_ge(turned, job + 1)
                act.activation(vc[:, a, :, 0:DH], ps[job % 4][0:SCR, 0:D].rearrange("p (h d) -> p h d", h=H),
                               ACT.Copy).then_inc(copied, 1)
                job += 1
            act.wait_ge(copied, JOBS - 2)

        @block.vector
        def _(dve):
            for p in range(2):
                dve.memset(xt[p][:, :, N:NP], 0.0)
            dve.wait_ge(w_in, 16)
            for eh in range(2):
                dve.tensor_copy(wperm[:, eh, :, :, :],
                                wraw[:, eh, :].rearrange("e (c j i) -> e i j c", j=2, i=PX)).then_inc(w_perm, 1)
            dve.memset(qs[0][:, :, :].bitcast(F32), 0.0).then_inc(q_zeroed, 1)
            dve.wait_ge(p_in, 16 * 5)
            dve.tensor_tensor(posb[0:ROWS[0], 0, :], posb[0:ROWS[0], 0, :], bias[0:ROWS[0], 0, :],
                              ALU.add).then_inc(summed, 1)
            dve.tensor_tensor(posb[:, 1, :], posb[:, 1, :], bias[:, 1, :], ALU.add).then_inc(summed, 1)
            for c in range(2):
                dve.wait_ge(hi_done, c + 1)
                dve.tensor_tensor(kcs[:, 1, c, :], ps[(PX + 3 + c) % 4][0:KD, 0:SC], kcs[:, 0, c, :].bitcast(F32),
                                  ALU.subtract).then_inc(summed, 1)
            dve.memset(qs[1][:, :, :].bitcast(F32), 0.0).then_inc(q_zeroed, 1)
            dve.wait_ge(summed, 4)
            dve.wait_ge(q_zeroed, 2)


def attention(nc, sb, pb, sem, t):
    hs, gw, ident, base, table = (t[k] for k in "hs gw ident base table".split())
    wp, posb, wqkv, wpj, gt, ut, ones = (t[k] for k in "wp posb wqkv wpj gt ut ones".split())
    iota8, halfneg, ids, qs, ko, kc, va, vc, xt, img = (t[k] for k in "iota8 halfneg ids qs ko kc va vc xt img".split())
    x, eq_d, em_d, xs_d, kc_in = t["x"], t["eq_d"], t["em_d"], t["xs_d"], t["kc_in"]
    with ExitStack() as st:
        xh = sb(st, "xh", [128, NT, D])
        qp = sb(st, "qp", [KD, 2, 2, 2, NP], F32R)
        pt = sb(st, "pt", [128, 3, HG, N])
        ots = sb(st, "ots", [128, N])
        rec = sb(st, "rec", [128, NT, HG])
        on = sb(st, "on", [128, NT, D])
        o2t = sb(st, "o2t", [KD + 1, 2, N])
        mxp = sb(st, "mxp", [128, NT * H, 2])
        negm = sb(st, "negm", [128, NT, H])
        negm2 = sb(st, "negm2", [128, NT, 2, H])
        mr = sb(st, "mr", [2 * H, NP], F32R)
        xa = sb(st, "xa", [128, NT, TOPK, ROW])
        x2t = sb(st, "x2t", [KD, 2, N])
        st1 = sb(st, "st1", [128, NT, 6])
        mv1 = sb(st, "mv1", [128, NT, 2])
        rs1 = sb(st, "rs1", [128, NT])
        st2 = sb(st, "st2", [128, NT, 6])
        mv2 = sb(st, "mv2", [128, NT, 2])
        rs2 = sb(st, "rs2", [128, NT])
        top = sb(st, "top", [128, NT, E])
        topi = sb(st, "topi", [128, NT, E], U32)
        topf = sb(st, "topf", [128, NT, TOPK])
        msk = sb(st, "msk", [128, NT, TOPK, E])
        both = sb(st, "both", [128, NT, E])
        ex = sb(st, "ex", [128, NT, E])
        zsum = sb(st, "zsum", [128, NT])
        den = sb(st, "den", [128, NT])
        place = sb(st, "place", [128, NT, E])
        pick = sb(st, "pick", [128, NT, TOPK, E])
        slotf = sb(st, "slotf", [128, NT, TOPK])
        slot = sb(st, "slot", [128, NT, TOPK], I32)

        ps_s = [pb(st, f"ps_s{i}", [128, 512]) for i in range(2)]
        ps_m = [pb(st, f"ps_m{i}", [128, 512]) for i in range(3)]
        ps_o = pb(st, "ps_o", [128, 512])
        ps_j = [pb(st, f"ps_j{i}", [128, 512]) for i in range(2)]

        zrow = sb(st, "zrow", [128, 2, ROW])
        start = sb(st, "start", [1, E])
        nexti = sb(st, "nexti", [1, E], I32)
        count = sb(st, "count", [1, E])
        counti = sb(st, "counti", [1, E], I32)
        nblk = sb(st, "nblk", [1, E])
        upto = sb(st, "upto", [1, E])
        skip = sb(st, "skip", [1, E])
        iblk = sb(st, "iblk", [1, NBLK])
        past = sb(st, "past", [1, NBLK, E])
        part = sb(st, "part", [1, NBLK, E])
        tabf = sb(st, "tabf", [1, 2, NBLK])

        S = {}
        for n in """img_in patch_done patch_used ln1_stat ln1_mv ln1_eps ln1_rstd xh_done xt_done xt_copied
                    qk_done qk_hi qk_split eq_out q_in k_in v_done v_copied
                    mx_filled mx_read mx_comb m_split mt_done mt_copied em_out m_in
                    st_filled exp_done pv_done ot_copied ot_turned rec_done on_done on_turned o2_copied
                    proj_done h2_done ln2_stat ln2_mv ln2_eps ln2_rstd xa_done xa_copied ids_next x2t_done x2t_copied
                    logit_done top_done topi_done topf_done msk_done both_done prefix_done base_step place_done
                    pick_done slotf_done slot_done ex_sub ex_done z_done den_a den_done rden_done gw_done
                    sent cleared route_made listing rows_known listed padded""".split():
            S[n] = sem(st, n)
        g_in = [[sem(st, f"{n}_in{g}") for g in range(NG)] for n in "qk"]
        block = st.enter_context(nc.Block())


        @block.sync
        def _(sp):
            def expand(b, par, g):
                hh = slice(HG * g, HG * g + HG)
                for qk, dst, order in ((0, qs[par], (0, 0, 1)), (1, ko[par], (0, 1, 0))):
                    for s, hl in enumerate(order):
                        sp.dma_start(dst[DH * s:DH * s + DH, hh, :].bitcast(F32),
                                     eq_d[par, qk, hl, hh].rearrange("h d n -> d h n")).then_inc(g_in[qk][g], 16)

            def step(i, par):
                if has(i + 3):
                    wait(sp, S["patch_done"], i + 3)
                    hold(sp)
                    load_image(sp, x, img, i + 3, S["img_in"])
                if has(i + 2):
                    wait(sp, S["qk_split"], 4 * (i + 2) + 4)
                    hold(sp)
                    for g in range(NG):
                        for qk in range(2):
                            wait(sp, g_in[qk][g], 48 * (i + 1) if not isinstance(i, int) or i >= 0 else 0)
                            hold(sp)
                    for qk in range(2):
                        for hl in range(2):
                            sp.dma_start(eq_d[par, qk, hl].rearrange("(c h) d n -> (h d) c n", c=2),
                                         qp[:, qk, hl, :, :].bitcast(F32)).then_inc(S["eq_out"], 16)
                if has(i + 2):
                    wait(sp, S["eq_out"], 64 * (i + 3))
                    hold(sp)
                    wait(sp, S["st_filled"], 60 * i + 20)
                    hold(sp)
                    expand(i + 2, par, 0)
                if has(i + 1):
                    wait(sp, S["mt_copied"], i + 2)
                    hold(sp)
                    sp.dma_start(em_d[1 - par].rearrange("l h n -> (l h) n"), mr[:, :].bitcast(F32)).then_inc(S["em_out"], 16)
                if has(i + 2):
                    wait(sp, S["st_filled"], 60 * i + 40)
                    hold(sp)
                    expand(i + 2, par, 1)
                if has(i + 1):
                    wait(sp, S["em_out"], 16 * (i + 2))
                    hold(sp)
                    sp.dma_start(qs[1 - par][KMAX:KEXP, :, :].bitcast(F32), em_d[1 - par]).then_inc(S["m_in"], 16)
                if has(i + 2):
                    wait(sp, S["st_filled"], 60 * i + 60)
                    hold(sp)
                    expand(i + 2, par, 2)

            run_steps(sp, step)
            sp.wait_ge(S["route_made"], 2)
            sp.dma_start(xs_d[E * REG:XROWS, :].rearrange("(a p) n -> p a n", p=128), zrow[:, :, :]).then_inc(S["padded"], 16)
            sp.wait_ge(S["rows_known"], 1)
            for e in range(E):
                row = sp.value_load(nexti[0:1, e:e + 1], min_val=e * REG, max_val=e * REG + T)
                sp.dma_start(xs_d[bass.ds(row, BLK), :].rearrange("(a p) n -> p a n", p=128), zrow[:, :, :])\
                    .then_inc(S["padded"], 16)
            sp.wait_ge(S["padded"], 16 * (E + 1))

        @block.gpsimd
        def _(pool):
            def rstd(b, mv, rs, mv_done, eps_done, rstd_done):
                wait(pool, mv_done, 3 * b + 3)
                hold(pool)
                pool.tensor_scalar(rs[:, :], mv[:, :, 1], LN_EPS, None, ALU.add).then_inc(eps_done, 1)
                wait(pool, eps_done, b + 1)
                hold(pool)
                pool.tensor_tensor(rs[:, :], rs[:, :], halfneg[:, :], ALU.pow).then_inc(rstd_done, 1)

            def step(i, par):
                if has(i + 2):
                    rstd(i + 2, mv1, rs1, S["ln1_mv"], S["ln1_eps"], S["ln1_rstd"])
                if has(i - 1):
                    rstd(i - 1, mv2, rs2, S["ln2_mv"], S["ln2_eps"], S["ln2_rstd"])
                    for tile in range(NT):
                        wait(pool, S["xa_done"], 3 * (i - 1) + tile + 1)
                        hold(pool)
                        r = ROWS[tile]
                        pool.tensor_copy(xa[0:r, tile, 1, 0:D], xa[0:r, tile, 0, 0:D]).then_inc(S["xa_copied"], 1)
                    pool.tensor_copy(xa[:, :, :, D:ROW].bitcast(I32), ids[:, :, :].unsqueeze(3)).then_inc(S["xa_copied"], 1)
                    pool.tensor_scalar(ids[:, :, :], ids[:, :, :], float(N), None, ALU.add).then_inc(S["ids_next"], 1)
                    wait(pool, S["slot_done"], i)
                    wait(pool, S["xa_copied"], 4 * i)
                    hold(pool)
                    for tile in range(NT):
                        for k in range(TOPK):
                            r = ROWS[tile]
                            pool.indirect_dma_start(
                                xs_d, bass.IndirectOffsetOnAxis(ap=slot[0:r, tile, k:k + 1], axis=0),
                                xa[0:r, tile, k, :], None).then_inc(S["sent"], 16)

            pool.memset(zrow[:, :, 0:D], 0.0).then_inc(S["route_made"], 1)
            pool.iota(zrow[:, :, D:ROW].bitcast(I32), pattern=[[0, 2], [0, 1]], base=SKIP,
                      channel_multiplier=0).then_inc(S["route_made"], 1)
            pool.iota(start[:, :], pattern=[[REG, E]], base=0, channel_multiplier=0,
                      allow_small_or_imprecise_dtypes=True).then_inc(S["route_made"], 1)
            pool.iota(iblk[:, :], pattern=[[1, NBLK]], base=0, channel_multiplier=0,
                      allow_small_or_imprecise_dtypes=True).then_inc(S["route_made"], 1)
            run_steps(pool, step)
            pool.wait_ge(S["sent"], 16 * 6 * B)

        @block.scalar
        def _(act):
            def step(i, par):
                for s in range(30):
                    if has(i):
                        u, pr = s // 2, s % 2
                        kcn = u % KC5
                        r = ROWS[kcn] if kcn < NT else SCR
                        if pr == 0:
                            wait(act, S["pv_done"], 15 * i + u - 2)
                        for e in range(2):
                            wait(act, S["st_filled"], 60 * i + 2 * s + e + 1)
                            act.activation(pt[0:r, u % 3, 2 * pr + e, :], ps_s[e][0:r, 0:N], ACT.Exp,
                                           scale=SCALE).then_inc(S["exp_done"], 1)
                    if s in (3, 13, 23):
                        b, g = (i - 1, 2) if s == 3 else (i, s // 10 - 1)
                        if has(b):
                            wait(act, S["pv_done"], 15 * b + 5 * g + 5)
                            wait(act, S["ot_turned"], 3 * b + g)
                            act.activation(ots[:, :], ps_o[:, 0:N], ACT.Copy).then_inc(S["ot_copied"], 1)
                    if s in (8, 9) and has(i + 2):
                        c = s - 8
                        wait(act, S["xt_done"], 2 * (i + 2) + c + 1)
                        act.activation(xt[par][:, c, 0:N], ps_j[c][0:KD, 0:N], ACT.Copy).then_inc(S["xt_copied"], 1)
                    if s in (6, 7) and has(i - 1):
                        c = s - 6
                        wait(act, S["on_turned"], 2 * (i - 1) + c + 1)
                        wait(act, S["proj_done"], 2 * (i - 1))
                        act.activation(o2t[0:KD, c, :], ps_j[c][0:KD, 0:N], ACT.Copy).then_inc(S["o2_copied"], 1)
                    if s == 19 and has(i + 1):
                        b = i + 1
                        wait(act, S["mt_done"], b + 1)
                        wait(act, S["em_out"], 16 * b)
                        act.activation(mr[:, 0:N], ps_j[1][0:2 * H, 0:N], ACT.Copy).then_inc(S["mt_copied"], 1)
                    if s in (20, 21) and has(i - 1):
                        c = s - 20
                        wait(act, S["x2t_done"], 2 * (i - 1) + c + 1)
                        wait(act, S["logit_done"], i - 1)
                        act.activation(x2t[:, c, :], ps_j[c][0:KD, 0:N], ACT.Copy).then_inc(S["x2t_copied"], 1)
                    if s in QK_SLOTS and has(i + 2):
                        j = QK_SLOTS.index(s)
                        wait(act, S["qk_done"], 4 * (i + 2) + j + 1)
                        wait(act, S["eq_out"], 64 * (i + 2))
                        act.activation(qp[:, j // 2, 0, j % 2, :], ps_j[j % 2][0:KD, 0:NP], ACT.Copy).then_inc(S["qk_hi"], 1)
                    if s == 24 and has(i - 1):
                        wait(act, S["ex_sub"], i)
                        act.activation(ex[:, :, :], ex[:, :, :], ACT.Exp).then_inc(S["ex_done"], 1)
                    if s in (26, 27) and has(i + 1):
                        vp = va[1 - par]
                        wait(act, S["v_done"], 2 * (i + 1) + s - 25)
                        for tile in (0, 1) if s == 26 else (2,):
                            r = ROWS[tile]
                            a = tile % 2
                            act.activation(vp[0:r, tile, :, 0:DH],
                                           ps_j[27 - s][0:r, a * D:(a + 1) * D].rearrange("p (h d) -> p h d", h=H),
                                           ACT.Copy).then_inc(S["v_copied"], 1)

            run_steps(act, step)

        @block.tensor
        def _(pe):
            def patches(i, tile, lo, hi_):
                for p in range(lo, hi_):
                    last = pe.matmul(ps_j[0][0:ROWS[0], tile * D:(tile + 1) * D],
                                     img[:, 7 * tile:7 * tile + 7, :].rearrange("k g (w q) -> k q (g w)", q=P)[:, p],
                                     wp[:, p, :], start=p == 0, stop=p == PX - 1)
                return last

            def turn(i, src, c, done):
                for tile in range(NT):
                    r = ROWS[tile]
                    last = pe.transpose(ps_j[c][0:KD, FIRST[tile]:FIRST[tile] + r], src(tile, r, c), ident[0:r, 0:r])
                last.then_inc(done, 1)

            def turn_outputs(b, g):
                pe.wait_ge(S["ot_copied"], 3 * b + g + 1)
                for tile in range(NT):
                    last = pe.transpose(ps_j[g // 2][:, 128 * tile:128 * tile + 128], ots[:, FIRST[tile]:FIRST[tile] + 128],
                                        ident[:, :])
                last.then_inc(S["ot_turned"], 1)

            def values(i, tiles, par):
                for tile in tiles:
                    r = ROWS[tile]
                    for kd in range(2):
                        last = pe.matmul(ps_j[0 if tile == 2 else 1][0:r, (tile % 2) * D:(tile % 2 + 1) * D],
                                         xt[1 - par][:, kd, FIRST[tile]:FIRST[tile] + r], wqkv[:, kd, 2 * D:3 * D],
                                         start=kd == 0, stop=kd == 1)
                last.then_inc(S["v_done"], 1)

            def with_values(b, par, u):
                g, kcn = u // KC5, u % KC5
                wait(pe, S["exp_done"], 60 * b + 4 * u + 4)
                if kcn == 0:
                    wait(pe, S["ot_copied"], 3 * b + g)
                    if g == 0:
                        wait(pe, S["v_copied"], 3 * b + 3)
                for j in range(HG):
                    h = HG * g + j
                    r = ROWS[kcn] if kcn < NT else SCR
                    v = va[par][0:r, kcn, h, :] if kcn < NT else vc[:, kcn - NT, h, :]
                    last = pe.matmul(ps_o[32 * j:32 * j + 32, 0:N], v, pt[0:r, u % 3, j, :],
                                     start=kcn == 0, stop=kcn == KC5 - 1)
                last.then_inc(S["pv_done"], 1)

            def maxima(b, par, unit, fills):
                g, tile, pr = unit // 6, unit % 6 // 2, unit % 2
                r = ROWS[tile]
                if unit % 6 == 0 and 0 in fills:
                    pe.wait_ge(g_in[0][g], 48 * (b + 1))
                    pe.wait_ge(g_in[1][g], 48 * (b + 1))
                    if isinstance(b, int) and b == 0:
                        pe.wait_ge(kc_in, 48)
                for f in fills:
                    n = 3 * unit + f
                    bank = ps_m[n % 3]
                    wait(pe, S["mx_read"], 54 * b + n - 2)
                    for e in ((f,) if f < 2 else (0, 1)):
                        h = HG * g + 2 * pr + e
                        q = qs[par][0:KMAX, h, FIRST[tile]:FIRST[tile] + r]
                        if f < 2:
                            last = pe.matmul(bank[0:r, 0:NP], q, ko[par][0:KMAX, h, :], start=True, stop=True)
                        else:
                            last = pe.matmul(bank[0:r, e * SC:(e + 1) * SC], q, kc[0:KMAX, h, :], start=True, stop=True)
                    last.then_inc(S["mx_filled"], 1)

            def step(i, par):
                for s in range(30):
                    u, pr = s // 2, s % 2
                    if has(i):
                        g, kcn = u // KC5, u % KC5
                        r = ROWS[kcn] if kcn < NT else SCR
                        if s == 0:
                            pe.wait_ge(S["m_in"], 16 * (i + 1))
                        for e in range(2):
                            n = 2 * s + e
                            wait(pe, S["exp_done"], 60 * i + n - 1)
                            h = HG * g + 2 * pr + e
                            k = ko[par][:, h, FIRST[kcn]:FIRST[kcn] + r] if kcn < NT else \
                                kc[:, h, (kcn - NT) * SCR:(kcn - NT + 1) * SCR]
                            pe.matmul(ps_s[e][0:r, 0:NP], k, qs[par][:, h, :], start=True, stop=True)\
                                .then_inc(S["st_filled"], 1)
                    unit = unit_at(i, s)
                    if unit:
                        maxima(unit[0], par if s in UNITS else 1 - par, unit[1], (0,))
                    if s < 4 and has(i + 2):
                        if s == 0:
                            wait_nearest(pe, [(i, S["v_copied"], 3 * i + 3),
                                              (i + 1, S["qk_split"], 4 * (i + 1) + 3)])
                            wait(pe, S["img_in"], 96 * (i + 2))
                        last = patches(i, s // 2, 4 * (s % 2), 4 * (s % 2) + 4)
                        if s == 3:
                            last.then_inc(S["patch_done"], 1)
                    if s == 5 and has(i - 1):
                        wait_nearest(pe, [(i, S["v_copied"], 3 * i + 2), (i - 2, S["place_done"], i - 1)])
                        turn_outputs(i - 1, 2)
                    if s in (6, 7) and has(i - 1):
                        c = s - 6
                        if c == 0:
                            pe.wait_ge(S["on_done"], 3 * i)
                            wait_nearest(pe, [(i + 2, S["patch_used"], i + 3), (i, S["v_copied"], 3 * i + 3),
                                              (i - 1, S["on_done"], 3 * i - 1)])
                        turn(i, lambda tile, r, c: on[0:r, tile, c * KD:(c + 1) * KD], c, S["on_turned"])
                    if s in (16, 17) and has(i - 1):
                        if s == 16:
                            pe.wait_ge(S["o2_copied"], 2 * i)
                            wait_nearest(pe, [(i + 2, S["qk_split"], 4 * (i + 3))])
                        else:
                            wait_nearest(pe, [(i, S["on_done"], 3 * i + 1)])
                        for tile in (0, 1) if s == 16 else (2,):
                            rr = ROWS[tile]
                            for kd in range(2):
                                last = pe.matmul(ps_j[17 - s][0:rr, (tile % 2) * D:(tile % 2 + 1) * D],
                                                 o2t[0:KD + kd, kd, FIRST[tile]:FIRST[tile] + rr],
                                                 wpj[0:KD + kd, kd, :], start=kd == 0, stop=kd == 1)
                        last.then_inc(S["proj_done"], 1)
                    if s in (8, 9) and has(i + 2):
                        c = s - 8
                        if c == 0:
                            pe.wait_ge(S["xh_done"], 3 * (i + 2) + 3)
                            wait_nearest(pe, [(i - 1, S["o2_copied"], 2 * i - 1), (i + 2, S["patch_used"], i + 3)])
                        else:
                            wait_nearest(pe, [(i - 1, S["o2_copied"], 2 * i), (i, S["v_copied"], 3 * i + 2),
                                              (i + 1, S["qk_split"], 4 * (i + 2))])
                        turn(i, lambda tile, r, c: xh[0:r, tile, c * KD:(c + 1) * KD], c, S["xt_done"])
                    if s in (20, 21) and has(i - 1):
                        c = s - 20
                        if c == 0:
                            pe.wait_ge(S["xa_done"], 3 * i)
                        else:
                            wait_nearest(pe, [(i + 1, S["mt_copied"], i + 2), (i - 1, S["h2_done"], 3 * i - 1)])
                        turn(i, lambda tile, r, c: xa[0:r, tile, 0, c * KD:(c + 1) * KD], c, S["x2t_done"])
                    if s == 15 and has(i):
                        wait_nearest(pe, [(i + 2, S["qk_split"], 4 * (i + 2) + 3), (i - 1, S["o2_copied"], 2 * i - 1)])
                        turn_outputs(i, 0)
                    if s == 22 and has(i - 1):
                        pe.wait_ge(S["x2t_copied"], 2 * (i - 1) + 2)
                        for tile in range(NT):
                            rr = ROWS[tile]
                            for kd in range(2):
                                last = pe.matmul(ps_j[0][0:rr, tile * E:(tile + 1) * E],
                                                 x2t[:, kd, FIRST[tile]:FIRST[tile] + rr], gt[:, kd, :],
                                                 start=kd == 0, stop=kd == 1)
                        last.then_inc(S["logit_done"], 1)
                    if s in QK_SLOTS and has(i + 2):
                        j = QK_SLOTS.index(s)
                        if j == 0:
                            pe.wait_ge(S["xt_copied"], 2 * (i + 2) + 2)
                        elif j >= 2:
                            pe.wait_ge(S["qk_split"], 4 * (i + 2) + j - 1)
                        for kd in range(2):
                            last = pe.matmul(ps_j[j % 2][0:KD, 0:NP],
                                             wqkv[:, kd, (j // 2) * D + (j % 2) * KD:(j // 2) * D + (j % 2 + 1) * KD],
                                             xt[par][:, kd, :], start=kd == 0, stop=kd == 1)
                        last.then_inc(S["qk_done"], 1)
                    if s == 24 and has(i - 1):
                        pe.wait_ge(S["both_done"], i)
                        m = both[:, :, :].rearrange("p t e -> p (t e)")
                        pe.matmul(ps_j[1][:, 0:NT * E], ut[:, :], m, start=True, stop=True)
                        pe.matmul(ps_j[1][:, NT * E:2 * NT * E], ones[:, :], m, start=True, stop=True)\
                            .then_inc(S["prefix_done"], 1)
                    if s == 19 and has(i + 1):
                        pe.wait_ge(S["m_split"], 2 * (i + 2))
                        wait_nearest(pe, [(i - 1, S["h2_done"], 3 * i - 1), (i + 2, S["qk_split"], 4 * (i + 3))])
                        for tile in range(NT):
                            rr = ROWS[tile]
                            last = pe.transpose(ps_j[1][0:2 * H, FIRST[tile]:FIRST[tile] + rr],
                                                negm2[0:rr, tile, :, :].rearrange("p l h -> p (l h)"), ident[0:rr, 0:rr])
                        last.then_inc(S["mt_done"], 1)
                    if s == 25 and has(i):
                        wait_nearest(pe, [(i - 1, S["topi_done"], 3 * i), (i, S["on_done"], 3 * i + 1)])
                        turn_outputs(i, 1)
                    if s in (26, 27) and has(i + 1):
                        if s == 26:
                            wait_nearest(pe, [(i - 1, S["place_done"], i), (i + 1, S["mt_copied"], i + 2)])
                        else:
                            wait_nearest(pe, [(i, S["on_done"], 3 * i + 2), (i + 2, S["qk_split"], 4 * (i + 2) + 3)])
                        values(i, (0, 1) if s == 26 else (2,), par)
                    if pr == 1:
                        if u < 2:
                            if has(i - 1):
                                with_values(i - 1, 1 - par, 13 + u)
                        elif has(i):
                            with_values(i, par, u - 2)
                    if unit:
                        maxima(unit[0], par if s in UNITS else 1 - par, unit[1], (1, 2))

            run_steps(pe, step)

        @block.vector
        def _(dve):
            def stats(b, src, stt, mv, s_stat, s_mv):
                hold(dve)
                for tile in range(NT):
                    r = ROWS[tile]
                    dve.bn_stats(stt[0:r, tile, :], src[0:r, b, tile, :]).then_inc(s_stat, 1)
                for tile in range(NT):
                    r = ROWS[tile]
                    wait(dve, s_stat, 3 * b + tile + 1)
                    hold(dve)
                    dve.bn_aggr(mv[0:r, tile, :], stt[0:r, tile, :]).then_inc(s_mv, 1)

            def maxima(b, unit, fills):
                g, tile, pr = unit // 6, unit % 6 // 2, unit % 2
                r = ROWS[tile]
                if unit == 0 and 0 in fills:
                    wait(dve, S["mx_comb"], b)
                for f in fills:
                    n = 3 * unit + f
                    c = tile * H + HG * g + 2 * pr
                    wait(dve, S["mx_filled"], 54 * b + n + 1)
                    if f < 2:
                        dve.tensor_reduce(mxp[0:r, c + f:c + f + 1, 0], ps_m[n % 3][0:r, 0:N], AX.X, ALU.max)\
                            .then_inc(S["mx_read"], 1)
                    else:
                        dve.tensor_reduce(mxp[0:r, c:c + 2, 1],
                                          ps_m[n % 3][0:r, 0:2 * SC].rearrange("p (e n) -> p e n", e=2),
                                          AX.X, ALU.max).then_inc(S["mx_read"], 1)

            def norm_outputs(b, g):
                o = ps_j[g // 2][:, 0:NT * 128].rearrange("p (t h c) -> p t h c", t=NT, h=HG)
                wait(dve, S["ot_turned"], 3 * b + g + 1)
                dve.reciprocal(rec[:, :, :], o[:, :, :, DH]).then_inc(S["rec_done"], 1)
                wait(dve, S["rec_done"], 3 * b + g + 1)
                if g == 0:
                    wait(dve, S["on_turned"], 2 * b)
                w = HG * DH
                dve.tensor_tensor(on[:, :, g * w:(g + 1) * w].rearrange("p t (h c) -> p t h c", h=HG), o[:, :, :, 0:DH],
                                  rec[:, :, :].unsqueeze(3).broadcast_to([128, NT, HG, DH]), ALU.mult)\
                    .then_inc(S["on_done"], 1)

            def step(i, par):
                for s in range(30):
                    unit = unit_at(i, s)
                    if unit:
                        maxima(unit[0], unit[1], (0,))
                    if s == 4 and has(i + 2):
                        b = i + 2
                        wait(dve, S["patch_done"], b + 1)
                        dve.tensor_tensor(hs[0:ROWS[0], b, 0:2, :],
                                          ps_j[0][0:ROWS[0], 0:2 * D].rearrange("p (a d) -> p a d", a=2),
                                          posb[0:ROWS[0], :, :], ALU.add).then_inc(S["patch_used"], 1)
                        wait(dve, S["patch_used"], b + 1)
                        wait(dve, S["ln1_rstd"], b)
                        stats(b, hs, st1, mv1, S["ln1_stat"], S["ln1_mv"])
                    if s == 5 and has(i - 1):
                        norm_outputs(i - 1, 2)
                    if s in (16, 17) and has(i - 1):
                        b = i - 1
                        wait(dve, S["proj_done"], 2 * b + s - 15)
                        for tile in (0, 1) if s == 16 else (2,):
                            r = ROWS[tile]
                            dve.tensor_tensor(hs[0:r, b, tile, :], ps_j[17 - s][0:r, (tile % 2) * D:(tile % 2 + 1) * D],
                                              hs[0:r, b, tile, :], ALU.add).then_inc(S["h2_done"], 1)
                        if s == 17:
                            wait(dve, S["h2_done"], 3 * b + 3)
                            wait(dve, S["ln2_rstd"], b)
                            stats(b, hs, st2, mv2, S["ln2_stat"], S["ln2_mv"])
                    if s == 6 and has(i + 2):
                        b = i + 2
                        wait(dve, S["ln1_rstd"], b + 1)
                        wait(dve, S["xt_done"], 2 * b)
                        for tile in range(NT):
                            r = ROWS[tile]
                            dve.tensor_scalar(xh[0:r, tile, :], hs[0:r, b, tile, :], mv1[0:r, tile, 0:1],
                                              rs1[0:r, tile:tile + 1], ALU.subtract, ALU.mult).then_inc(S["xh_done"], 1)
                    if s == 19 and has(i - 1):
                        b = i - 1
                        wait(dve, S["ln2_rstd"], b + 1)
                        wait(dve, S["sent"], 96 * b)
                        wait(dve, S["x2t_done"], 2 * b)
                        for tile in range(NT):
                            r = ROWS[tile]
                            dve.tensor_scalar(xa[0:r, tile, 0, 0:D], hs[0:r, b, tile, :], mv2[0:r, tile, 0:1],
                                              rs2[0:r, tile:tile + 1], ALU.subtract, ALU.mult).then_inc(S["xa_done"], 1)
                    if s == 15 and has(i):
                        norm_outputs(i, 0)
                    if s == 22 and has(i - 1):
                        b = i - 1
                        wait(dve, S["logit_done"], b + 1)
                        hold(dve)
                        for tile in range(NT):
                            r = ROWS[tile]
                            dve.max(top[0:r, tile, :], ps_j[0][0:r, tile * E:(tile + 1) * E]).then_inc(S["top_done"], 1)
                        for tile in range(NT):
                            r = ROWS[tile]
                            wait(dve, S["top_done"], 3 * b + tile + 1)
                            hold(dve)
                            dve.max_index(topi[0:r, tile, :], top[0:r, tile, :], ps_j[0][0:r, tile * E:(tile + 1) * E])\
                                .then_inc(S["topi_done"], 1)
                        wait(dve, S["topi_done"], 3 * b + 3)
                        dve.tensor_copy(topf[:, :, :], topi[:, :, 0:TOPK]).then_inc(S["topf_done"], 1)
                        wait(dve, S["topf_done"], b + 1)
                        full = [128, NT, TOPK, E]
                        dve.tensor_tensor(msk[:, :, :, :], iota8[:, :].unsqueeze(1).unsqueeze(1).broadcast_to(full),
                                          topf[:, :, :].unsqueeze(3).broadcast_to(full), ALU.is_equal)\
                            .then_inc(S["msk_done"], 1)
                        wait(dve, S["msk_done"], b + 1)
                        dve.tensor_tensor(both[:, :, :], msk[:, :, 0, :], msk[:, :, 1, :], ALU.add)\
                            .then_inc(S["both_done"], 1)
                        dve.tensor_tensor(ex[:, :, :], top[:, :, :], top[:, :, 0:1].broadcast_to([128, NT, E]),
                                          ALU.subtract).then_inc(S["ex_sub"], 1)
                    if s in QK_SLOTS and has(i + 2):
                        j = QK_SLOTS.index(s)
                        wait(dve, S["qk_hi"], 4 * (i + 2) + j + 1)
                        dve.tensor_tensor(qp[:, j // 2, 1, j % 2, :], ps_j[j % 2][0:KD, 0:NP],
                                          qp[:, j // 2, 0, j % 2, :].bitcast(F32), ALU.subtract)\
                            .then_inc(S["qk_split"], 1)
                    if s == 24 and has(i - 1):
                        b = i - 1
                        wait(dve, S["prefix_done"], b + 1)
                        for tile in range(NT):
                            wait(dve, S["base_step"], 4 * b + tile)
                            dve.tensor_tensor(base[:, tile + 1, :], ps_j[1][:, (NT + tile) * E:(NT + tile + 1) * E],
                                              base[:, tile, :], ALU.add).then_inc(S["base_step"], 1)
                        wait(dve, S["base_step"], 4 * b + NT)
                        dve.tensor_tensor(place[:, :, :], ps_j[1][:, 0:NT * E].rearrange("p (t e) -> p t e", t=NT),
                                          base[:, 0:NT, :], ALU.add).then_inc(S["place_done"], 1)
                        wait(dve, S["place_done"], b + 1)
                        dve.tensor_copy(base[:, 0, :], base[:, NT, :]).then_inc(S["base_step"], 1)
                        dve.tensor_tensor(pick[:, :, :, :], msk[:, :, :, :],
                                          place[:, :, :].unsqueeze(2).broadcast_to([128, NT, TOPK, E]), ALU.mult)\
                            .then_inc(S["pick_done"], 1)
                        wait(dve, S["pick_done"], b + 1)
                        dve.tensor_reduce(slotf[:, :, :], pick[:, :, :, :], AX.X, ALU.add).then_inc(S["slotf_done"], 1)
                        wait(dve, S["slotf_done"], b + 1)
                        wait(dve, S["sent"], 96 * b)
                        dve.tensor_copy(slot[:, :, :], slotf[:, :, :]).then_inc(S["slot_done"], 1)
                    if s == 18 and has(i + 1):
                        b = i + 1
                        wait(dve, S["mx_read"], 54 * b + 54)
                        wait(dve, S["mt_done"], b)
                        dve.tensor_reduce(negm[:, :, :].rearrange("p t h -> p (t h)"), mxp[:, :, :], AX.X, ALU.max,
                                          negate=True).then_inc(S["mx_comb"], 1)
                        wait(dve, S["mx_comb"], b + 1)
                        dve.tensor_copy(negm2[:, :, 0, :].bitcast(F32R), negm[:, :, :]).then_inc(S["m_split"], 1)
                        wait(dve, S["m_split"], 2 * b + 1)
                        dve.tensor_tensor(negm2[:, :, 1, :].bitcast(F32R), negm[:, :, :], negm2[:, :, 0, :],
                                          ALU.subtract).then_inc(S["m_split"], 1)
                    if s == 28 and has(i - 1):
                        b = i - 1
                        wait(dve, S["ex_done"], b + 1)
                        dve.tensor_reduce(zsum[:, :], ex[:, :, :], AX.X, ALU.add).then_inc(S["z_done"], 1)
                        wait(dve, S["z_done"], b + 1)
                        dve.scalar_tensor_tensor(out=den[:, :], in0=zsum[:, :], scalar=1e-9, in1=ex[:, :, 1],
                                                 op0=ALU.mult, op1=ALU.add).then_inc(S["den_a"], 1)
                        wait(dve, S["den_a"], b + 1)
                        dve.tensor_tensor(den[:, :], den[:, :], ex[:, :, 0], ALU.add).then_inc(S["den_done"], 1)
                        wait(dve, S["den_done"], b + 1)
                        dve.reciprocal(den[:, :], den[:, :]).then_inc(S["rden_done"], 1)
                        wait(dve, S["rden_done"], b + 1)
                        dve.tensor_tensor(gw[:, b, :, :], ex[:, :, 0:TOPK],
                                          den[:, :].unsqueeze(2).broadcast_to([128, NT, TOPK]), ALU.mult)\
                            .then_inc(S["gw_done"], 1)
                    if s == 25 and has(i):
                        norm_outputs(i, 1)
                    if unit:
                        maxima(unit[0], unit[1], (1, 2))

            def list_blocks():
                done = S["listing"]
                dve.wait_ge(S["route_made"], 4)
                dve.wait_ge(S["base_step"], 4 * B)
                dve.tensor_copy(nexti[:, :], base[0:1, 0, :]).then_inc(S["rows_known"], 1)
                dve.tensor_tensor(count[:, :], base[0:1, 0, :], start[:, :], ALU.subtract).then_inc(done, 1)
                dve.wait_ge(done, 1)
                dve.tensor_scalar(counti[:, :], count[:, :], float(BLK - 1), None, ALU.add).then_inc(done, 1)
                dve.wait_ge(done, 2)
                dve.tensor_scalar(counti[:, :], counti[:, :], BLK.bit_length() - 1, None, ALU.arith_shift_right)\
                    .then_inc(done, 1)
                dve.wait_ge(done, 3)
                dve.tensor_copy(nblk[:, :], counti[:, :]).then_inc(done, 1)
                dve.wait_ge(done, 4)
                dve.tensor_scalar(skip[:, :], nblk[:, :], -float(BLK), float(REG), ALU.mult, ALU.add).then_inc(done, 1)
                dve.tensor_copy(upto[:, 0:1], nblk[:, 0:1]).then_inc(done, 1)
                for e in range(1, E):
                    dve.wait_ge(done, 5 + e)
                    dve.tensor_tensor(upto[:, e:e + 1], nblk[:, e:e + 1], upto[:, e - 1:e], ALU.add).then_inc(done, 1)
                dve.wait_ge(done, 5 + E)
                full = [1, NBLK, E]
                dve.tensor_tensor(past[:, :, :], iblk[:, :].unsqueeze(2).broadcast_to(full),
                                  upto[:, :].unsqueeze(1).broadcast_to(full), ALU.is_ge).then_inc(done, 1)
                dve.wait_ge(done, 6 + E)
                dve.tensor_tensor(part[:, :, :], past[:, :, :], skip[:, :].unsqueeze(1).broadcast_to(full), ALU.mult)\
                    .then_inc(done, 1)
                dve.tensor_reduce(tabf[:, 0, :], past[:, :, :], AX.X, ALU.add).then_inc(done, 1)
                dve.wait_ge(done, 7 + E)
                dve.tensor_reduce(tabf[:, 1, :], part[:, :, :], AX.X, ALU.add).then_inc(done, 1)
                dve.wait_ge(done, 9 + E)
                dve.tensor_scalar(tabf[:, 0, :], tabf[:, 0, :], float(E - 1), None, ALU.min).then_inc(done, 1)
                dve.scalar_tensor_tensor(out=tabf[:, 1, :], in0=iblk[:, :], scalar=float(BLK), in1=tabf[:, 1, :],
                                         op0=ALU.mult, op1=ALU.add).then_inc(done, 1)
                dve.wait_ge(done, 11 + E)
                dve.tensor_scalar(tabf[:, 1, :], tabf[:, 1, :], float(E * REG), None, ALU.min).then_inc(done, 1)
                dve.wait_ge(done, 12 + E)
                dve.tensor_copy(table[:, :, :], tabf[:, :, :]).then_inc(S["listed"], 1)
                dve.wait_ge(S["listed"], 1)

            dve.memset(mxp[:, :, :], 0.0).then_inc(S["cleared"], 1)
            dve.memset(topi[:, :, :], 99).then_inc(S["cleared"], 1)
            dve.memset(top[:, :, :], 0.0).then_inc(S["cleared"], 1)
            dve.memset(mv1[:, :, :], 1.0).then_inc(S["cleared"], 1)
            dve.memset(mv2[:, :, :], 1.0).then_inc(S["cleared"], 1)
            dve.memset(mr[:, N:NP].bitcast(F32), 0.0).then_inc(S["cleared"], 1)
            dve.memset(ones[:, :], 1.0).then_inc(S["cleared"], 1)
            dve.memset(o2t[KD:KD + 1, :, :], 1.0).then_inc(S["cleared"], 1)
            dve.wait_ge(S["cleared"], 8)
            run_steps(dve, step)
            list_blocks()
            dve.wait_ge(S["gw_done"], B)


def experts(nc, sb, pb, sem, t):
    ident, xs_d, ys_d, table = t["ident"], t["xs_d"], t["ys_d"], t["table"]
    HC = HID // 128
    RING = 4
    with ExitStack() as st:
        xb = [sb(st, f"xb{p}", [128, 2, ROW]) for p in range(RING)]
        w1b = [sb(st, f"w1b{p}", [KD + 1, 2, HID]) for p in range(RING)]
        w2b = [sb(st, f"w2b{p}", [128, HC, D]) for p in range(RING)]
        b2b = [sb(st, f"b2b{p}", [128, D]) for p in range(RING)]
        w1s = [sb(st, f"w1s{p}", [KD + 1, 2, 2, HID], F32R) for p in range(2)]
        xbt = [sb(st, f"xbt{p}", [KD + 1, 2, 2, BLK], F32R) for p in range(RING)]
        ht = [sb(st, f"ht{p}", [128, HC, BLK]) for p in range(RING)]
        yb = [sb(st, f"yb{p}", [128, 2, D]) for p in range(RING)]
        ps_t = pb(st, "ps_t", [128, 512])
        ps_h = [[pb(st, f"ps_h{p}{m}", [128, 512]) for m in range(HC // 2)] for p in range(2)]
        ps_y = pb(st, "ps_y", [128, 512])
        x_in = [sem(st, f"x_in{p}") for p in range(RING)]
        w1_in = [sem(st, f"w1_in{p}") for p in range(RING)]
        w2_in = [sem(st, f"w2_in{p}") for p in range(RING)]
        y_sent = [sem(st, f"y_sent{p}") for p in range(RING)]
        xt_done, xt_hi, xt_lo, w_hi, w_lo, h_done, h_act, y_done, y_sum, set_up = (
            sem(st, f"ex_{n}") for n in ("xt_done", "xt_hi", "xt_lo", "w_hi", "w_lo", "h_done", "h_act", "y_done",
                                         "y_sum", "set_up"))
        block = st.enter_context(nc.Block())

        def after(blk, d=1):
            i, p, uses = blk
            return i + d, (p + d) % RING, uses + (p + d) // RING

        def run_blocks(eng, one):
            for i in range(RING):
                one((i, i, 0))
            turns = NBLK // RING
            with eng.Fori(1, turns - 1) as n:
                for p in range(RING):
                    one((n * RING + p, p, n))
            for i in range(RING * (turns - 1), NBLK):
                one((i, i % RING, i // RING))

        @block.sync
        def _(sp):
            def load(blk):
                i, p, uses = blk
                for done, value in ((xt_done, i - RING + 1), (y_done, i - RING + 1), (y_sum, i - RING + 1),
                                    (y_sent[p], 32 * uses)):
                    wait(sp, done, value)
                    hold(sp)
                e = sp.value_load(table[0:1, 0, bass.ds(i, 1)], min_val=0, max_val=E - 1)
                row = sp.value_load(table[0:1, 1, bass.ds(i, 1)], min_val=0, max_val=E * REG)
                sp.dma_start(xb[p][:, :, :], xs_d[bass.ds(row, BLK), :].rearrange("(a p) n -> p a n", p=128))\
                    .then_inc(x_in[p], 16)
                sp.dma_start(w1b[p][0:KD, :, :], t["w1"][bass.ds(e, 1)].rearrange("a (c p) n -> p (a c) n", c=2))\
                    .then_inc(w1_in[p], 16)
                sp.dma_start(w1b[p][KD:KD + 1, 1, :], t["b1"][bass.ds(e, 1), :]).then_inc(w1_in[p], 16)
                sp.dma_start(w2b[p][:, :, :], t["w2"][bass.ds(e, 1)].rearrange("a (c p) n -> p (a c) n", c=HC))\
                    .then_inc(w2_in[p], 16)
                sp.dma_start(b2b[p][:, :], t["b2"][bass.ds(e, 1), :].broadcast_to([128, D])).then_inc(w2_in[p], 16)

            run_blocks(sp, load)

        @block.tensor
        def _(pe):
            def turn(blk):
                i, p, uses = blk
                wait(pe, x_in[p], 16 * (uses + 1))
                wait(pe, xt_lo, i)
                for c in range(2):
                    for a in range(2):
                        last = pe.transpose(ps_t[0:KD, c * BLK + a * 128:c * BLK + a * 128 + 128],
                                            xb[p][:, a, c * KD:(c + 1) * KD], ident[:, :])
                last.then_inc(xt_done, 1)

            def up(blk):
                i, p, uses = blk
                wait(pe, xt_lo, i + 1)
                wait(pe, w_lo, 2 * (i + 1))
                terms = [(c, l, x) for c in range(2) for l, x in ((0, 0), (1, 0), (0, 1))]
                for m in range(HC):
                    bank = ps_h[p % 2][m // 2]
                    if m % 2 == 0:
                        wait(pe, h_act, 3 * (i - 2) + m // 2 + 1)
                    for c, l, x in terms:
                        k = KD + c * (1 - x)
                        last = pe.matmul(bank[:, (m % 2) * BLK:(m % 2 + 1) * BLK],
                                         w1s[p % 2][0:k, l, c, m * 128:(m + 1) * 128], xbt[p][0:k, x, c, :],
                                         start=(c, l, x) == terms[0], stop=(c, l, x) == terms[-1])
                    if m % 2:
                        last.then_inc(h_done, 1)

            def down(blk):
                i, p, uses = blk
                wait(pe, w2_in[p], 32 * (uses + 1))
                wait(pe, h_act, 3 * i + 3)
                wait(pe, y_sum, i)
                for a in range(2):
                    for m in range(HC):
                        last = pe.matmul(ps_y[:, a * D:(a + 1) * D], ht[p][:, m, a * 128:(a + 1) * 128],
                                         w2b[p][:, m, :], start=m == 0, stop=m == HC - 1)
                last.then_inc(y_done, 1)

            def one(blk):
                if isinstance(blk[0], int) and blk[0] == 0:
                    turn(blk)
                    up(blk)
                    turn(after(blk))
                    return
                up(blk)
                if not isinstance(blk[0], int) or blk[0] + 1 < NBLK:
                    turn(after(blk))
                down(after(blk, -1))

            run_blocks(pe, one)
            down((NBLK - 1, (NBLK - 1) % RING, (NBLK - 1) // RING))

        @block.scalar
        def _(act):
            def split(blk):
                i, p, uses = blk
                wait(act, w1_in[p], 32 * (uses + 1))
                wait(act, h_done, 3 * (i - 1))
                for c in range(2):
                    act.activation(w1s[p % 2][0:KD + c, 0, c, :], w1b[p][0:KD + c, c, :], ACT.Copy).then_inc(w_hi, 1)

            def one(blk):
                i, p, uses = blk
                if isinstance(i, int) and i == 0:
                    split(blk)
                if not isinstance(i, int) or i + 1 < NBLK:
                    split(after(blk))
                wait(act, y_done, i - RING + 1)
                for m in range(HC // 2):
                    wait(act, h_done, 3 * i + m + 1)
                    act.activation(ht[p][:, 2 * m:2 * m + 2, :], ps_h[p % 2][m][:, :].rearrange("p (m n) -> p m n", m=2),
                                   ACT.Gelu).then_inc(h_act, 1)

            run_blocks(act, one)

        @block.vector
        def _(dve):
            def split(blk):
                i, p, uses = blk
                for c in range(2):
                    wait(dve, w_hi, 2 * i + c + 1)
                    dve.tensor_tensor(w1s[p % 2][0:KD + c, 1, c, :], w1b[p][0:KD + c, c, :],
                                      w1s[p % 2][0:KD + c, 0, c, :].bitcast(F32), ALU.subtract).then_inc(w_lo, 1)

            def copy(blk):
                i, p, uses = blk
                turned = ps_t[0:KD, :].rearrange("p (c n) -> p c n", c=2)
                wait(dve, xt_done, i + 1)
                wait(dve, h_done, 3 * (i - RING + 1))
                dve.tensor_copy(xbt[p][0:KD, 0, :, :], turned).then_inc(xt_hi, 1)
                wait(dve, xt_hi, i + 1)
                dve.tensor_tensor(xbt[p][0:KD, 1, :, :], turned, xbt[p][0:KD, 0, :, :].bitcast(F32), ALU.subtract)\
                    .then_inc(xt_lo, 1)

            def finish(blk):
                i, p, uses = blk
                wait(dve, y_done, i + 1)
                wait(dve, w2_in[p], 32 * (uses + 1))
                wait(dve, y_sent[p], 32 * uses)
                dve.tensor_tensor(yb[p][:, :, :], ps_y[:, 0:2 * D].rearrange("p (a d) -> p a d", a=2),
                                  b2b[p][:, :].unsqueeze(1).broadcast_to([128, 2, D]), ALU.add).then_inc(y_sum, 1)

            def one(blk):
                if isinstance(blk[0], int) and blk[0] == 0:
                    copy(blk)
                    split(blk)
                    split(after(blk))
                    copy(after(blk))
                    return
                if not isinstance(blk[0], int) or blk[0] + 1 < NBLK:
                    split(after(blk))
                    copy(after(blk))
                finish(after(blk, -1))

            for p in range(RING):
                dve.memset(xbt[p][KD:KD + 1, 0, :, :].bitcast(F32), 1.0).then_inc(set_up, 1)
            run_blocks(dve, one)
            finish((NBLK - 1, (NBLK - 1) % RING, (NBLK - 1) // RING))

        @block.gpsimd
        def _(pool):
            def one(blk):
                i, p, uses = blk
                wait(pool, y_sum, i + 1)
                hold(pool)
                for a in range(2):
                    pool.indirect_dma_start(
                        ys_d, bass.IndirectOffsetOnAxis(ap=xb[p][:, a, D:ROW].bitcast(I32), axis=0), yb[p][:, a, :], None,
                        bounds_check=TOPK * T - 1, oob_is_err=False).then_inc(y_sent[p], 16)

            run_blocks(pool, one)
            for p in range(RING):
                pool.wait_ge(y_sent[p], 32 * NBLK // RING)


def combine(nc, sb, pb, sem, t):
    hs, gw, ys_d, out = t["hs"], t["gw"], t["ys_d"], t["out"]
    IG = 4
    with ExitStack() as st:
        yl = [sb(st, f"yl{g}", [128, NT, IG, TOPK, D]) for g in range(B // IG)]
        y_in = [[sem(st, f"yl_in{g}_{tile}") for tile in range(NT)] for g in range(B // IG)]
        half, summed, stored = (sem(st, f"co_{n}") for n in ("half", "summed", "stored"))
        block = st.enter_context(nc.Block())

        @block.sync
        def _(sp):
            rows = ys_d.rearrange("(k b n) d -> n b k d", k=TOPK, b=B)
            for g in range(B // IG):
                for tile in range(NT):
                    r = ROWS[tile]
                    for k in range(TOPK):
                        sp.dma_start(yl[g][0:r, tile, :, k, :], rows[FIRST[tile]:FIRST[tile] + r, g * IG:(g + 1) * IG, k, :])\
                            .then_inc(y_in[g][tile], 16)

        @block.vector
        def _(dve):
            for g in range(B // IG):
                for tile in range(NT):
                    r = ROWS[tile]
                    dve.wait_ge(y_in[g][tile], 32)
                    for k in range(TOPK):
                        for j in range(IG):
                            b = g * IG + j
                            if k:
                                dve.wait_ge(half, (g * NT + tile) * IG + j + 1)
                            dve.scalar_tensor_tensor(out=hs[0:r, b, tile, :], in0=yl[g][0:r, tile, j, k, :],
                                                     scalar=gw[0:r, b, tile, k:k + 1], in1=hs[0:r, b, tile, :],
                                                     op0=ALU.mult, op1=ALU.add).then_inc(summed if k else half, 1)

        @block.scalar
        def _(act):
            for g in range(B // IG):
                to = out[g * IG:(g + 1) * IG].rearrange("b n d -> n b d")
                of = hs[:, g * IG:(g + 1) * IG, :, :]
                act.wait_ge(summed, (g * NT + 1) * IG)
                act.dma_start(to[1:1 + ROWS[0]], of[0:ROWS[0], :, 0, :]).then_inc(stored, 16)
                act.wait_ge(summed, (g * NT + 2) * IG)
                act.dma_start(to[1 + ROWS[0]:1 + NPATCH], of[0:ROWS[0], :, 1, :]).then_inc(stored, 16)
                act.dma_start(to[0:1], of[ROWS[0]:ROWS[1], :, 1, :]).then_inc(stored, 16)
                act.wait_ge(summed, (g * NT + 3) * IG)
                act.dma_start(to[NPATCH + 1:N], of[0:TXT, :, 2, :]).then_inc(stored, 16)
            act.wait_ge(stored, 16 * 4 * B // IG)


_INS = ['x', 'txt', 'L0_tok_W', 'L0_tok_b', 'L0_tok_class_token', 'L0_tok_pos_emb', 'L0_attn_sc_token', 'L0_attn_W_qkv',
        'L0_attn_W_proj', 'L0_attn_b_proj', 'L0_ffn_gate_w', 'L0_ffn_w1', 'L0_ffn_b1', 'L0_ffn_w2', 'L0_ffn_b2']


def kernel(**inputs):
    import numpy as _np
    import concourse.bacc as _bacc
    from concourse import mybir as _mybir
    from concourse.bass_utils import run_bass_kernel_spmd as _run

    nc = _bacc.Bacc("TRN2", target_bir_lowering=False, num_devices=1)
    arrays, args = {}, []
    for name in _INS:
        a = _np.ascontiguousarray(inputs[name])
        arrays[f"in_{name}_dram"] = a
        args.append(nc.dram_tensor(f"in_{name}_dram", a.shape, _mybir.dt.from_np(a.dtype), kind="ExternalInput").ap())
    res = nc.dram_tensor("out_0_dram", (B, N, D), _mybir.dt.float32, kind="ExternalOutput").ap()
    build(nc, *args, res)
    r = _run(nc, [arrays], core_ids=[0])
    return r.results[0]["out_0_dram"]
```

```python
import concourse.bass as bass
from concourse import mybir
from contextlib import ExitStack
import numpy as np

F32 = mybir.dt.float32
F32R = mybir.dt.float32r
I32 = mybir.dt.int32
U32 = mybir.dt.uint32
ALU = mybir.AluOpType
ACT = mybir.ActivationFunctionType
AX = mybir.AxisListType

B, CH, IMG, P = 16, 3, 224, 16
G = IMG // P
D, H, DH = 192, 12, 16
TXT = 128
SC = 196
NPATCH = G * G
N = NPATCH + 1 + TXT
NP = N + 1
ROWS = [NPATCH // 2, NPATCH // 2 + 1, TXT]
FIRST = [0, ROWS[0], ROWS[0] + ROWS[1]]
NT = 3
SCR = SC // 2
KD = D // 2
HG = 4
NG = H // HG
KC5 = NT + 2
PX = 8
E, HID, TOPK = 8, 768, 2
T = B * N
BLK = 256
NBLK = (T * TOPK + E * (BLK - 1)) // BLK
REG = T + BLK
XROWS = E * REG + BLK
ROW = D + 1
SCALE = float(DH) ** -0.5
LN_EPS = 1e-5
SKIP = 1 << 20
KMAX, KEXP = 126, 128
TURN_BACK, XT, QK = (6, 7), (8, 9), (10, 11, 12, 14)
PROJECT, TURN_MAX, X2T, LOGITS, PREFIX, VALUES = (16, 17), 19, (20, 21), 22, 24, (26, 28)
TURN_OUT = (15, 25, 5)
LN1, NORM1, LN2, NORM2, MAX_DONE, WEIGHTS = 4, 7, 17, 19, 18, 28
UNITS = [22, 24, 26, 27, 28, 30, 31, 32, 33, 35, 38, 39, 40, 41, 43, 44, 45, 46]


def has(b):
    return not isinstance(b, int) or 0 <= b < B


def wait(eng, sem, value):
    if isinstance(value, int) and value <= 0:
        return
    eng.wait_ge(sem, value)


def hold(eng):
    eng.nop(nofuse=True)


def unit_at(i, s):
    for b, slot in ((i + 1, s + 30), (i + 2, s)):
        if slot in UNITS and has(b):
            return b, UNITS.index(slot)
    return None


def wait_nearest(eng, candidates):
    for b, sem, value in candidates:
        if has(b):
            wait(eng, sem, value)
            return


def run_steps(eng, step):
    for i in (-2, -1, 0):
        step(i, i % 2)
    with eng.Fori(1, B - 4, 2) as i:
        step(i, 1)
        step(i + 1, 0)
    for i in range(B - 3, B + 1):
        step(i, i % 2)


def build(nc, x, txt, tok_w, tok_b, cls, pos, sc_tok, w_qkv, w_proj, b_proj, gate_w, w1, b1, w2, b2, out):
    eq_d = nc.dram_tensor("eq_d", [2, 2, 2, H, DH, NP], F32, kind="Internal").ap()
    em_d = nc.dram_tensor("em_d", [2, 2, H, NP], F32, kind="Internal").ap()
    ec_d = nc.dram_tensor("ec_d", [2, H, DH, SC], F32, kind="Internal").ap()
    xs_d = nc.dram_tensor("xs_d", [XROWS, ROW], F32, kind="Internal").ap()
    b1t_d = nc.dram_tensor("b1t_d", [E, 128, HID // 128], F32, kind="Internal").ap()
    ys_d = nc.dram_tensor("ys_d", [TOPK * T, D], F32, kind="Internal").ap()

    keep = ExitStack()
    sb = lambda st, name, shape, dt=F32: st.enter_context(nc.sbuf_tensor(name, shape, dt))
    pb = lambda st, name, shape: st.enter_context(nc.psum_tensor(name, shape, F32))
    sem = lambda st, name: st.enter_context(nc.semaphore(name))

    with keep:
        hs = sb(keep, "hs", [128, B, NT, D])
        gw = sb(keep, "gw", [128, B, NT, TOPK])
        ident = sb(keep, "ident", [128, 128])
        base = sb(keep, "base", [128, NT + 1, E])

        b1_out = sem(keep, "b1_out")
        table = sb(keep, "table", [1, 2, NBLK], I32)

        attend = ExitStack()
        with attend:
            wp = sb(attend, "wp", [KD, PX, D])
            posb = sb(attend, "posb", [ROWS[1], 2, D])
            wqkv = sb(attend, "wqkv", [KD, 2, 3 * D])
            wqs = sb(attend, "wqs", [KD, 2, 2, 2 * D], F32R)
            wpj = sb(attend, "wpj", [KD + 1, 2, D])
            gt = sb(attend, "gt", [KD, 2, E])
            ut = sb(attend, "ut", [128, 128])
            ones = sb(attend, "ones", [128, 128])
            iota8 = sb(attend, "iota8", [128, E])
            halfneg = sb(attend, "halfneg", [128, NT])
            ids = sb(attend, "ids", [128, NT, TOPK])
            qs = [sb(attend, f"qs{p}", [KEXP, H, NP], F32R) for p in range(2)]
            ko = [sb(attend, f"ko{p}", [KEXP, H, NP], F32R) for p in range(2)]
            kc = sb(attend, "kc", [KEXP, H, SC], F32R)
            va = [sb(attend, f"va{p}", [128, NT, H, 32]) for p in range(2)]
            vc = sb(attend, "vc", [SCR, 2, H, 32])
            xt = [sb(attend, f"xt{p}", [KD, 2, NP]) for p in range(2)]
            img = sb(attend, "img", [KD, G, IMG])

            kc_in = sem(attend, "kc_in")
            setup(nc, sb, pb, sem, locals())
            attention(nc, sb, pb, sem, locals())
        experts(nc, sb, pb, sem, locals())
        combine(nc, sb, pb, sem, locals())


def load_image(sp, x, img, b, done):
    for h in range(2):
        for c in range(CH):
            src = x[b, c].rearrange("(g y) w -> y g w", y=P)
            r = h * CH * P + c * P
            sp.dma_start(img[r:r + P, :, 0:IMG - PX * h], src[:, :, PX * h:IMG]).then_inc(done, 16)


def setup(nc, sb, pb, sem, t):
    hs, ident, base = t["hs"], t["ident"], t["base"]
    wp, posb, wqkv, wpj, gt, ut, ones = (t[k] for k in "wp posb wqkv wpj gt ut ones".split())
    iota8, halfneg, ids, qs, ko, kc, va, vc, xt = (t[k] for k in "iota8 halfneg ids qs ko kc va vc xt".split())
    ec_d, kc_in, wqs = t["ec_d"], t["kc_in"], t["wqs"]
    with ExitStack() as st:
        wraw = sb(st, "wraw", [KD, 2, CH * P * P])
        wperm = sb(st, "wperm", [KD, 2, PX, 2, KD // 2])
        graw = sb(st, "graw", [E, D])
        sraw = sb(st, "sraw", [SCR, 2, D])
        bias = sb(st, "bias", [ROWS[1], 2, D])
        sct = sb(st, "sct", [KD, 2, SC])
        kcs = sb(st, "kcs", [KD, 2, 2, SC], F32R)
        ps = [pb(st, f"su{i}", [128, 512]) for i in range(4)]
        w_in, s_in, q_in, img0_in, p_in, b_in, h_in = (sem(st, f"su_{n}") for n in
                                                    ("w_in", "s_in", "q_in", "img0_in", "p_in", "b_in", "h_in"))
        zeroed, made, turned, copied = (sem(st, f"su_{n}") for n in ("zeroed", "made", "turned", "copied"))
        wq_hi, wq_lo, summed, hi_done, ec_out, cls_in, w_perm, v_made, k_made, q_zeroed = (
            sem(st, f"su_{n}") for n in ("wq_hi", "wq_lo", "summed", "hi_done", "ec_out", "cls_in", "w_perm", "v_made", "k_made", "q_zeroed"))
        block = st.enter_context(nc.Block())
        JOBS = PX + 1 + 2 + 2 + 2

        @block.sync
        def _(sp):
            sp.dma_start(wraw[:, :, :], t["tok_w"].rearrange("(h e) d -> e h d", h=2)).then_inc(w_in, 16)
            sp.dma_start(graw[:, :], t["gate_w"]).then_inc(s_in, 16)
            sp.dma_start(sraw[:, :, :], t["sc_tok"][0].rearrange("(a p) d -> p a d", a=2)).then_inc(s_in, 16)
            sp.dma_start(wqkv[:, :, :], t["w_qkv"].rearrange("(c p) n -> p c n", c=2)).then_inc(q_in, 16)
            pos = t["pos"]
            sp.dma_start(posb[0:ROWS[0], :, :],
                         pos[1:1 + NPATCH, :].rearrange("(a p) d -> p a d", a=2)).then_inc(p_in, 16)
            sp.dma_start(posb[ROWS[0]:ROWS[1], 1:2, :], pos[0:1, :].unsqueeze(1)).then_inc(p_in, 16)
            tb = t["tok_b"].unsqueeze(0)
            sp.dma_start(bias[0:ROWS[0], 0, :], tb.broadcast_to([ROWS[0], D])).then_inc(p_in, 16)
            sp.dma_start(bias[0:ROWS[0], 1, :], tb.broadcast_to([ROWS[0], D])).then_inc(p_in, 16)
            sp.dma_start(bias[ROWS[0]:ROWS[1], 1, :], t["cls"].unsqueeze(0)).then_inc(p_in, 16)
            load_image(sp, t["x"], t["img"], 0, img0_in)
            sp.dma_start(hs[:, :, 2, :], t["txt"].rearrange("b t d -> t b d")).then_inc(h_in, 16)
            sp.dma_start(wpj[0:KD, :, :], t["w_proj"].rearrange("(c p) n -> p c n", c=2)).then_inc(b_in, 16)
            sp.dma_start(wpj[KD:KD + 1, 1, :], t["b_proj"].unsqueeze(0)).then_inc(b_in, 16)
            sp.wait_ge(summed, 2)
            sp.dma_start(hs[ROWS[0]:ROWS[1], :, 1, :],
                         posb[ROWS[0]:ROWS[1], 1:2, :].broadcast_to([1, B, D])).then_inc(cls_in, 16)
            sp.wait_ge(summed, 4)
            for hl in range(2):
                sp.dma_start(ec_d[hl].rearrange("(c h) d n -> (h d) c n", c=2),
                             kcs[:, hl, :, :].bitcast(F32)).then_inc(ec_out, 16)
            sp.wait_ge(ec_out, 32)
            sp.wait_ge(k_made, 1)
            for s, hl in enumerate((0, 1, 0)):
                sp.dma_start(kc[DH * s:DH * s + DH, :, :].bitcast(F32),
                             ec_d[hl].rearrange("h d n -> d h n")).then_inc(kc_in, 16)
            sp.wait_ge(img0_in, 96)
            sp.wait_ge(cls_in, 16)
            sp.wait_ge(b_in, 32)
            sp.wait_ge(h_in, 16)

        @block.gpsimd
        def _(pool):
            pool.memset(ident[:, :], 0.0).then_inc(zeroed, 1)
            pool.memset(ut[:, :], 0.0).then_inc(zeroed, 1)
            pool.wait_ge(zeroed, 2)
            pool.affine_select(out=ident[:, :], in_=ident[:, :], compare_op=ALU.not_equal, fill=1.0, base=0,
                               pattern=[[-1, 128]], channel_multiplier=1).then_inc(made, 1)
            pool.affine_select(out=ut[:, :], in_=ut[:, :], compare_op=ALU.is_ge, fill=1.0, base=0,
                               pattern=[[-1, 128]], channel_multiplier=1).then_inc(made, 1)
            pool.iota(iota8[:, :], pattern=[[1, E]], base=0, channel_multiplier=0,
                      allow_small_or_imprecise_dtypes=True).then_inc(made, 1)
            pool.iota(base[:, 0, :], pattern=[[REG, E]], base=0, channel_multiplier=0,
                      allow_small_or_imprecise_dtypes=True).then_inc(made, 1)
            for tile in range(NT):
                pool.iota(ids[:, tile, :], pattern=[[T, TOPK]], base=FIRST[tile], channel_multiplier=1,
                          allow_small_or_imprecise_dtypes=True).then_inc(made, 1)
            pool.memset(halfneg[:, :], -0.5).then_inc(made, 1)
            for n, v in enumerate((vc, va[0], va[1])):
                pool.memset(v[:, :, :, :], 0.0).then_inc(zeroed, 1)
                pool.wait_ge(zeroed, 3 + n)
                pool.memset(v[:, :, :, DH:DH + 1], 1.0).then_inc(v_made, 1)
            for k in (kc, ko[0], ko[1]):
                pool.memset(k[:, :, :].bitcast(F32), 1.0).then_inc(k_made, 1)
            pool.wait_ge(made, 8)
            pool.wait_ge(v_made, 3)
            pool.wait_ge(k_made, 3)

        @block.tensor
        def _(pe):
            pe.wait_ge(made, 1)
            pe.wait_ge(w_perm, 2)
            job = 0
            for i in range(PX):
                if job >= 4:
                    pe.wait_ge(copied, job - 3)
                for eh in range(2):
                    last = pe.transpose(ps[job % 4][0:KD, eh * KD:(eh + 1) * KD],
                                        wperm[:, eh, i, :, :].rearrange("e j c -> e (j c)"), ident[0:KD, 0:KD])
                last.then_inc(turned, 1)
                job += 1
            pe.wait_ge(s_in, 32)
            pe.wait_ge(copied, job - 3)
            for c in range(2):
                last = pe.transpose(ps[job % 4][0:KD, c * E:(c + 1) * E], graw[:, c * KD:(c + 1) * KD], ident[0:E, 0:E])
            last.then_inc(turned, 1)
            job += 1
            for c in range(2):
                pe.wait_ge(copied, job - 3)
                for a in range(2):
                    last = pe.transpose(ps[job % 4][0:KD, a * SCR:(a + 1) * SCR], sraw[:, a, c * KD:(c + 1) * KD],
                                        ident[0:SCR, 0:SCR])
                last.then_inc(turned, 1)
                job += 1
            pe.wait_ge(q_in, 16)
            pe.wait_ge(copied, job)
            for c in range(2):
                for kd in range(2):
                    last = pe.matmul(ps[job % 4][0:KD, 0:SC], wqkv[:, kd, D + c * KD:D + (c + 1) * KD], sct[:, kd, :],
                                     start=kd == 0, stop=kd == 1)
                last.then_inc(turned, 1)
                job += 1
            for a in range(2):
                for kd in range(2):
                    last = pe.matmul(ps[job % 4][0:SCR, 0:D], sct[:, kd, a * SCR:(a + 1) * SCR], wqkv[:, kd, 2 * D:3 * D],
                                     start=kd == 0, stop=kd == 1)
                last.then_inc(turned, 1)
                job += 1
            assert job == JOBS

        @block.scalar
        def _(act):
            job = 0
            for i in range(PX):
                act.wait_ge(turned, job + 1)
                act.activation(wp[:, i, :], ps[job % 4][0:KD, 0:D], ACT.Copy).then_inc(copied, 1)
                job += 1
            act.wait_ge(turned, job + 1)
            act.activation(gt[:, :, :], ps[job % 4][0:KD, 0:2 * E].rearrange("p (c e) -> p c e", c=2),
                           ACT.Copy).then_inc(copied, 1)
            job += 1
            for c in range(2):
                act.wait_ge(turned, job + 1)
                act.activation(sct[:, c, :], ps[job % 4][0:KD, 0:SC], ACT.Copy).then_inc(copied, 1)
                job += 1
            for c in range(2):
                act.wait_ge(turned, job + 1)
                act.activation(kcs[:, 0, c, :], ps[job % 4][0:KD, 0:SC], ACT.Copy).then_inc(hi_done, 1)
                job += 1
            act.wait_ge(v_made, 1)
            for a in range(2):
                act.wait_ge(turned, job + 1)
                act.activation(vc[:, a, :, 0:DH], ps[job % 4][0:SCR, 0:D].rearrange("p (h d) -> p h d", h=H),
                               ACT.Copy).then_inc(copied, 1)
                job += 1
            act.activation(wqs[:, 0, :, :], wqkv[:, :, 0:2 * D], ACT.Copy).then_inc(wq_hi, 1)
            act.wait_ge(copied, JOBS - 2)

        @block.vector
        def _(dve):
            for p in range(2):
                dve.memset(xt[p][:, :, N:NP], 0.0)
            dve.wait_ge(w_in, 16)
            for eh in range(2):
                dve.tensor_copy(wperm[:, eh, :, :, :],
                                wraw[:, eh, :].rearrange("e (c j i) -> e i j c", j=2, i=PX)).then_inc(w_perm, 1)
            dve.memset(qs[0][:, :, :].bitcast(F32), 0.0).then_inc(q_zeroed, 1)
            dve.wait_ge(p_in, 16 * 5)
            dve.tensor_tensor(posb[0:ROWS[0], 0, :], posb[0:ROWS[0], 0, :], bias[0:ROWS[0], 0, :],
                              ALU.add).then_inc(summed, 1)
            dve.tensor_tensor(posb[:, 1, :], posb[:, 1, :], bias[:, 1, :], ALU.add).then_inc(summed, 1)
            for c in range(2):
                dve.wait_ge(hi_done, c + 1)
                dve.tensor_tensor(kcs[:, 1, c, :], ps[(PX + 3 + c) % 4][0:KD, 0:SC], kcs[:, 0, c, :].bitcast(F32),
                                  ALU.subtract).then_inc(summed, 1)
            dve.memset(qs[1][:, :, :].bitcast(F32), 0.0).then_inc(q_zeroed, 1)
            dve.wait_ge(wq_hi, 1)
            dve.tensor_tensor(wqs[:, 1, :, :], wqkv[:, :, 0:2 * D], wqs[:, 0, :, :].bitcast(F32), ALU.subtract)\
                .then_inc(wq_lo, 1)
            dve.wait_ge(summed, 4)
            dve.wait_ge(q_zeroed, 2)
            dve.wait_ge(wq_lo, 1)


def attention(nc, sb, pb, sem, t):
    hs, gw, ident, base, table = (t[k] for k in "hs gw ident base table".split())
    wp, posb, wqkv, wpj, gt, ut, ones = (t[k] for k in "wp posb wqkv wpj gt ut ones".split())
    iota8, halfneg, ids, qs, ko, kc, va, vc, xt, img = (t[k] for k in "iota8 halfneg ids qs ko kc va vc xt img".split())
    x, eq_d, em_d, xs_d, kc_in, wqs = (t[k] for k in "x eq_d em_d xs_d kc_in wqs".split())
    with ExitStack() as st:
        xh = sb(st, "xh", [128, NT, D])
        qp = sb(st, "qp", [KD, 2, 2, 2, NP], F32R)
        pt = sb(st, "pt", [128, 3, HG, N])
        ots = sb(st, "ots", [128, N])
        rec = sb(st, "rec", [128, NT, HG])
        on = sb(st, "on", [128, NT, D])
        o2t = sb(st, "o2t", [KD + 1, 2, N])
        xs = sb(st, "xs", [KD, 2, 2, NP], F32R)
        mxp = sb(st, "mxp", [128, NT * H, 2])
        negm = sb(st, "negm", [128, NT, H])
        negm2 = sb(st, "negm2", [128, NT, 2, H])
        mr = sb(st, "mr", [2 * H, NP], F32R)
        xa = sb(st, "xa", [128, NT, TOPK, ROW])
        x2t = sb(st, "x2t", [KD, 2, N])
        st1 = sb(st, "st1", [128, NT, 6])
        mv1 = sb(st, "mv1", [128, NT, 2])
        rs1 = sb(st, "rs1", [128, NT])
        st2 = sb(st, "st2", [128, NT, 6])
        mv2 = sb(st, "mv2", [128, NT, 2])
        rs2 = sb(st, "rs2", [128, NT])
        top = sb(st, "top", [128, NT, E])
        topi = sb(st, "topi", [128, NT, E], U32)
        topf = sb(st, "topf", [128, NT, TOPK])
        msk = sb(st, "msk", [128, NT, TOPK, E])
        both = sb(st, "both", [128, NT, E])
        ex = sb(st, "ex", [128, NT, E])
        zsum = sb(st, "zsum", [128, NT])
        den = sb(st, "den", [128, NT])
        place = sb(st, "place", [128, NT, E])
        pick = sb(st, "pick", [128, NT, TOPK, E])
        slotf = sb(st, "slotf", [128, NT, TOPK])
        slot = sb(st, "slot", [128, NT, TOPK], I32)

        ps_s = [pb(st, f"ps_s{i}", [128, 512]) for i in range(2)]
        ps_m = [pb(st, f"ps_m{i}", [128, 512]) for i in range(3)]
        ps_o = pb(st, "ps_o", [128, 512])
        ps_j = [pb(st, f"ps_j{i}", [128, 512]) for i in range(2)]

        flat = qp[0:1].rearrange("p a b c n -> p (a b c n)").bitcast(F32)
        at = [0]

        def piece(*shape):
            n = int(np.prod(shape))
            at[0] += n
            v = flat[:, at[0] - n:at[0]]
            return v if len(shape) == 1 else v.rearrange("p (a e) -> p a e", a=shape[0])

        zrow = xh[:, :, :].rearrange("p t d -> p (t d)")[:, 0:2 * ROW]\
            .rearrange("p (a n) -> p a n", a=2)
        start = piece(E)
        nexti = piece(E).bitcast(I32)
        count, counti, nblk = piece(E), piece(E).bitcast(I32), piece(E)
        upto = piece(E)
        skip = piece(E)
        iblk = piece(NBLK)
        past, part = piece(NBLK, E), piece(NBLK, E)
        tabf = piece(2, NBLK)

        S = {}
        for n in """img_in patch_done patch_used ln1_stat ln1_mv ln1_eps ln1_rstd xh_done xt_done xt_copied xs_hi xs_lo
                    qk_done qk_hi qk_split eq_out v_done v_copied
                    mx_filled mx_read mx_comb m_split mt_done mt_copied em_out m_in
                    st_filled exp_done pv_done ot_copied ot_turned rec_done on_done on_turned o2_copied
                    proj_done h2_done ln2_stat ln2_mv ln2_eps ln2_rstd xa_done xa_copied ids_next x2t_done x2t_copied
                    logit_done top_done topi_done topf_done msk_done both_done prefix_done base_step place_done
                    pick_done slotf_done slot_done ex_sub ex_done z_done den_a den_done rden_done gw_done
                    sent cleared route_made listing rows_known listed padded""".split():
            S[n] = sem(st, n)
        g_in = [[sem(st, f"{n}_in{g}") for g in range(NG)] for n in "qk"]
        block = st.enter_context(nc.Block())


        @block.sync
        def _(sp):
            def expand(b, par, g):
                hh = slice(HG * g, HG * g + HG)
                for qk, dst, order in ((0, qs[par], (0, 0, 1)), (1, ko[par], (0, 1, 0))):
                    for s, hl in enumerate(order):
                        sp.dma_start(dst[DH * s:DH * s + DH, hh, :].bitcast(F32),
                                     eq_d[par, qk, hl, hh].rearrange("h d n -> d h n")).then_inc(g_in[qk][g], 16)

            def step(i, par):
                if has(i + 3):
                    wait(sp, S["patch_done"], i + 3)
                    hold(sp)
                    load_image(sp, x, img, i + 3, S["img_in"])
                if has(i + 2):
                    wait(sp, S["qk_split"], 4 * (i + 2) + 4)
                    hold(sp)
                    for g in range(NG):
                        for qk in range(2):
                            wait(sp, g_in[qk][g], 48 * (i + 1) if not isinstance(i, int) or i >= 0 else 0)
                            hold(sp)
                    for qk in range(2):
                        for hl in range(2):
                            sp.dma_start(eq_d[par, qk, hl].rearrange("(c h) d n -> (h d) c n", c=2),
                                         qp[:, qk, hl, :, :].bitcast(F32)).then_inc(S["eq_out"], 16)
                if has(i + 2):
                    wait(sp, S["eq_out"], 64 * (i + 3))
                    hold(sp)
                    wait(sp, S["st_filled"], 60 * i + 20)
                    hold(sp)
                    expand(i + 2, par, 0)
                if has(i + 1):
                    wait(sp, S["mt_copied"], i + 2)
                    hold(sp)
                    sp.dma_start(em_d[1 - par].rearrange("l h n -> (l h) n"), mr[:, :].bitcast(F32)).then_inc(S["em_out"], 16)
                if has(i + 2):
                    wait(sp, S["st_filled"], 60 * i + 40)
                    hold(sp)
                    expand(i + 2, par, 1)
                if has(i + 1):
                    wait(sp, S["em_out"], 16 * (i + 2))
                    hold(sp)
                    sp.dma_start(qs[1 - par][KMAX:KEXP, :, :].bitcast(F32), em_d[1 - par]).then_inc(S["m_in"], 16)
                if has(i + 2):
                    wait(sp, S["st_filled"], 60 * i + 60)
                    hold(sp)
                    expand(i + 2, par, 2)

            for e in range(E):
                sp.dma_start(t["b1t_d"][e], t["b1"][e].rearrange("(m p) -> p m", p=128),
                             allow_slow_non_contiguous=True).then_inc(t["b1_out"], 16)
            run_steps(sp, step)
            sp.wait_ge(S["route_made"], 2)
            sp.dma_start(xs_d[E * REG:XROWS, :].rearrange("(a p) n -> p a n", p=128), zrow[:, :, :]).then_inc(S["padded"], 16)
            sp.wait_ge(S["rows_known"], 1)
            for e in range(E):
                row = sp.value_load(nexti[0:1, e:e + 1], min_val=e * REG, max_val=e * REG + T)
                sp.dma_start(xs_d[bass.ds(row, BLK), :].rearrange("(a p) n -> p a n", p=128), zrow[:, :, :])\
                    .then_inc(S["padded"], 16)
            sp.wait_ge(S["padded"], 16 * (E + 1))

        @block.gpsimd
        def _(pool):
            def rstd(b, mv, rs, mv_done, eps_done, rstd_done):
                wait(pool, mv_done, 3 * b + 3)
                hold(pool)
                pool.tensor_scalar(rs[:, :], mv[:, :, 1], LN_EPS, None, ALU.add).then_inc(eps_done, 1)
                wait(pool, eps_done, b + 1)
                hold(pool)
                pool.tensor_tensor(rs[:, :], rs[:, :], halfneg[:, :], ALU.pow).then_inc(rstd_done, 1)

            def step(i, par):
                if has(i + 2):
                    rstd(i + 2, mv1, rs1, S["ln1_mv"], S["ln1_eps"], S["ln1_rstd"])
                if has(i - 1):
                    rstd(i - 1, mv2, rs2, S["ln2_mv"], S["ln2_eps"], S["ln2_rstd"])
                    for tile in range(NT):
                        wait(pool, S["xa_done"], 3 * (i - 1) + tile + 1)
                        hold(pool)
                        r = ROWS[tile]
                        pool.tensor_copy(xa[0:r, tile, 1, 0:D], xa[0:r, tile, 0, 0:D]).then_inc(S["xa_copied"], 1)
                    pool.tensor_copy(xa[:, :, :, D:ROW].bitcast(I32), ids[:, :, :].unsqueeze(3)).then_inc(S["xa_copied"], 1)
                    pool.tensor_scalar(ids[:, :, :], ids[:, :, :], float(N), None, ALU.add).then_inc(S["ids_next"], 1)
                    if isinstance(i, int) and i == B:
                        pool.wait_ge(S["xt_done"], 2 * B)
                        pool.wait_ge(S["eq_out"], 64 * B)
                        pool.memset(zrow[:, :, 0:D], 0.0).then_inc(S["route_made"], 1)
                        pool.iota(zrow[:, :, D:ROW].bitcast(I32), pattern=[[0, 2], [0, 1]], base=SKIP,
                                  channel_multiplier=0).then_inc(S["route_made"], 1)
                        pool.iota(start[:, :], pattern=[[REG, E]], base=0, channel_multiplier=0,
                                  allow_small_or_imprecise_dtypes=True).then_inc(S["route_made"], 1)
                        pool.iota(iblk[:, :], pattern=[[1, NBLK]], base=0, channel_multiplier=0,
                                  allow_small_or_imprecise_dtypes=True).then_inc(S["route_made"], 1)
                    wait(pool, S["slot_done"], i)
                    wait(pool, S["xa_copied"], 4 * i)
                    hold(pool)
                    for tile in range(NT):
                        for k in range(TOPK):
                            r = ROWS[tile]
                            pool.indirect_dma_start(
                                xs_d, bass.IndirectOffsetOnAxis(ap=slot[0:r, tile, k:k + 1], axis=0),
                                xa[0:r, tile, k, :], None).then_inc(S["sent"], 16)

            run_steps(pool, step)
            pool.wait_ge(S["sent"], 16 * 6 * B)

        @block.scalar
        def _(act):
            def step(i, par):
                for s in range(30):
                    if has(i):
                        u, pr = s // 2, s % 2
                        kcn = u % KC5
                        r = ROWS[kcn] if kcn < NT else SCR
                        if pr == 0:
                            wait(act, S["pv_done"], 15 * i + u - 2)
                        for e in range(2):
                            wait(act, S["st_filled"], 60 * i + 2 * s + e + 1)
                            act.activation(pt[0:r, u % 3, 2 * pr + e, :], ps_s[e][0:r, 0:N], ACT.Exp,
                                           scale=SCALE).then_inc(S["exp_done"], 1)
                    if s in (3, 13, 23):
                        b, g = (i - 1, 2) if s == 3 else (i, s // 10 - 1)
                        if has(b):
                            wait(act, S["pv_done"], 15 * b + 5 * g + 5)
                            wait(act, S["ot_turned"], 3 * b + g)
                            act.activation(ots[:, :], ps_o[:, 0:N], ACT.Copy).then_inc(S["ot_copied"], 1)
                    if s in XT and has(i + 2):
                        c = XT.index(s)
                        wait(act, S["xt_done"], 2 * (i + 2) + c + 1)
                        wait(act, S["qk_done"], 4 * (i + 2))
                        act.activation(xs[:, 0, c, 0:N], ps_j[c][0:KD, 0:N], ACT.Copy).then_inc(S["xs_hi"], 1)
                        act.activation(xt[par][:, c, 0:N], ps_j[c][0:KD, 0:N], ACT.Copy).then_inc(S["xt_copied"], 1)
                    if s in TURN_BACK and has(i - 1):
                        c = TURN_BACK.index(s)
                        wait(act, S["on_turned"], 2 * (i - 1) + c + 1)
                        wait(act, S["proj_done"], 2 * (i - 1))
                        act.activation(o2t[0:KD, c, :], ps_j[c][0:KD, 0:N], ACT.Copy).then_inc(S["o2_copied"], 1)
                    if s == TURN_MAX and has(i + 1):
                        b = i + 1
                        wait(act, S["mt_done"], b + 1)
                        wait(act, S["em_out"], 16 * b)
                        act.activation(mr[:, 0:N], ps_j[1][0:2 * H, 0:N], ACT.Copy).then_inc(S["mt_copied"], 1)
                    if s in X2T and has(i - 1):
                        c = X2T.index(s)
                        wait(act, S["x2t_done"], 2 * (i - 1) + c + 1)
                        wait(act, S["logit_done"], i - 1)
                        act.activation(x2t[:, c, :], ps_j[c][0:KD, 0:N], ACT.Copy).then_inc(S["x2t_copied"], 1)
                    if s in QK and has(i + 2):
                        j = QK.index(s)
                        wait(act, S["qk_done"], 4 * (i + 2) + j + 1)
                        wait(act, S["eq_out"], 64 * (i + 2))
                        act.activation(qp[:, j // 2, 0, j % 2, :], ps_j[j % 2][0:KD, 0:NP], ACT.Copy).then_inc(S["qk_hi"], 1)
                    if s == PREFIX and has(i - 1):
                        wait(act, S["ex_sub"], i)
                        act.activation(ex[:, :, :], ex[:, :, :], ACT.Exp).then_inc(S["ex_done"], 1)
                    if s in VALUES and has(i + 1):
                        vp = va[1 - par]
                        wait(act, S["v_done"], 2 * (i + 1) + VALUES.index(s) + 1)
                        for tile in (0, 1) if s == VALUES[0] else (2,):
                            r = ROWS[tile]
                            a = tile % 2
                            act.activation(vp[0:r, tile, :, 0:DH],
                                           ps_j[1 - VALUES.index(s)][0:r, a * D:(a + 1) * D].rearrange("p (h d) -> p h d", h=H),
                                           ACT.Copy).then_inc(S["v_copied"], 1)

            run_steps(act, step)

        @block.tensor
        def _(pe):
            def patches(i, tile, lo, hi_):
                for p in range(lo, hi_):
                    last = pe.matmul(ps_j[0][0:ROWS[0], tile * D:(tile + 1) * D],
                                     img[:, 7 * tile:7 * tile + 7, :].rearrange("k g (w q) -> k q (g w)", q=P)[:, p],
                                     wp[:, p, :], start=p == 0, stop=p == PX - 1)
                return last

            def turn(i, src, c, done):
                for tile in range(NT):
                    r = ROWS[tile]
                    last = pe.transpose(ps_j[c][0:KD, FIRST[tile]:FIRST[tile] + r], src(tile, r, c), ident[0:r, 0:r])
                last.then_inc(done, 1)

            def turn_outputs(b, g):
                pe.wait_ge(S["ot_copied"], 3 * b + g + 1)
                for tile in range(NT):
                    last = pe.transpose(ps_j[g // 2][:, 128 * tile:128 * tile + 128], ots[:, FIRST[tile]:FIRST[tile] + 128],
                                        ident[:, :])
                last.then_inc(S["ot_turned"], 1)

            def values(i, tiles, par):
                for tile in tiles:
                    r = ROWS[tile]
                    for kd in range(2):
                        last = pe.matmul(ps_j[0 if tile == 2 else 1][0:r, (tile % 2) * D:(tile % 2 + 1) * D],
                                         xt[1 - par][:, kd, FIRST[tile]:FIRST[tile] + r], wqkv[:, kd, 2 * D:3 * D],
                                         start=kd == 0, stop=kd == 1)
                last.then_inc(S["v_done"], 1)

            def with_values(b, par, u):
                g, kcn = u // KC5, u % KC5
                wait(pe, S["exp_done"], 60 * b + 4 * u + 4)
                if kcn == 0:
                    wait(pe, S["ot_copied"], 3 * b + g)
                    if g == 0:
                        wait(pe, S["v_copied"], 3 * b + 3)
                for j in range(HG):
                    h = HG * g + j
                    r = ROWS[kcn] if kcn < NT else SCR
                    v = va[par][0:r, kcn, h, :] if kcn < NT else vc[:, kcn - NT, h, :]
                    last = pe.matmul(ps_o[32 * j:32 * j + 32, 0:N], v, pt[0:r, u % 3, j, :],
                                     start=kcn == 0, stop=kcn == KC5 - 1)
                last.then_inc(S["pv_done"], 1)

            def maxima(b, par, unit, fills):
                g, tile, pr = unit // 6, unit % 6 // 2, unit % 2
                r = ROWS[tile]
                if unit % 6 == 0 and 0 in fills:
                    pe.wait_ge(g_in[0][g], 48 * (b + 1))
                    pe.wait_ge(g_in[1][g], 48 * (b + 1))
                    if isinstance(b, int) and b == 0:
                        pe.wait_ge(kc_in, 48)
                for f in fills:
                    n = 3 * unit + f
                    bank = ps_m[n % 3]
                    wait(pe, S["mx_read"], 54 * b + n - 2)
                    for e in ((f,) if f < 2 else (0, 1)):
                        h = HG * g + 2 * pr + e
                        q = qs[par][0:KMAX, h, FIRST[tile]:FIRST[tile] + r]
                        if f < 2:
                            last = pe.matmul(bank[0:r, 0:NP], q, ko[par][0:KMAX, h, :], start=True, stop=True)
                        else:
                            last = pe.matmul(bank[0:r, e * SC:(e + 1) * SC], q, kc[0:KMAX, h, :], start=True, stop=True)
                    last.then_inc(S["mx_filled"], 1)

            def step(i, par):
                for s in range(30):
                    u, pr = s // 2, s % 2
                    if has(i):
                        g, kcn = u // KC5, u % KC5
                        r = ROWS[kcn] if kcn < NT else SCR
                        if s == 0:
                            pe.wait_ge(S["m_in"], 16 * (i + 1))
                        for e in range(2):
                            n = 2 * s + e
                            wait(pe, S["exp_done"], 60 * i + n - 1)
                            h = HG * g + 2 * pr + e
                            k = ko[par][:, h, FIRST[kcn]:FIRST[kcn] + r] if kcn < NT else \
                                kc[:, h, (kcn - NT) * SCR:(kcn - NT + 1) * SCR]
                            pe.matmul(ps_s[e][0:r, 0:NP], k, qs[par][:, h, :], start=True, stop=True)\
                                .then_inc(S["st_filled"], 1)
                    unit = unit_at(i, s)
                    if unit:
                        maxima(unit[0], par if s in UNITS else 1 - par, unit[1], (0,))
                    if s < 4 and has(i + 2):
                        if s == 0:
                            wait_nearest(pe, [(i, S["v_copied"], 3 * i + 3),
                                              (i + 1, S["qk_split"], 4 * (i + 1) + 3)])
                            wait(pe, S["img_in"], 96 * (i + 2))
                        last = patches(i, s // 2, 4 * (s % 2), 4 * (s % 2) + 4)
                        if s == 3:
                            last.then_inc(S["patch_done"], 1)
                    if s == TURN_OUT[2] and has(i - 1):
                        wait_nearest(pe, [(i, S["v_copied"], 3 * i + 2), (i - 2, S["place_done"], i - 1)])
                        turn_outputs(i - 1, 2)
                    if s in TURN_BACK and has(i - 1):
                        c = TURN_BACK.index(s)
                        if c == 0:
                            pe.wait_ge(S["on_done"], 3 * i)
                            wait_nearest(pe, [(i + 2, S["patch_used"], i + 3), (i, S["v_copied"], 3 * i + 3),
                                              (i - 1, S["on_done"], 3 * i - 1)])
                        turn(i, lambda tile, r, c: on[0:r, tile, c * KD:(c + 1) * KD], c, S["on_turned"])
                    if s in PROJECT and has(i - 1):
                        if s == PROJECT[0]:
                            pe.wait_ge(S["o2_copied"], 2 * i)
                            wait_nearest(pe, [(i + 2, S["qk_split"], 4 * (i + 3))])
                        else:
                            wait_nearest(pe, [(i, S["on_done"], 3 * i + 1)])
                        for tile in (0, 1) if s == PROJECT[0] else (2,):
                            rr = ROWS[tile]
                            for kd in range(2):
                                last = pe.matmul(ps_j[1 - PROJECT.index(s)][0:rr, (tile % 2) * D:(tile % 2 + 1) * D],
                                                 o2t[0:KD + kd, kd, FIRST[tile]:FIRST[tile] + rr],
                                                 wpj[0:KD + kd, kd, :], start=kd == 0, stop=kd == 1)
                        last.then_inc(S["proj_done"], 1)
                    if s in XT and has(i + 2):
                        c = XT.index(s)
                        if c == 0:
                            pe.wait_ge(S["xh_done"], 3 * (i + 2) + 3)
                            wait_nearest(pe, [(i - 1, S["o2_copied"], 2 * i - 1), (i + 2, S["patch_used"], i + 3)])
                        else:
                            wait_nearest(pe, [(i - 1, S["o2_copied"], 2 * i), (i, S["v_copied"], 3 * i + 2),
                                              (i + 1, S["qk_split"], 4 * (i + 2))])
                        turn(i, lambda tile, r, c: xh[0:r, tile, c * KD:(c + 1) * KD], c, S["xt_done"])
                    if s in X2T and has(i - 1):
                        c = X2T.index(s)
                        if c == 0:
                            pe.wait_ge(S["xa_done"], 3 * i)
                        else:
                            wait_nearest(pe, [(i + 1, S["mt_copied"], i + 2), (i - 1, S["h2_done"], 3 * i - 1)])
                        turn(i, lambda tile, r, c: xa[0:r, tile, 0, c * KD:(c + 1) * KD], c, S["x2t_done"])
                    if s == TURN_OUT[0] and has(i):
                        wait_nearest(pe, [(i + 2, S["qk_split"], 4 * (i + 2) + 3), (i - 1, S["o2_copied"], 2 * i - 1)])
                        turn_outputs(i, 0)
                    if s == LOGITS and has(i - 1):
                        pe.wait_ge(S["x2t_copied"], 2 * (i - 1) + 2)
                        for tile in range(NT):
                            rr = ROWS[tile]
                            for kd in range(2):
                                last = pe.matmul(ps_j[0][0:rr, tile * E:(tile + 1) * E],
                                                 x2t[:, kd, FIRST[tile]:FIRST[tile] + rr], gt[:, kd, :],
                                                 start=kd == 0, stop=kd == 1)
                        last.then_inc(S["logit_done"], 1)
                    if s in QK and has(i + 2):
                        j = QK.index(s)
                        if j == 0:
                            pe.wait_ge(S["xs_lo"], 2 * (i + 2) + 2)
                        elif j >= 2:
                            pe.wait_ge(S["qk_split"], 4 * (i + 2) + j - 1)
                        cols = slice((j // 2) * D + (j % 2) * KD, (j // 2) * D + (j % 2 + 1) * KD)
                        terms = [(kd, l, x) for kd in range(2) for l, x in ((0, 0), (1, 0), (0, 1))]
                        for kd, l, x in terms:
                            last = pe.matmul(ps_j[j % 2][0:KD, 0:NP], wqs[:, l, kd, cols], xs[:, x, kd, :],
                                             start=(kd, l, x) == terms[0], stop=(kd, l, x) == terms[-1])
                        last.then_inc(S["qk_done"], 1)
                    if s == PREFIX and has(i - 1):
                        pe.wait_ge(S["both_done"], i)
                        m = both[:, :, :].rearrange("p t e -> p (t e)")
                        pe.matmul(ps_j[1][:, 0:NT * E], ut[:, :], m, start=True, stop=True)
                        pe.matmul(ps_j[1][:, NT * E:2 * NT * E], ones[:, :], m, start=True, stop=True)\
                            .then_inc(S["prefix_done"], 1)
                    if s == TURN_MAX and has(i + 1):
                        pe.wait_ge(S["m_split"], 2 * (i + 2))
                        wait_nearest(pe, [(i - 1, S["h2_done"], 3 * i - 1), (i + 2, S["qk_split"], 4 * (i + 3))])
                        for tile in range(NT):
                            rr = ROWS[tile]
                            last = pe.transpose(ps_j[1][0:2 * H, FIRST[tile]:FIRST[tile] + rr],
                                                negm2[0:rr, tile, :, :].rearrange("p l h -> p (l h)"), ident[0:rr, 0:rr])
                        last.then_inc(S["mt_done"], 1)
                    if s == TURN_OUT[1] and has(i):
                        wait_nearest(pe, [(i - 1, S["topi_done"], 3 * i), (i, S["on_done"], 3 * i + 1)])
                        turn_outputs(i, 1)
                    if s in VALUES and has(i + 1):
                        if s == VALUES[0]:
                            wait_nearest(pe, [(i - 1, S["place_done"], i), (i + 1, S["mt_copied"], i + 2)])
                        else:
                            wait_nearest(pe, [(i, S["on_done"], 3 * i + 2), (i + 2, S["qk_split"], 4 * (i + 2) + 3)])
                        values(i, (0, 1) if s == VALUES[0] else (2,), par)
                    if pr == 1:
                        if u < 2:
                            if has(i - 1):
                                with_values(i - 1, 1 - par, 13 + u)
                        elif has(i):
                            with_values(i, par, u - 2)
                    if unit:
                        maxima(unit[0], par if s in UNITS else 1 - par, unit[1], (1, 2))

            run_steps(pe, step)

        @block.vector
        def _(dve):
            def stats(b, src, stt, mv, s_stat, s_mv):
                hold(dve)
                for tile in range(NT):
                    r = ROWS[tile]
                    dve.bn_stats(stt[0:r, tile, :], src[0:r, b, tile, :]).then_inc(s_stat, 1)
                for tile in range(NT):
                    r = ROWS[tile]
                    wait(dve, s_stat, 3 * b + tile + 1)
                    hold(dve)
                    dve.bn_aggr(mv[0:r, tile, :], stt[0:r, tile, :]).then_inc(s_mv, 1)

            def maxima(b, unit, fills):
                g, tile, pr = unit // 6, unit % 6 // 2, unit % 2
                r = ROWS[tile]
                if unit == 0 and 0 in fills:
                    wait(dve, S["mx_comb"], b)
                for f in fills:
                    n = 3 * unit + f
                    c = tile * H + HG * g + 2 * pr
                    wait(dve, S["mx_filled"], 54 * b + n + 1)
                    if f < 2:
                        dve.tensor_reduce(mxp[0:r, c + f:c + f + 1, 0], ps_m[n % 3][0:r, 0:N], AX.X, ALU.max)\
                            .then_inc(S["mx_read"], 1)
                    else:
                        dve.tensor_reduce(mxp[0:r, c:c + 2, 1],
                                          ps_m[n % 3][0:r, 0:2 * SC].rearrange("p (e n) -> p e n", e=2),
                                          AX.X, ALU.max).then_inc(S["mx_read"], 1)

            def norm_outputs(b, g):
                o = ps_j[g // 2][:, 0:NT * 128].rearrange("p (t h c) -> p t h c", t=NT, h=HG)
                wait(dve, S["ot_turned"], 3 * b + g + 1)
                dve.reciprocal(rec[:, :, :], o[:, :, :, DH]).then_inc(S["rec_done"], 1)
                wait(dve, S["rec_done"], 3 * b + g + 1)
                if g == 0:
                    wait(dve, S["on_turned"], 2 * b)
                w = HG * DH
                dve.tensor_tensor(on[:, :, g * w:(g + 1) * w].rearrange("p t (h c) -> p t h c", h=HG), o[:, :, :, 0:DH],
                                  rec[:, :, :].unsqueeze(3).broadcast_to([128, NT, HG, DH]), ALU.mult)\
                    .then_inc(S["on_done"], 1)

            def step(i, par):
                for s in range(30):
                    unit = unit_at(i, s)
                    if unit:
                        maxima(unit[0], unit[1], (0,))
                    if s == 4 and has(i + 2):
                        b = i + 2
                        wait(dve, S["patch_done"], b + 1)
                        dve.tensor_tensor(hs[0:ROWS[0], b, 0:2, :],
                                          ps_j[0][0:ROWS[0], 0:2 * D].rearrange("p (a d) -> p a d", a=2),
                                          posb[0:ROWS[0], :, :], ALU.add).then_inc(S["patch_used"], 1)
                    if s == TURN_OUT[2] and has(i - 1):
                        norm_outputs(i - 1, 2)
                    if s in PROJECT and has(i - 1):
                        b = i - 1
                        wait(dve, S["proj_done"], 2 * b + PROJECT.index(s) + 1)
                        for tile in (0, 1) if s == PROJECT[0] else (2,):
                            r = ROWS[tile]
                            dve.tensor_tensor(hs[0:r, b, tile, :], ps_j[1 - PROJECT.index(s)][0:r, (tile % 2) * D:(tile % 2 + 1) * D],
                                              hs[0:r, b, tile, :], ALU.add).then_inc(S["h2_done"], 1)
                    if s in XT and has(i + 2):
                        c = XT.index(s)
                        wait(dve, S["xs_hi"], 2 * (i + 2) + c + 1)
                        wait(dve, S["xt_copied"], 2 * (i + 2) + c + 1)
                        dve.tensor_tensor(xs[:, 1, c, 0:N], ps_j[c][0:KD, 0:N], xs[:, 0, c, 0:N].bitcast(F32),
                                          ALU.subtract).then_inc(S["xs_lo"], 1)
                    if s == NORM1 and has(i + 2):
                        b = i + 2
                        wait(dve, S["ln1_rstd"], b + 1)
                        wait(dve, S["xt_done"], 2 * b)
                        for tile in range(NT):
                            r = ROWS[tile]
                            dve.tensor_scalar(xh[0:r, tile, :], hs[0:r, b, tile, :], mv1[0:r, tile, 0:1],
                                              rs1[0:r, tile:tile + 1], ALU.subtract, ALU.mult).then_inc(S["xh_done"], 1)
                    if s == NORM2 and has(i - 1):
                        b = i - 1
                        wait(dve, S["ln2_rstd"], b + 1)
                        wait(dve, S["sent"], 96 * b)
                        wait(dve, S["x2t_done"], 2 * b)
                        for tile in range(NT):
                            r = ROWS[tile]
                            dve.tensor_scalar(xa[0:r, tile, 0, 0:D], hs[0:r, b, tile, :], mv2[0:r, tile, 0:1],
                                              rs2[0:r, tile:tile + 1], ALU.subtract, ALU.mult).then_inc(S["xa_done"], 1)
                    if s == TURN_OUT[0] and has(i):
                        norm_outputs(i, 0)
                    if s == LOGITS and has(i - 1):
                        b = i - 1
                        wait(dve, S["logit_done"], b + 1)
                        hold(dve)
                        for tile in range(NT):
                            r = ROWS[tile]
                            dve.max(top[0:r, tile, :], ps_j[0][0:r, tile * E:(tile + 1) * E]).then_inc(S["top_done"], 1)
                        for tile in range(NT):
                            r = ROWS[tile]
                            wait(dve, S["top_done"], 3 * b + tile + 1)
                            hold(dve)
                            dve.max_index(topi[0:r, tile, :], top[0:r, tile, :], ps_j[0][0:r, tile * E:(tile + 1) * E])\
                                .then_inc(S["topi_done"], 1)
                        wait(dve, S["topi_done"], 3 * b + 3)
                        dve.tensor_copy(topf[:, :, :], topi[:, :, 0:TOPK]).then_inc(S["topf_done"], 1)
                        wait(dve, S["topf_done"], b + 1)
                        full = [128, NT, TOPK, E]
                        dve.tensor_tensor(msk[:, :, :, :], iota8[:, :].unsqueeze(1).unsqueeze(1).broadcast_to(full),
                                          topf[:, :, :].unsqueeze(3).broadcast_to(full), ALU.is_equal)\
                            .then_inc(S["msk_done"], 1)
                        wait(dve, S["msk_done"], b + 1)
                        dve.tensor_tensor(both[:, :, :], msk[:, :, 0, :], msk[:, :, 1, :], ALU.add)\
                            .then_inc(S["both_done"], 1)
                        dve.tensor_tensor(ex[:, :, :], top[:, :, :], top[:, :, 0:1].broadcast_to([128, NT, E]),
                                          ALU.subtract).then_inc(S["ex_sub"], 1)
                    if s in QK and has(i + 2):
                        j = QK.index(s)
                        wait(dve, S["qk_hi"], 4 * (i + 2) + j + 1)
                        dve.tensor_tensor(qp[:, j // 2, 1, j % 2, :], ps_j[j % 2][0:KD, 0:NP],
                                          qp[:, j // 2, 0, j % 2, :].bitcast(F32), ALU.subtract)\
                            .then_inc(S["qk_split"], 1)
                    if s == PREFIX and has(i - 1):
                        b = i - 1
                        wait(dve, S["prefix_done"], b + 1)
                        for tile in range(NT):
                            wait(dve, S["base_step"], 4 * b + tile)
                            dve.tensor_tensor(base[:, tile + 1, :], ps_j[1][:, (NT + tile) * E:(NT + tile + 1) * E],
                                              base[:, tile, :], ALU.add).then_inc(S["base_step"], 1)
                        wait(dve, S["base_step"], 4 * b + NT)
                        dve.tensor_tensor(place[:, :, :], ps_j[1][:, 0:NT * E].rearrange("p (t e) -> p t e", t=NT),
                                          base[:, 0:NT, :], ALU.add).then_inc(S["place_done"], 1)
                        wait(dve, S["place_done"], b + 1)
                        dve.tensor_copy(base[:, 0, :], base[:, NT, :]).then_inc(S["base_step"], 1)
                        dve.tensor_tensor(pick[:, :, :, :], msk[:, :, :, :],
                                          place[:, :, :].unsqueeze(2).broadcast_to([128, NT, TOPK, E]), ALU.mult)\
                            .then_inc(S["pick_done"], 1)
                        wait(dve, S["pick_done"], b + 1)
                        dve.tensor_reduce(slotf[:, :, :], pick[:, :, :, :], AX.X, ALU.add).then_inc(S["slotf_done"], 1)
                        wait(dve, S["slotf_done"], b + 1)
                        wait(dve, S["sent"], 96 * b)
                        dve.tensor_copy(slot[:, :, :], slotf[:, :, :]).then_inc(S["slot_done"], 1)
                    if s == MAX_DONE and has(i + 1):
                        b = i + 1
                        wait(dve, S["mx_read"], 54 * b + 54)
                        wait(dve, S["mt_done"], b)
                        dve.tensor_reduce(negm[:, :, :].rearrange("p t h -> p (t h)"), mxp[:, :, :], AX.X, ALU.max,
                                          negate=True).then_inc(S["mx_comb"], 1)
                        wait(dve, S["mx_comb"], b + 1)
                        dve.tensor_copy(negm2[:, :, 0, :].bitcast(F32R), negm[:, :, :]).then_inc(S["m_split"], 1)
                        wait(dve, S["m_split"], 2 * b + 1)
                        dve.tensor_tensor(negm2[:, :, 1, :].bitcast(F32R), negm[:, :, :], negm2[:, :, 0, :],
                                          ALU.subtract).then_inc(S["m_split"], 1)
                    if s == LN1 and has(i + 2):
                        b = i + 2
                        wait(dve, S["patch_used"], b + 1)
                        wait(dve, S["ln1_rstd"], b)
                        stats(b, hs, st1, mv1, S["ln1_stat"], S["ln1_mv"])
                    if s == LN2 and has(i - 1):
                        b = i - 1
                        wait(dve, S["h2_done"], 3 * b + 3)
                        wait(dve, S["ln2_rstd"], b)
                        stats(b, hs, st2, mv2, S["ln2_stat"], S["ln2_mv"])
                    if s == WEIGHTS and has(i - 1):
                        b = i - 1
                        wait(dve, S["ex_done"], b + 1)
                        dve.tensor_reduce(zsum[:, :], ex[:, :, :], AX.X, ALU.add).then_inc(S["z_done"], 1)
                        wait(dve, S["z_done"], b + 1)
                        dve.scalar_tensor_tensor(out=den[:, :], in0=zsum[:, :], scalar=1e-9, in1=ex[:, :, 1],
                                                 op0=ALU.mult, op1=ALU.add).then_inc(S["den_a"], 1)
                        wait(dve, S["den_a"], b + 1)
                        dve.tensor_tensor(den[:, :], den[:, :], ex[:, :, 0], ALU.add).then_inc(S["den_done"], 1)
                        wait(dve, S["den_done"], b + 1)
                        dve.reciprocal(den[:, :], den[:, :]).then_inc(S["rden_done"], 1)
                        wait(dve, S["rden_done"], b + 1)
                        dve.tensor_tensor(gw[:, b, :, :], ex[:, :, 0:TOPK],
                                          den[:, :].unsqueeze(2).broadcast_to([128, NT, TOPK]), ALU.mult)\
                            .then_inc(S["gw_done"], 1)
                    if s == TURN_OUT[1] and has(i):
                        norm_outputs(i, 1)
                    if unit:
                        maxima(unit[0], unit[1], (1, 2))

            def list_blocks():
                done = S["listing"]
                dve.wait_ge(S["route_made"], 4)
                dve.wait_ge(S["base_step"], 4 * B)
                dve.tensor_copy(nexti[:, :], base[0:1, 0, :]).then_inc(S["rows_known"], 1)
                dve.tensor_tensor(count[:, :], base[0:1, 0, :], start[:, :], ALU.subtract).then_inc(done, 1)
                dve.wait_ge(done, 1)
                dve.tensor_scalar(counti[:, :], count[:, :], float(BLK - 1), None, ALU.add).then_inc(done, 1)
                dve.wait_ge(done, 2)
                dve.tensor_scalar(counti[:, :], counti[:, :], BLK.bit_length() - 1, None, ALU.arith_shift_right)\
                    .then_inc(done, 1)
                dve.wait_ge(done, 3)
                dve.tensor_copy(nblk[:, :], counti[:, :]).then_inc(done, 1)
                dve.wait_ge(done, 4)
                dve.tensor_scalar(skip[:, :], nblk[:, :], -float(BLK), float(REG), ALU.mult, ALU.add).then_inc(done, 1)
                dve.tensor_copy(upto[:, 0:1], nblk[:, 0:1]).then_inc(done, 1)
                for e in range(1, E):
                    dve.wait_ge(done, 5 + e)
                    dve.tensor_tensor(upto[:, e:e + 1], nblk[:, e:e + 1], upto[:, e - 1:e], ALU.add).then_inc(done, 1)
                dve.wait_ge(done, 5 + E)
                full = [1, NBLK, E]
                dve.tensor_tensor(past[:, :, :], iblk[:, :].unsqueeze(2).broadcast_to(full),
                                  upto[:, :].unsqueeze(1).broadcast_to(full), ALU.is_ge).then_inc(done, 1)
                dve.wait_ge(done, 6 + E)
                dve.tensor_tensor(part[:, :, :], past[:, :, :], skip[:, :].unsqueeze(1).broadcast_to(full), ALU.mult)\
                    .then_inc(done, 1)
                dve.tensor_reduce(tabf[:, 0, :], past[:, :, :], AX.X, ALU.add).then_inc(done, 1)
                dve.wait_ge(done, 7 + E)
                dve.tensor_reduce(tabf[:, 1, :], part[:, :, :], AX.X, ALU.add).then_inc(done, 1)
                dve.wait_ge(done, 9 + E)
                dve.tensor_scalar(tabf[:, 0, :], tabf[:, 0, :], float(E - 1), None, ALU.min).then_inc(done, 1)
                dve.scalar_tensor_tensor(out=tabf[:, 1, :], in0=iblk[:, :], scalar=float(BLK), in1=tabf[:, 1, :],
                                         op0=ALU.mult, op1=ALU.add).then_inc(done, 1)
                dve.wait_ge(done, 11 + E)
                dve.tensor_scalar(tabf[:, 1, :], tabf[:, 1, :], float(E * REG), None, ALU.min).then_inc(done, 1)
                dve.wait_ge(done, 12 + E)
                dve.tensor_copy(table[:, :, :], tabf[:, :, :]).then_inc(S["listed"], 1)
                dve.wait_ge(S["listed"], 1)

            dve.memset(mxp[:, :, :], 0.0).then_inc(S["cleared"], 1)
            dve.memset(topi[:, :, :], 99).then_inc(S["cleared"], 1)
            dve.memset(top[:, :, :], 0.0).then_inc(S["cleared"], 1)
            dve.memset(mv1[:, :, :], 1.0).then_inc(S["cleared"], 1)
            dve.memset(mv2[:, :, :], 1.0).then_inc(S["cleared"], 1)
            dve.memset(mr[:, N:NP].bitcast(F32), 0.0).then_inc(S["cleared"], 1)
            dve.memset(ones[:, :], 1.0).then_inc(S["cleared"], 1)
            dve.memset(o2t[KD:KD + 1, :, :], 1.0).then_inc(S["cleared"], 1)
            dve.memset(xs[:, :, :, N:NP].bitcast(F32), 0.0).then_inc(S["cleared"], 1)
            dve.wait_ge(S["cleared"], 9)
            run_steps(dve, step)
            list_blocks()
            dve.wait_ge(S["gw_done"], B)


def experts(nc, sb, pb, sem, t):
    ident, xs_d, ys_d, table = t["ident"], t["xs_d"], t["ys_d"], t["table"]
    HC = HID // 128
    RING = 4
    with ExitStack() as st:
        R2 = D - 128
        xb = [sb(st, f"xb{p}", [128, 2, R2 + ROW]) for p in range(RING)]
        w1b = [sb(st, f"w1b{p}", [128, 2, HID]) for p in range(RING)]
        b1b = [sb(st, f"b1b{p}", [128, HC]) for p in range(RING)]
        w2b = [sb(st, f"w2b{p}", [128, HC, D]) for p in range(RING)]
        b2b = [sb(st, f"b2b{p}", [128, D]) for p in range(RING)]
        w1h = [sb(st, f"w1h{p}", [128, 2, HID], F32R) for p in range(2)]
        w1l = [sb(st, f"w1l{p}", [128, 2, HID], F32R) for p in range(2)]
        xbh = [sb(st, f"xbh{p}", [128, 2, BLK], F32R) for p in range(RING)]
        xbl = [sb(st, f"xbl{p}", [128, BLK], F32R) for p in range(RING)]
        w2s = [sb(st, f"w2s{p}", [128, HC, 2, D], F32R) for p in range(2)]
        ht = [sb(st, f"ht{p}", [128, HC, BLK]) for p in range(2)]
        hh = [sb(st, f"hh{p}", [128, HC, BLK], F32R) for p in range(2)]
        hl = [sb(st, f"hl{p}", [128, HC, BLK], F32R) for p in range(2)]
        yb = [sb(st, f"yb{p}", [128, 2, D]) for p in range(RING)]
        ps_t = pb(st, "ps_t", [128, 512])
        ps_h = [pb(st, f"ps_h{n}", [128, 512]) for n in range(4)]
        ps_y = pb(st, "ps_y", [128, 2, 512])
        x_in = [sem(st, f"x_in{p}") for p in range(RING)]
        w1_in = [sem(st, f"w1_in{p}") for p in range(RING)]
        w2_in = [sem(st, f"w2_in{p}") for p in range(RING)]
        y_sent = [sem(st, f"y_sent{p}") for p in range(RING)]
        xt_done, xt_hi, xt_lo, w_hi, w_lo, w2_hi, w2_lo, w2_lo_pool, h_done, h_act, h_hi, h_lo = (
            sem(st, f"ex_{n}") for n in ("xt_done", "xt_hi", "xt_lo", "w_hi", "w_lo", "w2_hi", "w2_lo", "w2_lo_pool",
                                         "h_done", "h_act", "h_hi", "h_lo"))
        y_done, y_half, y_sum = (sem(st, f"ex_{n}") for n in ("y_done", "y_half", "y_sum"))
        POOL_HC = 2
        block = st.enter_context(nc.Block())

        def after(blk, d=1):
            i, p, uses = blk
            return i + d, (p + d) % RING, uses + (p + d) // RING

        def run_blocks(eng, one):
            for i in range(RING):
                one((i, i, 0))
            turns = NBLK // RING
            with eng.Fori(1, turns - 1) as n:
                for p in range(RING):
                    one((n * RING + p, p, n))
            for i in range(RING * (turns - 1), NBLK):
                one((i, i % RING, i // RING))

        @block.sync
        def _(sp):
            def load(blk):
                i, p, uses = blk
                def last_block(done, value):
                    wait(sp, done, value)
                    hold(sp)

                last_block(y_done, i - RING + 1)
                e = sp.value_load(table[0:1, 0, bass.ds(i, 1)], min_val=0, max_val=E - 1)
                row = sp.value_load(table[0:1, 1, bass.ds(i, 1)], min_val=0, max_val=E * REG)
                sp.dma_start(w1b[p][:, 0, :], t["w1"][bass.ds(e, 1), 0:128].rearrange("a p n -> p (a n)"))\
                    .then_inc(w1_in[p], 16)
                for h in range(2):
                    sp.dma_start(w1b[p][R2 * h:R2 * h + R2, 1, :],
                                 t["w1"][bass.ds(e, 1), 128:D].rearrange("a p n -> p (a n)")).then_inc(w1_in[p], 16)
                sp.dma_start(b1b[p][:, :], t["b1t_d"][bass.ds(e, 1)].rearrange("a p n -> p (a n)")).then_inc(w1_in[p], 16)
                last_block(xt_done, i - RING + 1)
                last_block(y_sent[p], 32 * uses)
                rows = xs_d[bass.ds(row, BLK), :].rearrange("(a p) n -> p a n", p=128)
                sp.dma_start(xb[p][:, :, 0:D], rows[:, :, 0:D]).then_inc(x_in[p], 16)
                sp.dma_start(xb[p][:, :, D:R2 + ROW], rows[:, :, 128:ROW]).then_inc(x_in[p], 16)
                sp.dma_start(w2b[p][:, :, :], t["w2"][bass.ds(e, 1)].rearrange("a (c p) n -> p (a c) n", c=HC))\
                    .then_inc(w2_in[p], 16)
                last_block(y_sum, i - RING + 1)
                sp.dma_start(b2b[p][:, :], t["b2"][bass.ds(e, 1), :].broadcast_to([128, D])).then_inc(w2_in[p], 16)

            sp.wait_ge(t["b1_out"], 16 * E)
            run_blocks(sp, load)

        @block.tensor
        def _(pe):
            def turn(blk):
                i, p, uses = blk
                wait(pe, x_in[p], 32 * (uses + 1))
                wait(pe, xt_lo, 2 * i)
                for c in range(2):
                    for a in range(2):
                        last = pe.transpose(ps_t[:, c * BLK + a * 128:c * BLK + a * 128 + 128],
                                            xb[p][:, a, c * 128:(c + 1) * 128], ident[:, :])
                last.then_inc(xt_done, 1)

            def up(blk):
                i, p, uses = blk
                wait(pe, xt_lo, 2 * (i + 1))
                wait(pe, w_lo, 2 * (i + 1))
                q = p % 2
                terms = [(w1h[q][:, 0], xbh[p][:, 0]), (w1h[q][:, 0], xbl[p][:, :]), (w1l[q][:, 0], xbh[p][:, 0]),
                         (w1h[q][:, 1], xbh[p][:, 1]), (w1l[q][0:R2, 1], xbh[p][0:R2, 1])]
                for m in range(HC):
                    bank = ps_h[(3 * p + m // 2) % 4]
                    if m % 2 == 0:
                        wait(pe, h_hi, 6 * i + m - 6)
                    for n, (w, x) in enumerate(terms):
                        last = pe.matmul(bank[:, (m % 2) * BLK:(m % 2 + 1) * BLK], w[:, m * 128:(m + 1) * 128], x,
                                         start=n == 0, stop=n == len(terms) - 1)
                    if m % 2:
                        last.then_inc(h_done, 1)

            def down(blk):
                i, p, uses = blk
                q = p % 2
                wait(pe, w2_lo, i + 1)
                wait(pe, w2_lo_pool, i + 1)
                wait(pe, h_lo, 3 * i + 3)
                wait(pe, y_sum, i)
                for a in range(2):
                    rows = slice(a * 128, (a + 1) * 128)
                    terms = [(m, x) for m in range(HC) for x in ("hi lo" if m == 0 else "lo hi").split()]
                    for m, x in terms:
                        if x == "hi":
                            last = pe.matmul(ps_y[:, a, 0:2 * D], hh[q][:, m, rows],
                                             w2s[q][:, m, :, :].rearrange("p l d -> p (l d)"),
                                             start=m == 0, stop=m == HC - 1)
                        else:
                            pe.matmul(ps_y[:, a, 0:D], hl[q][:, m, rows], w2s[q][:, m, 0, :], start=False, stop=False)
                last.then_inc(y_done, 1)

            def one(blk):
                if isinstance(blk[0], int) and blk[0] == 0:
                    turn(blk)
                    up(blk)
                    turn(after(blk))
                    return
                up(blk)
                if not isinstance(blk[0], int) or blk[0] + 1 < NBLK:
                    turn(after(blk))
                down(after(blk, -1))

            run_blocks(pe, one)
            down((NBLK - 1, (NBLK - 1) % RING, (NBLK - 1) // RING))

        @block.scalar
        def _(act):
            def split(blk):
                i, p, uses = blk
                wait(act, w1_in[p], 64 * (uses + 1))
                wait(act, h_done, 3 * (i - 1))
                for c in range(2):
                    act.activation(w1h[p % 2][:, c, :], w1b[p][:, c, :], ACT.Copy).then_inc(w_hi, 1)

            def one(blk):
                i, p, uses = blk
                if isinstance(i, int) and i == 0:
                    split(blk)
                if not isinstance(i, int) or i + 1 < NBLK:
                    split(after(blk))
                q = p % 2
                wait(act, y_done, i - 1)
                wait(act, h_lo, 3 * (i - 1))
                for m in range(HC // 2):
                    wait(act, h_done, 3 * i + m + 1)
                    for to, done in ((ht[q], h_act), (hh[q], h_hi)):
                        for c in range(2):
                            act.activation(to[:, 2 * m + c, :], ps_h[(3 * p + m) % 4][:, c * BLK:(c + 1) * BLK], ACT.Gelu,
                                           bias=b1b[p][:, 2 * m + c:2 * m + c + 1]).then_inc(done, 1)
                wait(act, w2_in[p], 32 * (uses + 1))
                act.activation(w2s[q][:, :, 0, :], w2b[p][:, :, :], ACT.Copy).then_inc(w2_hi, 1)

            run_blocks(act, one)

        @block.vector
        def _(dve):
            def split(blk):
                i, p, uses = blk
                for c, k in enumerate((128, R2)):
                    wait(dve, w_hi, 2 * i + c + 1)
                    dve.tensor_tensor(w1l[p % 2][0:k, c, :], w1b[p][0:k, c, :], w1h[p % 2][0:k, c, :].bitcast(F32),
                                      ALU.subtract).then_inc(w_lo, 1)

            def copy(blk):
                i, p, uses = blk
                turned = ps_t[:, :].rearrange("p (c n) -> p c n", c=2)
                wait(dve, xt_done, i + 1)
                wait(dve, h_done, 3 * (i - RING + 1))
                dve.tensor_copy(xbh[p][:, :, :], turned).then_inc(xt_hi, 1)
                wait(dve, xt_hi, i + 1)
                dve.tensor_tensor(xbl[p][:, :], turned[:, 0, :], xbh[p][:, 0, :].bitcast(F32), ALU.subtract).then_inc(xt_lo, 1)
                dve.tensor_tensor(xbh[p][R2:128, 1, :], turned[R2:128, 1, :], xbh[p][R2:128, 1, :].bitcast(F32),
                                  ALU.subtract).then_inc(xt_lo, 1)

            def split_weights_down(blk):
                i, p, uses = blk
                q = p % 2
                wait(dve, w2_hi, i + 1)
                dve.tensor_tensor(w2s[q][:, POOL_HC:HC, 1, :], w2b[p][:, POOL_HC:HC, :],
                                  w2s[q][:, POOL_HC:HC, 0, :].bitcast(F32), ALU.subtract).then_inc(w2_lo, 1)

            def split_hidden(blk, pairs):
                i, p, uses = blk
                q = p % 2
                for m in pairs:
                    wait(dve, h_act, 6 * i + 2 * m + 2)
                    wait(dve, h_hi, 6 * i + 2 * m + 2)
                    mm = slice(2 * m, 2 * m + 2)
                    dve.tensor_tensor(hl[q][:, mm, :], ht[q][:, mm, :], hh[q][:, mm, :].bitcast(F32), ALU.subtract)\
                        .then_inc(h_lo, 1)

            def finish(blk):
                i, p, uses = blk
                wait(dve, y_done, i + 1)
                wait(dve, w2_in[p], 32 * (uses + 1))
                wait(dve, y_sent[p], 32 * uses)
                dve.tensor_tensor(yb[p][:, :, :], ps_y[:, :, 0:D],
                                  b2b[p][:, :].unsqueeze(1).broadcast_to([128, 2, D]), ALU.add).then_inc(y_half, 1)
                wait(dve, y_half, i + 1)
                dve.tensor_tensor(yb[p][:, :, :], ps_y[:, :, D:2 * D], yb[p][:, :, :], ALU.add).then_inc(y_sum, 1)

            def one(blk):
                if isinstance(blk[0], int) and blk[0] == 0:
                    copy(blk)
                    split(blk)
                    split(after(blk))
                    split_hidden(blk, (0,))
                    copy(after(blk))
                    split_hidden(blk, (1, 2))
                    split_weights_down(blk)
                    return
                if not isinstance(blk[0], int) or blk[0] + 1 < NBLK:
                    split(after(blk))
                split_hidden(blk, (0,))
                if not isinstance(blk[0], int) or blk[0] + 1 < NBLK:
                    copy(after(blk))
                split_hidden(blk, (1, 2))
                finish(after(blk, -1))
                split_weights_down(blk)

            run_blocks(dve, one)
            finish((NBLK - 1, (NBLK - 1) % RING, (NBLK - 1) // RING))

        @block.gpsimd
        def _(pool):
            def split_down(blk):
                i, p, uses = blk
                q = p % 2
                wait(pool, w2_hi, i + 1)
                hold(pool)
                pool.tensor_tensor(w2s[q][:, 0:POOL_HC, 1, :], w2b[p][:, 0:POOL_HC, :],
                                   w2s[q][:, 0:POOL_HC, 0, :].bitcast(F32), ALU.subtract).then_inc(w2_lo_pool, 1)

            def send(blk):
                i, p, uses = blk
                wait(pool, y_sum, i + 1)
                hold(pool)
                for a in range(2):
                    pool.indirect_dma_start(
                        ys_d, bass.IndirectOffsetOnAxis(ap=xb[p][:, a, R2 + D:R2 + ROW].bitcast(I32), axis=0), yb[p][:, a, :], None,
                        bounds_check=TOPK * T - 1, oob_is_err=False).then_inc(y_sent[p], 16)

            def one(blk):
                split_down(blk)
                if not (isinstance(blk[0], int) and blk[0] == 0):
                    send(after(blk, -1))

            run_blocks(pool, one)
            send((NBLK - 1, (NBLK - 1) % RING, (NBLK - 1) // RING))
            for p in range(RING):
                pool.wait_ge(y_sent[p], 32 * NBLK // RING)


def combine(nc, sb, pb, sem, t):
    hs, gw, ys_d, out = t["hs"], t["gw"], t["ys_d"], t["out"]
    IG = 4
    with ExitStack() as st:
        yl = [sb(st, f"yl{g}", [128, NT, IG, TOPK, D]) for g in range(B // IG)]
        y_in = [[sem(st, f"yl_in{g}_{tile}") for tile in range(NT)] for g in range(B // IG)]
        half, summed, stored = (sem(st, f"co_{n}") for n in ("half", "summed", "stored"))
        block = st.enter_context(nc.Block())

        @block.sync
        def _(sp):
            rows = ys_d.rearrange("(k b n) d -> n b k d", k=TOPK, b=B)
            for g in range(B // IG):
                for tile in range(NT):
                    r = ROWS[tile]
                    for k in range(TOPK):
                        sp.dma_start(yl[g][0:r, tile, :, k, :], rows[FIRST[tile]:FIRST[tile] + r, g * IG:(g + 1) * IG, k, :])\
                            .then_inc(y_in[g][tile], 16)

        @block.vector
        def _(dve):
            for g in range(B // IG):
                for tile in range(NT):
                    r = ROWS[tile]
                    dve.wait_ge(y_in[g][tile], 32)
                    for k in range(TOPK):
                        for j in range(IG):
                            b = g * IG + j
                            if k:
                                dve.wait_ge(half, (g * NT + tile) * IG + j + 1)
                            dve.scalar_tensor_tensor(out=hs[0:r, b, tile, :], in0=yl[g][0:r, tile, j, k, :],
                                                     scalar=gw[0:r, b, tile, k:k + 1], in1=hs[0:r, b, tile, :],
                                                     op0=ALU.mult, op1=ALU.add).then_inc(summed if k else half, 1)

        @block.scalar
        def _(act):
            for g in range(B // IG):
                to = out[g * IG:(g + 1) * IG].rearrange("b n d -> n b d")
                of = hs[:, g * IG:(g + 1) * IG, :, :]
                act.wait_ge(summed, (g * NT + 1) * IG)
                act.dma_start(to[1:1 + ROWS[0]], of[0:ROWS[0], :, 0, :]).then_inc(stored, 16)
                act.wait_ge(summed, (g * NT + 2) * IG)
                act.dma_start(to[1 + ROWS[0]:1 + NPATCH], of[0:ROWS[0], :, 1, :]).then_inc(stored, 16)
                act.dma_start(to[0:1], of[ROWS[0]:ROWS[1], :, 1, :]).then_inc(stored, 16)
                act.wait_ge(summed, (g * NT + 3) * IG)
                act.dma_start(to[NPATCH + 1:N], of[0:TXT, :, 2, :]).then_inc(stored, 16)
            act.wait_ge(stored, 16 * 4 * B // IG)


_INS = ['x', 'txt', 'L0_tok_W', 'L0_tok_b', 'L0_tok_class_token', 'L0_tok_pos_emb', 'L0_attn_sc_token', 'L0_attn_W_qkv',
        'L0_attn_W_proj', 'L0_attn_b_proj', 'L0_ffn_gate_w', 'L0_ffn_w1', 'L0_ffn_b1', 'L0_ffn_w2', 'L0_ffn_b2']


def kernel(**inputs):
    import numpy as _np
    import concourse.bacc as _bacc
    from concourse import mybir as _mybir
    from concourse.bass_utils import run_bass_kernel_spmd as _run

    nc = _bacc.Bacc("TRN2", target_bir_lowering=False, num_devices=1)
    arrays, args = {}, []
    for name in _INS:
        a = _np.ascontiguousarray(inputs[name])
        arrays[f"in_{name}_dram"] = a
        args.append(nc.dram_tensor(f"in_{name}_dram", a.shape, _mybir.dt.from_np(a.dtype), kind="ExternalInput").ap())
    res = nc.dram_tensor("out_0_dram", (B, N, D), _mybir.dt.float32, kind="ExternalOutput").ap()
    build(nc, *args, res)
    r = _run(nc, [arrays], core_ids=[0])
    return r.results[0]["out_0_dram"]
```
